# Optimizing a Trainium2 kernel written in Bass

```python
import numpy as np
import jax
import jax.numpy as jnp

def _softmax(x, axis=-1):
    return jax.nn.softmax(x, axis=axis)

def _gelu(x):
    return jax.nn.gelu(x, approximate=True)

def _silu(x):
    return jax.nn.silu(x)

def _sigmoid(x):
    return jax.nn.sigmoid(x)

def _layernorm(x, axis=-1, eps=1e-05):
    m = jnp.mean(x, axis=axis, keepdims=True)
    v = jnp.var(x, axis=axis, keepdims=True)
    return (x - m) / jnp.sqrt(v + eps)

def _scatter_add(tgt, idx, src, axis=0):
    return tgt.at[idx].add(src)

def _segment_sum(src, seg, n):
    return jax.ops.segment_sum(src, seg, n)
kernel_name = 'mk_xattn_ffn_d4_seqx_r8_f165da'

def setup_inputs(seed: int=0):
    np.random.seed(seed)
    _w = jnp.asarray

    def _rec_inputs():
        import jax
        import jax.numpy as jnp
        _rk = jax.random.key(seed)
        x = -0.0003929 + 0.9999 * jax.random.normal(jax.random.fold_in(_rk, 1), (16, 100, 128), jnp.float32)
        _lenS = 100 - jax.random.randint(jax.random.fold_in(_rk, 7), (16,), 0, max(1, 100 // 4) + 1, jnp.int32)
        _lenS2 = 1444 - jax.random.randint(jax.random.fold_in(_rk, 8), (16,), 0, max(1, 1444 // 4) + 1, jnp.int32)
        _ctx_1024P = jax.random.normal(jax.random.fold_in(_rk, 11), (16, 16, 128), jnp.float32)
        _ctx_1024c = jax.random.dirichlet(jax.random.fold_in(_rk, 511), 0.3 * jnp.ones((16,), jnp.float32), (16, 1444))
        _ctx_1024t = jnp.einsum('bsk,bkd->bsd', _ctx_1024c, _ctx_1024P)
        _ctx_1024t = _ctx_1024t * jax.lax.rsqrt(jnp.mean(jnp.square(_ctx_1024t)) + 1e-12) * 0.953939
        ctx_1024 = 2.81802e-05 + 1.00001 * (_ctx_1024t + 0.3 * jax.random.normal(jax.random.fold_in(_rk, 611), (16, 1444, 128), jnp.float32))
        _validS = jnp.arange(100)[None, :] < _lenS[:, None]
        _validS2 = jnp.arange(1444)[None, :] < _lenS2[:, None]
        _causal = jnp.tril(jnp.ones((100, 100), dtype=bool))
        mask_BxSxS2_ik0 = jnp.where(jnp.broadcast_to(_validS2[:, None, :], (16, 100, 1444)), 0, 1).astype(jnp.int32)
        mask_Bx1x1xS2_ik0 = jnp.where(jnp.broadcast_to(_validS2[:, None, None, :], (16, 1, 1, 1444)), 0, 1).astype(jnp.int32)
        return (x, ctx_1024, mask_BxSxS2_ik0, mask_Bx1x1xS2_ik0)
    x, ctx_1024, mask_BxSxS2_ik0, mask_Bx1x1xS2_ik0 = _rec_inputs()

    def _L0_xattn_setup():
        import jax, jax.numpy as jnp
        import numpy as np
        NEG = -1000000000.0
        key = jax.random.key(seed)
        k1, k2, k3, k4 = jax.random.split(key, 4)
        B, Sq, Sk, D = (8, 256, 256, 128)
        query = jax.random.normal(k1, (B, Sq, D), dtype=jnp.float32)
        memories = jax.random.normal(k2, (B, Sk, D), dtype=jnp.float32)
        mask = jax.random.randint(k3, (B, Sq, Sk), 0, 2).astype(jnp.int32)
        W = jax.random.normal(k4, (D, D), dtype=jnp.float32) * (1.0 / np.sqrt(D))
        b = jnp.zeros((D,), dtype=jnp.float32)
        return {'query': query, 'memories': memories, 'mask': mask, 'W': W, 'b': b}
    _L0_xattn_all = _L0_xattn_setup()
    _L0_xattn_in = {k: v for k, v in _L0_xattn_all.items() if k in ('W', 'b')}
    del _L0_xattn_all

    def _L0_ffn_setup():
        import jax, jax.numpy as jnp
        import numpy as np
        B, S, D, FF, E, L = (8, 256, 128, 512, 16, 4)

        def _unipool_layer(xt, router, W1, W2):
            logits = xt @ router
            probs = jax.nn.softmax(logits, axis=-1)
            w = jnp.max(probs, axis=-1)
            idx = jnp.argmax(probs, axis=-1)

            def body(acc, params):
                w1, w2, i = params
                h = jax.nn.silu(xt @ w1) @ w2
                sel = jnp.where(idx == i, w, 0.0)
                return (acc + sel[:, None] * h, None)
            out, _ = jax.lax.scan(body, jnp.zeros_like(xt), (W1, W2, jnp.arange(W1.shape[0])))
            return out
        key = jax.random.key(seed)
        k0, k1, k2, k3 = jax.random.split(key, 4)
        x = jax.random.normal(k0, (B, S, D), dtype=jnp.float32)
        routers = jax.random.normal(k1, (L, D, E), dtype=jnp.float32) * 0.02
        W1 = jax.random.normal(k2, (E, D, FF), dtype=jnp.float32) * 0.02
        W2 = jax.random.normal(k3, (E, FF, D), dtype=jnp.float32) * 0.02
        return {'x': x, 'routers': routers, 'W1': W1, 'W2': W2}
    _L0_ffn_all = _L0_ffn_setup()
    _L0_ffn_in = {k: v for k, v in _L0_ffn_all.items() if k in ('routers', 'W1', 'W2')}
    del _L0_ffn_all

    def _L1_xattn_setup():
        import jax, jax.numpy as jnp
        import numpy as np
        B, S, D, H = (4, 256, 128, 16)
        DK = D // H
        key = jax.random.key(seed)
        ks = jax.random.split(key, 8)
        scale = 1.0 / np.sqrt(D)
        return {'q': jax.random.normal(ks[0], (B, S, D), jnp.float32), 'k': jax.random.normal(ks[1], (B, S, D), jnp.float32), 'v': jax.random.normal(ks[2], (B, S, D), jnp.float32), 'wq': jax.random.normal(ks[3], (D, D), jnp.float32) * scale, 'bq': jnp.zeros((D,), jnp.float32), 'wk': jax.random.normal(ks[4], (D, D), jnp.float32) * scale, 'bk': jnp.zeros((D,), jnp.float32), 'wv': jax.random.normal(ks[5], (D, D), jnp.float32) * scale, 'bv': jnp.zeros((D,), jnp.float32), 'wo': jax.random.normal(ks[6], (D, D), jnp.float32) * scale, 'bo': jnp.zeros((D,), jnp.float32)}
    _L1_xattn_all = _L1_xattn_setup()
    _L1_xattn_in = {k: v for k, v in _L1_xattn_all.items() if k in ('wq', 'bq', 'wk', 'bk', 'wv', 'bv', 'wo', 'bo')}
    del _L1_xattn_all

    def _L1_ffn_setup():
        import jax, jax.numpy as jnp
        import numpy as np
        DIM = 128

        def _reference_tuple_inner(x, W_r, W_k, W_v, mu_r, mu_k):
            B, T, C = x.shape
            x_prev = jnp.concatenate([jnp.zeros((B, 1, C), x.dtype), x[:, :-1, :]], axis=1)
            xr = mu_r * x + (1.0 - mu_r) * x_prev
            xk = mu_k * x + (1.0 - mu_k) * x_prev
            r = jax.nn.sigmoid(jnp.einsum('btc,dc->btd', xr, W_r))
            k = jnp.einsum('btc,dc->btd', xk, W_k)
            k_act = jnp.square(jax.nn.relu(k))
            out = r * jnp.einsum('btc,dc->btd', k_act, W_v)
            new_state = x[:, -1, :]
            return (out, new_state)
        key = jax.random.key(seed)
        ks = jax.random.split(key, 6)
        B, T, C = (8, 256, DIM)
        x = jax.random.normal(ks[0], (B, T, C), dtype=jnp.float32)
        s = 1.0 / np.sqrt(C)
        W_r = jax.random.uniform(ks[1], (C, C), jnp.float32, -s, s)
        W_k = jax.random.uniform(ks[2], (C, C), jnp.float32, -s, s)
        W_v = jax.random.uniform(ks[3], (C, C), jnp.float32, -s, s)
        mu_r = jax.random.uniform(ks[4], (C,), jnp.float32)
        mu_k = jax.random.uniform(ks[5], (C,), jnp.float32)
        return {'x': x, 'W_r': W_r, 'W_k': W_k, 'W_v': W_v, 'mu_r': mu_r, 'mu_k': mu_k}
    _L1_ffn_all = _L1_ffn_setup()
    _L1_ffn_in = {k: v for k, v in _L1_ffn_all.items() if k in ('W_r', 'W_k', 'W_v', 'mu_r', 'mu_k')}
    del _L1_ffn_all

    def _L2_xattn_setup():
        import jax, jax.numpy as jnp
        import numpy as np
        import math
        D_MODEL = 128
        HEADS = 16
        D_K = D_MODEL // HEADS
        N, L = (4, 256)
        key0 = jax.random.key(seed)
        ks = jax.random.split(key0, 12)
        s = 1.0 / math.sqrt(D_MODEL)
        return {'value': jax.random.normal(ks[0], (N, L, D_MODEL), jnp.float32), 'key': jax.random.normal(ks[1], (N, L, D_MODEL), jnp.float32), 'query': jax.random.normal(ks[2], (N, L, D_MODEL), jnp.float32), 'mask': jax.random.randint(ks[3], (N, 1, 1, L), 0, 2, jnp.int32), 'wq': jax.random.normal(ks[4], (D_MODEL, D_MODEL), jnp.float32) * s, 'bq': jax.random.normal(ks[5], (D_MODEL,), jnp.float32) * s, 'wk': jax.random.normal(ks[6], (D_MODEL, D_MODEL), jnp.float32) * s, 'bk': jax.random.normal(ks[7], (D_MODEL,), jnp.float32) * s, 'wv': jax.random.normal(ks[8], (D_MODEL, D_MODEL), jnp.float32) * s, 'bv': jax.random.normal(ks[9], (D_MODEL,), jnp.float32) * s, 'wo': jax.random.normal(ks[10], (D_MODEL, D_MODEL), jnp.float32) * s, 'bo': jax.random.normal(ks[11], (D_MODEL,), jnp.float32) * s}
    _L2_xattn_all = _L2_xattn_setup()
    _L2_xattn_in = {k: v for k, v in _L2_xattn_all.items() if k in ('wq', 'bq', 'wk', 'bk', 'wv', 'bv', 'wo', 'bo')}
    del _L2_xattn_all

    def _L2_ffn_setup():
        import jax, jax.numpy as jnp
        import numpy as np
        B, S, D = (4, 64, 128)
        E, K, H = (64, 8, 32)
        ES, HS = (2, 256)
        key = jax.random.key(seed)
        ks = jax.random.split(key, 8)
        scale = 0.02
        rn = lambda k, shape, s: jax.random.normal(k, shape, jnp.float32) * s
        return {'x': rn(ks[0], (B, S, D), 1.0), 'router_w': rn(ks[1], (D, E), scale), 'router_b': jnp.zeros((E,), jnp.float32), 'w1': rn(ks[2], (E, D, H), scale), 'b1': jnp.zeros((E, H), jnp.float32), 'w2': rn(ks[3], (E, H, D), scale), 'b2': jnp.zeros((E, D), jnp.float32), 'sw1': rn(ks[4], (ES, D, HS), scale), 'sb1': jnp.zeros((ES, HS), jnp.float32), 'sw2': rn(ks[5], (ES, HS, D), scale), 'sb2': jnp.zeros((ES, D), jnp.float32)}
    _L2_ffn_all = _L2_ffn_setup()
    _L2_ffn_in = {k: v for k, v in _L2_ffn_all.items() if k in ('router_w', 'router_b', 'w1', 'b1', 'w2', 'b2', 'sw1', 'sb1', 'sw2', 'sb2')}
    del _L2_ffn_all

    def _L3_xattn_setup():
        import jax, jax.numpy as jnp
        import numpy as np
        D = 128
        H = 16
        HD = D // H
        EPS = 1e-06

        def rms_norm(x, w):
            xf = x.astype(jnp.float32)
            rms = jnp.sqrt(jnp.mean(xf * xf, axis=-1, keepdims=True) + EPS)
            return (xf / rms * w.astype(jnp.float32)).astype(x.dtype)
        key = jax.random.key(seed)
        ks = jax.random.split(key, 10)
        B, S, Sc = (4, 256, 256)
        s = 0.02
        return {'x': jax.random.normal(ks[0], (B, S, D), jnp.float32), 'ctx': jax.random.normal(ks[1], (B, Sc, D), jnp.float32), 'Wq': jax.random.normal(ks[2], (D, D), jnp.float32) * s, 'bq': jnp.zeros((D,), jnp.float32), 'Wkv': jax.random.normal(ks[3], (D, 2 * D), jnp.float32) * s, 'bkv': jnp.zeros((2 * D,), jnp.float32), 'Wproj': jax.random.normal(ks[4], (D, D), jnp.float32) * s, 'bproj': jnp.zeros((D,), jnp.float32), 'gq': jnp.ones((HD,), jnp.float32), 'gk': jnp.ones((HD,), jnp.float32)}
    _L3_xattn_all = _L3_xattn_setup()
    _L3_xattn_in = {k: v for k, v in _L3_xattn_all.items() if k in ('Wq', 'bq', 'Wkv', 'bkv', 'Wproj', 'bproj', 'gq', 'gk')}
    del _L3_xattn_all

    def _L3_ffn_setup():
        import jax, jax.numpy as jnp
        import numpy as np
        B, S, D, F, E, K = (2, 256, 128, 512, 8, 2)
        key = jax.random.key(seed)
        ks = jax.random.split(key, 5)
        x = jax.random.normal(ks[0], (B, S, D), dtype=jnp.float32)
        Wg = jax.random.normal(ks[1], (D, E), dtype=jnp.float32) * 0.02
        W1 = jax.random.normal(ks[2], (E, D, F), dtype=jnp.float32) * 0.02
        b1 = jnp.zeros((E, F), dtype=jnp.float32)
        W2 = jax.random.normal(ks[3], (E, F, D), dtype=jnp.float32) * 0.02
        b2 = jnp.zeros((E, D), dtype=jnp.float32)
        return {'x': x, 'Wg': Wg, 'W1': W1, 'b1': b1, 'W2': W2, 'b2': b2}
    _L3_ffn_all = _L3_ffn_setup()
    _L3_ffn_in = {k: v for k, v in _L3_ffn_all.items() if k in ('Wg', 'W1', 'b1', 'W2', 'b2')}
    del _L3_ffn_all
    return {'x': x, 'ctx_1024': ctx_1024, 'mask_BxSxS2_ik0': mask_BxSxS2_ik0, 'mask_Bx1x1xS2_ik0': mask_Bx1x1xS2_ik0, 'L0_xattn_W': _L0_xattn_in['W'], 'L0_xattn_b': _L0_xattn_in['b'], 'L0_ffn_routers': _L0_ffn_in['routers'], 'L0_ffn_W1': _L0_ffn_in['W1'], 'L0_ffn_W2': _L0_ffn_in['W2'], 'L1_xattn_wq': _L1_xattn_in['wq'], 'L1_xattn_bq': _L1_xattn_in['bq'], 'L1_xattn_wk': _L1_xattn_in['wk'], 'L1_xattn_bk': _L1_xattn_in['bk'], 'L1_xattn_wv': _L1_xattn_in['wv'], 'L1_xattn_bv': _L1_xattn_in['bv'], 'L1_xattn_wo': _L1_xattn_in['wo'], 'L1_xattn_bo': _L1_xattn_in['bo'], 'L1_ffn_W_r': _L1_ffn_in['W_r'], 'L1_ffn_W_k': _L1_ffn_in['W_k'], 'L1_ffn_W_v': _L1_ffn_in['W_v'], 'L1_ffn_mu_r': _L1_ffn_in['mu_r'], 'L1_ffn_mu_k': _L1_ffn_in['mu_k'], 'L2_xattn_wq': _L2_xattn_in['wq'], 'L2_xattn_bq': _L2_xattn_in['bq'], 'L2_xattn_wk': _L2_xattn_in['wk'], 'L2_xattn_bk': _L2_xattn_in['bk'], 'L2_xattn_wv': _L2_xattn_in['wv'], 'L2_xattn_bv': _L2_xattn_in['bv'], 'L2_xattn_wo': _L2_xattn_in['wo'], 'L2_xattn_bo': _L2_xattn_in['bo'], 'L2_ffn_router_w': _L2_ffn_in['router_w'], 'L2_ffn_router_b': _L2_ffn_in['router_b'], 'L2_ffn_w1': _L2_ffn_in['w1'], 'L2_ffn_b1': _L2_ffn_in['b1'], 'L2_ffn_w2': _L2_ffn_in['w2'], 'L2_ffn_b2': _L2_ffn_in['b2'], 'L2_ffn_sw1': _L2_ffn_in['sw1'], 'L2_ffn_sb1': _L2_ffn_in['sb1'], 'L2_ffn_sw2': _L2_ffn_in['sw2'], 'L2_ffn_sb2': _L2_ffn_in['sb2'], 'L3_xattn_Wq': _L3_xattn_in['Wq'], 'L3_xattn_bq': _L3_xattn_in['bq'], 'L3_xattn_Wkv': _L3_xattn_in['Wkv'], 'L3_xattn_bkv': _L3_xattn_in['bkv'], 'L3_xattn_Wproj': _L3_xattn_in['Wproj'], 'L3_xattn_bproj': _L3_xattn_in['bproj'], 'L3_xattn_gq': _L3_xattn_in['gq'], 'L3_xattn_gk': _L3_xattn_in['gk'], 'L3_ffn_Wg': _L3_ffn_in['Wg'], 'L3_ffn_W1': _L3_ffn_in['W1'], 'L3_ffn_b1': _L3_ffn_in['b1'], 'L3_ffn_W2': _L3_ffn_in['W2'], 'L3_ffn_b2': _L3_ffn_in['b2']}

def reference(x, ctx_1024, mask_BxSxS2_ik0, mask_Bx1x1xS2_ik0, L0_xattn_W, L0_xattn_b, L0_ffn_routers, L0_ffn_W1, L0_ffn_W2, L1_xattn_wq, L1_xattn_bq, L1_xattn_wk, L1_xattn_bk, L1_xattn_wv, L1_xattn_bv, L1_xattn_wo, L1_xattn_bo, L1_ffn_W_r, L1_ffn_W_k, L1_ffn_W_v, L1_ffn_mu_r, L1_ffn_mu_k, L2_xattn_wq, L2_xattn_bq, L2_xattn_wk, L2_xattn_bk, L2_xattn_wv, L2_xattn_bv, L2_xattn_wo, L2_xattn_bo, L2_ffn_router_w, L2_ffn_router_b, L2_ffn_w1, L2_ffn_b1, L2_ffn_w2, L2_ffn_b2, L2_ffn_sw1, L2_ffn_sb1, L2_ffn_sw2, L2_ffn_sb2, L3_xattn_Wq, L3_xattn_bq, L3_xattn_Wkv, L3_xattn_bkv, L3_xattn_Wproj, L3_xattn_bproj, L3_xattn_gq, L3_xattn_gk, L3_ffn_Wg, L3_ffn_W1, L3_ffn_b1, L3_ffn_W2, L3_ffn_b2):
    import jax
    import jax.numpy as jnp

    def _L0_xattn_ref(query, memories, mask, W, b):
        import jax, jax.numpy as jnp
        import numpy as np
        NEG = -1000000000.0
        q = jnp.einsum('bsd,od->bso', query, W) + b
        add_mask = (1.0 - mask.astype(q.dtype)) * NEG
        attn_logits = jnp.einsum('bqd,bkd->bqk', q, memories) + add_mask
        attn_weights = jax.nn.softmax(attn_logits, axis=-1)
        attn_outputs = jnp.einsum('bqk,bkd->bqd', attn_weights, memories)
        return attn_outputs

    def _L0_ffn_ref(x, routers, W1, W2):
        import jax, jax.numpy as jnp
        import numpy as np
        B, S, D, FF, E, L = (8, 256, 128, 512, 16, 4)

        def _unipool_layer(xt, router, W1, W2):
            logits = xt @ router
            probs = jax.nn.softmax(logits, axis=-1)
            w = jnp.max(probs, axis=-1)
            idx = jnp.argmax(probs, axis=-1)

            def body(acc, params):
                w1, w2, i = params
                h = jax.nn.silu(xt @ w1) @ w2
                sel = jnp.where(idx == i, w, 0.0)
                return (acc + sel[:, None] * h, None)
            out, _ = jax.lax.scan(body, jnp.zeros_like(xt), (W1, W2, jnp.arange(W1.shape[0])))
            return out
        b, s, d = x.shape
        xt = x.reshape(-1, d)

        def step(carry, router):
            return (_unipool_layer(carry, router, W1, W2), None)
        xt, _ = jax.lax.scan(step, xt, routers)
        return xt.reshape(b, s, d)

    def _L1_xattn_ref(q, k, v, wq, bq, wk, bk, wv, bv, wo, bo):
        import jax, jax.numpy as jnp
        import numpy as np
        B, S, D, H = (4, 256, 128, 16)
        DK = D // H
        b, s, _ = q.shape

        def proj(x, w, bias):
            y = x @ w + bias
            return y.reshape(b, -1, H, DK).transpose(0, 2, 1, 3)
        qh, kh, vh = (proj(q, wq, bq), proj(k, wk, bk), proj(v, wv, bv))
        scores = jnp.einsum('bhqd,bhkd->bhqk', qh, kh) / np.sqrt(DK).astype(jnp.float32)
        attn = jax.nn.softmax(scores, axis=-1)
        out = jnp.einsum('bhqk,bhkd->bhqd', attn, vh)
        out = out.transpose(0, 2, 1, 3).reshape(b, s, D)
        return out @ wo + bo

    def _L1_ffn_ref(x, W_r, W_k, W_v, mu_r, mu_k):
        import jax, jax.numpy as jnp
        import numpy as np
        DIM = 128

        def _reference_tuple_inner(x, W_r, W_k, W_v, mu_r, mu_k):
            B, T, C = x.shape
            x_prev = jnp.concatenate([jnp.zeros((B, 1, C), x.dtype), x[:, :-1, :]], axis=1)
            xr = mu_r * x + (1.0 - mu_r) * x_prev
            xk = mu_k * x + (1.0 - mu_k) * x_prev
            r = jax.nn.sigmoid(jnp.einsum('btc,dc->btd', xr, W_r))
            k = jnp.einsum('btc,dc->btd', xk, W_k)
            k_act = jnp.square(jax.nn.relu(k))
            out = r * jnp.einsum('btc,dc->btd', k_act, W_v)
            new_state = x[:, -1, :]
            return (out, new_state)
        return _reference_tuple_inner(x, W_r, W_k, W_v, mu_r, mu_k)[0]

    def _L2_xattn_ref(value, key, query, mask, wq, bq, wk, bk, wv, bv, wo, bo):
        import jax, jax.numpy as jnp
        import numpy as np
        import math
        D_MODEL = 128
        HEADS = 16
        D_K = D_MODEL // HEADS
        N, L = (4, 256)
        n, qlen = (query.shape[0], query.shape[1])
        h, dk = (HEADS, D_K)
        v = (value @ wv.T + bv).reshape(n, -1, h, dk).transpose(0, 2, 1, 3)
        k = (key @ wk.T + bk).reshape(n, -1, h, dk).transpose(0, 2, 1, 3)
        q = (query @ wq.T + bq).reshape(n, qlen, h, dk).transpose(0, 2, 1, 3)
        scores = jnp.einsum('nhqd,nhkd->nhqk', q, k)
        scores = jnp.where(mask == 0, jnp.float32(-1000000000.0), scores)
        attn = jax.nn.softmax(scores / math.sqrt(dk), axis=-1)
        out = jnp.einsum('nhqk,nhkd->nhqd', attn, v)
        out = out.transpose(0, 2, 1, 3).reshape(n, qlen, h * dk)
        return out @ wo.T + bo

    def _L2_ffn_ref(x, router_w, router_b, w1, b1, w2, b2, sw1, sb1, sw2, sb2):
        import jax, jax.numpy as jnp
        import numpy as np
        B, S, D = (4, 64, 128)
        E, K, H = (64, 8, 32)
        ES, HS = (2, 256)
        b_, s_, d_ = x.shape
        xf = x.reshape(-1, d_)
        probs = jax.nn.softmax(xf @ router_w + router_b, axis=-1)
        tw, ti = jax.lax.top_k(probs, K)
        tw = tw / jnp.sum(tw, axis=-1, keepdims=True)

        def body(acc, p):
            W1, B1, W2, B2, e = p
            h = jax.nn.silu(xf @ W1 + B1) @ W2 + B2
            cw = jnp.sum(jnp.where(ti == e, tw, 0.0), axis=-1)
            return (acc + cw[:, None] * h, None)
        routed, _ = jax.lax.scan(body, jnp.zeros_like(xf), (w1, b1, w2, b2, jnp.arange(w1.shape[0])))

        def shared_mlp(W1, B1, W2, B2):
            return jax.nn.silu(xf @ W1 + B1) @ W2 + B2
        shared = jnp.sum(jax.vmap(shared_mlp)(sw1, sb1, sw2, sb2), axis=0)
        return (routed + shared).reshape(b_, s_, d_)

    def _L3_xattn_ref(x, ctx, Wq, bq, Wkv, bkv, Wproj, bproj, gq, gk):
        import jax, jax.numpy as jnp
        import numpy as np
        D = 128
        H = 16
        HD = D // H
        EPS = 1e-06

        def rms_norm(x, w):
            xf = x.astype(jnp.float32)
            rms = jnp.sqrt(jnp.mean(xf * xf, axis=-1, keepdims=True) + EPS)
            return (xf / rms * w.astype(jnp.float32)).astype(x.dtype)
        B, S, _ = x.shape
        Sc = ctx.shape[1]
        q = (x @ Wq + bq).reshape(B, S, H, HD)
        q = rms_norm(q, gq).transpose(0, 2, 1, 3)
        kv = (ctx @ Wkv + bkv).reshape(B, Sc, 2, H, HD)
        k = rms_norm(kv[:, :, 0], gk).transpose(0, 2, 1, 3)
        v = kv[:, :, 1].transpose(0, 2, 1, 3)
        scale = 1.0 / jnp.sqrt(jnp.asarray(HD, q.dtype))
        scores = jnp.einsum('bhsd,bhtd->bhst', q, k) * scale
        attn = jax.nn.softmax(scores, axis=-1)
        out = jnp.einsum('bhst,bhtd->bhsd', attn, v)
        out = out.transpose(0, 2, 1, 3).reshape(B, S, D)
        return out @ Wproj + bproj

    def _L3_ffn_ref(x, Wg, W1, b1, W2, b2):
        import jax, jax.numpy as jnp
        import numpy as np
        B, S, D, F, E, K = (2, 256, 128, 512, 8, 2)
        b, s, d = x.shape
        e = Wg.shape[1]
        T = b * s
        C = 2 * K * T // e
        xt = x.reshape(T, d)
        logits = xt.astype(jnp.float32) @ Wg.astype(jnp.float32)
        gates = jax.nn.softmax(logits, axis=-1)
        idx1 = jnp.argmax(gates, axis=-1)
        mask1 = jax.nn.one_hot(idx1, e, dtype=gates.dtype)
        gate1 = jnp.sum(gates * mask1, axis=-1)
        logits2 = jnp.where(mask1 > 0, -jnp.inf, logits)
        idx2 = jnp.argmax(logits2, axis=-1)
        mask2 = jax.nn.one_hot(idx2, e, dtype=gates.dtype)
        gate2 = jnp.sum(gates * mask2, axis=-1)
        denom = gate1 + gate2 + 1e-09
        w1 = gate1 / denom
        w2 = gate2 / denom
        p1 = jnp.cumsum(mask1, axis=0) - mask1
        pos1 = jnp.sum(p1 * mask1, axis=-1).astype(jnp.int32)
        off = jnp.sum(mask1, axis=0)
        p2 = jnp.cumsum(mask2, axis=0) - mask2 + off[None, :]
        pos2 = jnp.sum(p2 * mask2, axis=-1).astype(jnp.int32)
        keep1 = (pos1 < C).astype(xt.dtype)
        keep2 = (pos2 < C).astype(xt.dtype)
        pos1 = jnp.clip(pos1, 0, C - 1)
        pos2 = jnp.clip(pos2, 0, C - 1)
        xe = jnp.zeros((e, C, d), dtype=xt.dtype)
        xe = xe.at[idx1, pos1].add(xt * keep1[:, None])
        xe = xe.at[idx2, pos2].add(xt * keep2[:, None])
        h = jax.nn.gelu(jnp.einsum('ecd,edf->ecf', xe, W1) + b1[:, None, :], approximate=False)
        ye = jnp.einsum('ecf,efd->ecd', h, W2) + b2[:, None, :]
        out = ye[idx1, pos1] * (w1 * keep1)[:, None] + ye[idx2, pos2] * (w2 * keep2)[:, None]
        return out.reshape(b, s, d)
    x = x + _L0_xattn_ref(_layernorm(x, axis=-1), ctx_1024, mask_BxSxS2_ik0, L0_xattn_W, L0_xattn_b)
    x = x + _L0_ffn_ref(_layernorm(x, axis=-1), L0_ffn_routers, L0_ffn_W1, L0_ffn_W2)
    x = x + _L1_xattn_ref(_layernorm(x, axis=-1), ctx_1024, ctx_1024, L1_xattn_wq, L1_xattn_bq, L1_xattn_wk, L1_xattn_bk, L1_xattn_wv, L1_xattn_bv, L1_xattn_wo, L1_xattn_bo)
    x = x + _L1_ffn_ref(_layernorm(x, axis=-1), L1_ffn_W_r, L1_ffn_W_k, L1_ffn_W_v, L1_ffn_mu_r, L1_ffn_mu_k)
    x = x + _L2_xattn_ref(ctx_1024, ctx_1024, _layernorm(x, axis=-1), mask_Bx1x1xS2_ik0, L2_xattn_wq, L2_xattn_bq, L2_xattn_wk, L2_xattn_bk, L2_xattn_wv, L2_xattn_bv, L2_xattn_wo, L2_xattn_bo)
    x = x + _L2_ffn_ref(_layernorm(x, axis=-1), L2_ffn_router_w, L2_ffn_router_b, L2_ffn_w1, L2_ffn_b1, L2_ffn_w2, L2_ffn_b2, L2_ffn_sw1, L2_ffn_sb1, L2_ffn_sw2, L2_ffn_sb2)
    x = x + _L3_xattn_ref(_layernorm(x, axis=-1), ctx_1024, L3_xattn_Wq, L3_xattn_bq, L3_xattn_Wkv, L3_xattn_bkv, L3_xattn_Wproj, L3_xattn_bproj, L3_xattn_gq, L3_xattn_gk)
    x = x + _L3_ffn_ref(_layernorm(x, axis=-1), L3_ffn_Wg, L3_ffn_W1, L3_ffn_b1, L3_ffn_W2, L3_ffn_b2)
    return x

_drawn_inputs = setup_inputs


def setup_inputs(seed=0):
    import zlib

    import numpy as np

    out = dict(_drawn_inputs(seed))
    spreads = {'L0_xattn_b': (0.0, 0.1),
     'L1_xattn_bq': (0.0, 0.1),
     'L1_xattn_bk': (0.0, 0.1),
     'L1_xattn_bv': (0.0, 0.1),
     'L1_xattn_bo': (0.0, 0.1),
     'L2_ffn_router_b': (0.0, 0.1),
     'L2_ffn_b1': (0.0, 0.1),
     'L2_ffn_b2': (0.0, 0.1),
     'L2_ffn_sb1': (0.0, 0.1),
     'L2_ffn_sb2': (0.0, 0.1),
     'L3_xattn_bq': (0.0, 0.1),
     'L3_xattn_bkv': (0.0, 0.1),
     'L3_xattn_bproj': (0.0, 0.1),
     'L3_xattn_gq': (1.0, 0.2),
     'L3_xattn_gk': (1.0, 0.2),
     'L3_ffn_b1': (0.0, 0.1),
     'L3_ffn_b2': (0.0, 0.1)}
    factors = {}
    for name, (base, spread) in spreads.items():
        noise = np.random.default_rng([zlib.crc32(name.encode()), seed]).standard_normal(out[name].shape)
        drawn = base * np.exp(spread * noise) if base else spread * noise
        out[name] = jnp.asarray(drawn.astype(out[name].dtype))
    for name, factor in factors.items():
        out[name] = (out[name] * factor).astype(out[name].dtype)
    return out
```

```python
from contextlib import ExitStack

import concourse.bass as bass
from concourse import mybir

F32 = mybir.dt.float32
F32R = mybir.dt.float32r
I32 = mybir.dt.int32
ALU = mybir.AluOpType
ACT = mybir.ActivationFunctionType
X = mybir.AxisListType.X

B, SQ, D = 16, 100, 128
SK = 1444
NT = B * SQ
KT = (SK + 127) // 128
KLAST = SK - 128 * (KT - 1)
H, HD = 16, 8
GH = 4
GROUPS = H // GH
GQ = GH * SQ
HALF = 2 * GQ
SLOTS = 2 * KT
TG = 4
BG = B // TG
NTG = NT // TG
E0, FF, L0 = 16, 512, 4
FC = FF // 128
E2, H2, K2 = 64, 32, 8
HC2 = E2 * H2 // 128
ES, HS2 = 2, 256
SC2 = ES * HS2 // 128
E3, K3 = 8, 2
CAP = 2 * K3 * NT // E3
NEG = -1.0e9
HSCALE = float(HD) ** -0.5
KCHUNKS = [(0, 512), (512, 512), (1024, SK - 1024)]
SAFE = 60.0


def rows(t):
    return 128 if t < KT - 1 else KLAST


class Chain:

    def __init__(self, eng, sem, per=0):
        self.eng, self.sem, self.per, self.base, self.n = eng, sem, per, 0, 0

    def begin(self, b):
        assert self.n in (0, self.per), (self.n, self.per)
        self.base, self.n = b * self.per, 0

    def done(self, ins):
        ins.then_inc(self.sem, 1)
        self.n += 1
        self.eng.wait_ge(self.sem, self.base + self.n)


class Scope:

    def __init__(self, nc, tag):
        self.nc, self.tag, self.stack, self.taken = nc, tag, ExitStack(), []

    def __enter__(self):
        self.stack.__enter__()
        return self

    def __exit__(self, *a):
        said = self.stack.__exit__(*a)
        if self.taken:
            self.nc.clear_and_free_semaphores(self.taken)
            self.nc.all_engine_barrier()
        return said

    def sb(self, name, shape, dtype=F32):
        return self.stack.enter_context(self.nc.sbuf_tensor(f"{self.tag}_{name}", shape, dtype))

    def ps(self, name, shape):
        return self.stack.enter_context(self.nc.psum_tensor(f"{self.tag}_{name}", shape, F32))

    def sem(self, name):
        self.taken.append(self.nc.alloc_semaphore(f"{self.tag}_{name}"))
        return self.taken[-1]

    def sems(self, names):
        return [self.sem(n) for n in names.split()]

    def block(self):
        return self.stack.enter_context(self.nc.Block())


def setup(nc, k, ins):
    with Scope(nc, "setup") as c:
        x_in, filled, cut, made = c.sems("x_in filled cut made")
        block = c.block()

        @block.sync
        def _(sp):
            sp.dma_start(k.x[:, :, :], ins["x"].rearrange("b q d -> q b d")).then_inc(x_in, 16)
            sp.wait_ge(x_in, 16)

        @block.gpsimd
        def _(pool):
            pool.memset(k.ident[:, :], 0.0).then_inc(filled, 1)
            pool.memset(k.headmask[:, :], 1.0).then_inc(filled, 1)
            pool.memset(k.blockavg[:, :], 1.0 / HD).then_inc(filled, 1)
            pool.memset(k.expertcols[:, :, :], 1.0).then_inc(filled, 1)
            pool.memset(k.lower[:, :], 1.0).then_inc(filled, 1)
            pool.memset(k.ones[:, :], 1.0).then_inc(filled, 1)
            pool.wait_ge(filled, 6)

            def select(t, pattern, base, mult, op, fill=0.0):
                pool.affine_select(out=t, in_=t, pattern=pattern, base=base, channel_multiplier=mult,
                                   compare_op=op, fill=fill).then_inc(cut, 1)

            per = E2 // HC2
            select(k.headmask[:, :], [[-HD, H]], 0, 1, ALU.is_ge)
            select(k.blockavg[:, :].rearrange("p (h d) -> p h d", d=HD), [[-HD, H], [0, HD]], 0, 1, ALU.is_ge)
            select(k.expertcols[:, :, :].rearrange("e c (j f) -> e (c j) f", f=H2),
                   [[-1, E2], [0, H2]], 0, 1, ALU.is_ge)
            pool.wait_ge(cut, 3)
            select(k.headmask[:, :], [[HD, H]], HD - 1, -1, ALU.is_ge)
            select(k.blockavg[:, :].rearrange("p (h d) -> p h d", d=HD), [[HD, H], [0, HD]], HD - 1, -1, ALU.is_ge)
            select(k.expertcols[:, :, :].rearrange("e c (j f) -> e (c j) f", f=H2),
                   [[1, E2], [0, H2]], 0, -1, ALU.is_ge)
            select(k.ident[:, :], [[-1, 128]], 0, 1, ALU.not_equal, 1.0)
            select(k.lower[:, :], [[1, 128]], 0, -1, ALU.is_gt)
            pool.iota(k.backwards[:, :], [[-1, E2]], base=E2, channel_multiplier=0,
                      allow_small_or_imprecise_dtypes=True).then_inc(cut, 1)
            pool.wait_ge(cut, 9)
            pool.sem_inc(made, 1)

        @block.vector
        def _(dve):
            dve.wait_ge(made, 1)
            ch = Chain(dve, made)
            ch.n = 1
            ch.done(dve.tensor_reduce(k.groupmask[:, :], k.headmask[:, :].rearrange("p (g j) -> p j g", j=GH), X, ALU.add))
            ch.done(dve.tensor_scalar(k.negident[:, :], k.ident[0:H, 0:H], -1.0, None, ALU.mult))


def layernorm(nc, k, tag):
    with Scope(nc, tag) as c:
        centred = c.sb("centred", [SQ, B, D])
        square = c.sb("square", [SQ, B, D])
        total, mean, spread, var, std, inv = (c.sb(n, [SQ, B]) for n in "total mean spread var std inv".split())
        turned = c.ps("turned", [128, TG, 512])
        step, var_ready, std_ready, xn_ready, turned_ready, copied = c.sems("step var std xn turned copied")
        block = c.block()

        @block.vector
        def _(dve):
            ch = Chain(dve, step)
            ch.done(dve.tensor_reduce(total[:, :], k.x[:, :, :], X, ALU.add))
            ch.done(dve.tensor_scalar(mean[:, :], total[:, :], 1.0 / D, None, ALU.mult))
            ch.done(dve.tensor_tensor(centred[:, :, :], k.x[:, :, :],
                                      mean[:, :].unsqueeze(2).to_broadcast([SQ, B, D]), ALU.subtract))
            ch.done(dve.tensor_tensor(square[:, :, :], centred[:, :, :], centred[:, :, :], ALU.mult))
            ch.done(dve.tensor_reduce(spread[:, :], square[:, :, :], X, ALU.add))
            dve.tensor_scalar(var[:, :], spread[:, :], 1.0 / D, 1e-5, ALU.mult, ALU.add).then_inc(var_ready, 1)
            dve.wait_ge(std_ready, 1)
            ch.done(dve.reciprocal(inv[:, :], std[:, :]))
            for g in range(TG):
                s = slice(g * BG, (g + 1) * BG)
                dve.tensor_tensor(square[:, s, :], centred[:, s, :],
                                  inv[:, s].unsqueeze(2).to_broadcast([SQ, BG, D]), ALU.mult).then_inc(xn_ready, 1)

        @block.tensor
        def _(pe):
            for g in range(TG):
                pe.wait_ge(xn_ready, g + 1)
                for j in range(BG):
                    last = pe.transpose(turned[:, g, j * SQ:(j + 1) * SQ], square[:, g * BG + j, :], k.ident[0:SQ, 0:SQ])
                last.then_inc(turned_ready, 1)

        @block.scalar
        def _(act):
            act.wait_ge(var_ready, 1)
            act.activation(std[:, :], var[:, :], ACT.Sqrt).then_inc(std_ready, 1)
            for g in range(TG):
                act.wait_ge(turned_ready, g + 1)
                act.copy(k.xnT[:, g * NTG:(g + 1) * NTG], turned[:, g, 0:NTG]).then_inc(copied, 1)


def l0_attention(nc, k, ins):
    with Scope(nc, "l0a") as c:
        qT = c.sb("qT", [128, B, SQ])
        w = c.sb("w", [128, D])
        bias = c.sb("b", [128, 1])
        q1 = c.sb("q1", [128, 2, SQ])
        ctxT = c.sb("ctxT", [128, 2, SK])
        ctxN = c.sb("ctx", [128, 2, KT, D])
        mask = c.sb("mask", [SQ, 2, SK], I32)
        dropped = c.sb("dropped", [SQ, 2, SK])
        logits = c.sb("logits", [SQ, 2, SK])
        probs = c.sb("probs", [SQ, 2, SK])
        probsT = c.sb("probsT", [128, 2, KT, SQ])
        negmax = c.sb("negmax", [SQ, 2])
        total = c.sb("total", [SQ, 2])
        inv = c.sb("inv", [SQ, 2])
        ps = c.ps("ps", [128, 2, 3 * 512])
        py = c.ps("py", [128, 2, 512])
        w_in, q_made, q_kept = c.sems("w_in q_made q_kept")
        ctxT_in = c.sems("ctxT_in0 ctxT_in1")
        ctx_in = c.sems("ctx_in0 ctx_in1")
        mask_in = c.sems("mask_in0 mask_in1")
        q1_ready, scored, masked, maxed, exped, turned, kept, outed, added, step = c.sems(
            "q1_ready scored masked maxed exped turned kept outed added step")
        block = c.block()

        @block.sync
        def _(sp):
            sp.dma_start(w[:, :], ins["L0_xattn_W"]).then_inc(w_in, 16)
            sp.dma_start(bias[:, :], ins["L0_xattn_b"]).then_inc(w_in, 16)

            def load(b, j, again):
                if again:
                    sp.wait_ge(scored, b - 1)
                sp.dma_start(ctxT[:, j, :], ins["ctxT"][b]).then_inc(ctxT_in[j], 16)
                if again:
                    sp.wait_ge(masked, b - 1)
                sp.dma_start(mask[:, j, :], ins["mask_BxSxS2_ik0"][b]).then_inc(mask_in[j], 16)
                if again:
                    sp.wait_ge(outed, b + 1)
                n = 128 * (KT - 1)
                sp.dma_start(ctxN[:, j, 0:KT - 1, :],
                             ins["ctx_1024"][b][0:n, :].rearrange("(t p) d -> p t d", p=128)).then_inc(ctx_in[j], 16)
                sp.dma_start(ctxN[0:KLAST, j, KT - 1, :], ins["ctx_1024"][b][n:SK, :]).then_inc(ctx_in[j], 16)

            load(0, 0, False)
            load(1, 1, False)
            with sp.Fori(0, (B - 2) // 2) as i:
                load(2 * i + 2, 0, True)
                load(2 * i + 3, 1, True)

        @block.tensor
        def _(pe):
            pe.wait_ge(w_in, 32)
            for g in range(TG):
                if g >= 2:
                    pe.wait_ge(q_kept, g - 1)
                pe.matmul(py[:, g % 2, 0:NTG], w[:, :], k.xnT[:, g * NTG:(g + 1) * NTG],
                          start=True, stop=True).then_inc(q_made, 1)

            def scores(b, h, j):
                pe.wait_ge(ctxT_in[j], 16 * h + 16)
                pe.wait_ge(q1_ready, b + 1)
                pe.wait_ge(kept, b + 1)
                for at, n in KCHUNKS:
                    last = pe.matmul(ps[0:SQ, j, at:at + n], q1[:, j, :], ctxT[:, j, at:at + n],
                                     start=True, stop=True)
                last.then_inc(scored, 1)

            def outputs(b, h, j):
                pe.wait_ge(exped, b + 1)
                for t in range(KT):
                    last = pe.transpose(ps[0:rows(t), j, t * 128:t * 128 + SQ],
                                        probs[:, j, t * 128:t * 128 + rows(t)], k.ident[0:SQ, 0:SQ])
                last.then_inc(turned, 1)
                pe.wait_ge(kept, b + 3)
                pe.wait_ge(ctx_in[j], 32 * h + 32)
                pe.wait_ge(added, b + 1)
                for t in range(KT):
                    last = pe.matmul(py[0:SQ, j, 0:D], probsT[0:rows(t), j, t, :], ctxN[0:rows(t), j, t, :],
                                     start=(t == 0), stop=(t == KT - 1))
                last.then_inc(outed, 1)

            scores(0, 0, 0)
            with pe.Fori(0, (B - 2) // 2) as i:
                scores(2 * i + 1, i, 1)
                outputs(2 * i, i, 0)
                scores(2 * i + 2, i + 1, 0)
                outputs(2 * i + 1, i, 1)
            scores(B - 1, B // 2 - 1, 1)
            outputs(B - 2, B // 2 - 1, 0)
            outputs(B - 1, B // 2 - 1, 1)

        @block.scalar
        def _(act):
            act.sem_inc(kept, 2)

            def exps(b, j):
                act.wait_ge(maxed, b + 1)
                act.wait_ge(turned, b + 1)
                act.wait_ge(added, b + 1)
                act.activation(probs[:, j, :], logits[:, j, :], ACT.Exp, bias=negmax[:, j:j + 1],
                               accum_out=total[:, j:j + 1]).then_inc(exped, 1)

            def turns(b, j):
                act.wait_ge(turned, b + 3)
                act.wait_ge(outed, b + 1)
                act.copy(probsT[:, j, 0:KT - 1, :],
                         ps[:, j, 0:128 * (KT - 1)].rearrange("p (t q) -> p t q", q=128)[:, :, 0:SQ]).then_inc(step, 1)
                act.copy(probsT[0:KLAST, j, KT - 1, :],
                         ps[0:KLAST, j, 128 * (KT - 1):128 * (KT - 1) + SQ]).then_inc(step, 1)
                act.wait_ge(step, 2 * b + 2)
                act.sem_inc(kept, 1)

            act.sem_inc(turned, 2)
            act.sem_inc(outed, 2)
            exps(0, 0)
            with act.Fori(0, (B - 2) // 2) as i:
                exps(2 * i + 1, 1)
                turns(2 * i, 0)
                exps(2 * i + 2, 0)
                turns(2 * i + 1, 1)
            exps(B - 1, 1)
            turns(B - 2, 0)
            turns(B - 1, 1)

        @block.vector
        def _(dve):
            dve.sem_inc(added, 2)
            for g in range(TG):
                dve.wait_ge(q_made, g + 1)
                dve.tensor_scalar(qT[:, g * BG:(g + 1) * BG, :], py[:, g % 2, 0:NTG].rearrange("p (b q) -> p b q", q=SQ), bias[:, 0:1],
                                  None, ALU.add).then_inc(q_kept, 1)
            dve.wait_ge(q_kept, TG)
            PER = 4
            base = c.sem("dve_step")

            def maxes(b, h, j):
                dve.tensor_copy(q1[:, j, :], qT[:, b, :]).then_inc(q1_ready, 1)
                dve.wait_ge(mask_in[j], 16 * h + 16)
                dve.tensor_scalar(dropped[:, j, :], mask[:, j, :], -1.0, 1.0, ALU.mult, ALU.add).then_inc(masked, 1)
                dve.wait_ge(masked, b + 1)
                dve.wait_ge(scored, b + 1)
                dve.scalar_tensor_tensor(logits[:, j, :], dropped[:, j, :], NEG, ps[0:SQ, j, 0:SK],
                                         ALU.mult, ALU.add).then_inc(base, 1)
                dve.wait_ge(base, b + 1)
                dve.tensor_reduce(negmax[:, j:j + 1], logits[:, j, :], X, ALU.max, negate=True).then_inc(maxed, 1)

            def adds(b, j):
                dve.wait_ge(exped, b + 1)
                dve.reciprocal(inv[:, j:j + 1], total[:, j:j + 1]).then_inc(inv_ready, 1)
                dve.wait_ge(outed, b + 3)
                dve.wait_ge(inv_ready, b + 1)
                dve.scalar_tensor_tensor(k.x[:, b, :], py[0:SQ, j, 0:D], inv[:, j:j + 1], k.x[:, b, :],
                                         ALU.mult, ALU.add).then_inc(added, 1)

            inv_ready = c.sem("inv_ready")
            maxes(0, 0, 0)
            with dve.Fori(0, (B - 2) // 2) as i:
                maxes(2 * i + 1, i, 1)
                adds(2 * i, 0)
                maxes(2 * i + 2, i + 1, 0)
                adds(2 * i + 1, 1)
            maxes(B - 1, B // 2 - 1, 1)
            adds(B - 2, 0)
            adds(B - 1, 1)


def heads_attention(nc, k, ins, layer):
    masked, normed = layer == 2, layer == 3
    with Scope(nc, f"a{layer}") as c:
        w = c.sb("w", [128, 4, D])
        cols = c.sb("cols", [128, 8])
        bo = c.sb("bo", [SQ, D])
        qrep = c.sb("qrep", [128, GROUPS, B, SQ])
        qmax = c.sb("qmax", [128, B])
        ctxT = c.sb("ctxT", [128, 2, SK])
        kT = c.sb("kT", [128, SK])
        khigh = c.sb("khigh", [128, SK])
        kstack = c.sb("kstack", [128, 2, GROUPS * SK + 128 - KLAST], F32R)
        v = c.sb("v", [128, 2, KT, D])
        qstack = c.sb("qstack", [128, 2, H, SQ], F32R)
        NP = 6
        probs = c.sb("probs", [128, NP, HALF])
        sums = c.sb("sums", [128, 2, 2, HALF])
        own = c.sb("own", [128, GH, SQ])
        att = c.sb("att", [128, 5, SQ])
        kmax = c.sb("kmax", [128, 2, 2])
        bound = c.sb("bound", [1, 2])
        unsafe = c.sb("unsafe", [1, 2], I32)
        rowmax = c.sb("rowmax", [SQ, H])
        shift = k.xnT[0:H, :].rearrange("h (a q) -> h a q", q=SQ)
        early = probs[:, :, :].rearrange("p n c -> p (n c)")
        qT = early[:, 0:NT].rearrange("p (b q) -> p b q", q=SQ)
        qsq = early[:, NT:2 * NT]
        qparts = sums[:, :, :, :].rearrange("p n h c -> p n (h c)")
        if masked:
            maskrow = c.sb("maskrow", [128, SK], I32)
            valid = c.sb("valid", [128, SK])
            anyvalid = c.sb("anyvalid", [128, 2])
            maskcol = c.sb("maskcol", [128, B, KT], I32)
            droppedcol = c.sb("droppedcol", [128, B, KT])
            keybias = c.sb("keybias", [128, 2, KT])
            lifted = kT[0:SQ, :]
            weight = c.sb("weight", [SQ, 1])
        if normed:
            eps = c.sb("eps", [128, 1])
            ksq = c.sb("ksq", [128, 512])
            klog = c.sb("klog", [128, 512])
            kinv = c.sb("kinv", [128, 512])
        score = c.ps("score", [128, 6 * 512])
        numer = c.ps("numer", [128, 512])
        misc = c.ps("misc", [128, 512])
        slot_ps = score[:, :].rearrange("p (s g c) -> p s g c", s=3, g=2)

        w_in, cols_in, q_full, q_free, q_ready = c.sems("w_in cols_in q_full q_free q_ready")
        ctx_in, row_in = c.sems("ctx_in0 ctx_in1"), c.sem("row_in")
        scored, exped, mixed, summed_v, summed_p = c.sems("scored exped mixed summed_v summed_p")
        misc_full, misc_free = c.sems("misc_full misc_free")
        k_made, k_high, k_split, stack_in, q_split, rep_in, v_ready, qstack_ready, numer_free, att_ready = c.sems(
            "k_made k_high k_split stack_in q_split rep_in v_ready qstack_ready numer_free att_ready")
        prod_ready, flag_ready, tail_clear = c.sems("prod_ready flag_ready tail_clear")
        max_full, max_free, shift_ready = c.sems("max_full max_free shift_ready")
        valid_ready, bias_ready, ksq_ready, kraw_ready, kinv_ready, kinv_used = c.sems(
            "valid_ready bias_ready ksq_ready kraw_ready kinv_ready kinv_used")
        v_step, f_step, a_step, parted, blocked = c.sems("v_step f_step a_step parted blocked")
        block = c.block()

        if normed:
            uses = dict(K0=2, sums=3, N0=4, y=5, K1=6, N1=7, K2=8, N2=9, V0=11, V1=13, V2=15, bound=17)
        else:
            uses = dict(sums=3, K0=4, y=5, K1=6, K2=7, V0=11, V1=13, V2=15, bound=17)
        SUMS, Y = uses["sums"], uses["y"]
        prep = [n for n in uses if n not in ("sums", "y")]
        at = {n: uses[n] for n in prep}
        order = ["max"] + list(uses)
        PRE, USES = len(prep), len(order)

        def use(b, name):
            if isinstance(b, int):
                if b < 0:
                    return prep.index(name)
                if b == 0:
                    return PRE + (["max"] + prep).index(name)
                if b == B - 1:
                    return PRE + b * USES - 2 + ["max", "sums", "y"].index(name)
                if b == B:
                    return use(B - 1, "y") + ["max", "sums", "y"].index(name)
            return PRE + b * USES - 2 + order.index(name)

        COLS = 16 * (4 + (2 if normed else 0) + (1 if masked else 0))
        CR_S, CR_M, CR_A = 3, NP, 3

        def whole(eng, batch):
            batch(0, 0, 0)
            with eng.Fori(0, (B - 2) // 2) as i:
                batch(2 * i + 1, 1, i + 1)
                batch(2 * i + 2, 0, i + 1)
            batch(B - 1, 1, None)
            batch(B, 0, None)

        def add(eng, done, b, n, j, pooled):
            t, hf = n // 2, n % 2
            r = rows(t)
            if t == 1 and pooled and not (isinstance(b, int) and b < 1):
                eng.wait_ge(misc_full, use(b - 1, "sums") + 1 if not isinstance(b, int) or b > 1 else PRE)
            eng.wait_ge(exped, b * SLOTS + n + 1 + CR_S)
            if t > 1:
                eng.wait_ge(done, b * (KT - 1) + CR_A + t - 1)
            old = probs[0:r, (n - 2) % NP, :] if t == 1 else sums[0:r, j, hf, :]
            eng.tensor_tensor(sums[0:r, j, hf, :], old, probs[0:r, n % NP, :], ALU.add).then_inc(done, 1)

        @block.sync
        def _(sp):
            for n, name in enumerate(("wq", "wk", "wv", "wo")):
                sp.dma_start(w[:, n, :], ins[f"{name}{layer}"]).then_inc(w_in, 16)
            names = ["bq", "bk", "bv"] + (["gq", "gk"] if normed else [])
            for n, name in enumerate(names):
                sp.dma_start(cols[:, n:n + 1], ins[f"{name}{layer}"]).then_inc(cols_in, 16)
            sp.dma_start(bo[:, :], ins[f"bo{layer}"].partition_broadcast(SQ)).then_inc(cols_in, 16)
            if masked:
                sp.dma_start(maskcol[:, :, :], ins["keymask_cols"]).then_inc(cols_in, 16)

            def load(b, j, free_at=None):
                if free_at is not None:
                    sp.wait_ge(misc_full, free_at)
                sp.dma_start(ctxT[:, j, :], ins["ctxT"][b]).then_inc(ctx_in[j], 16)

            def load_row(b):
                if masked:
                    if not isinstance(b, int) or b > 0:
                        sp.wait_ge(valid_ready, b)
                    sp.dma_start(maskrow[:, :], ins["keymask"][b].partition_broadcast(128)).then_inc(row_in, 16)

            def restack(b, j):
                sp.wait_ge(k_split, 3 * b + 3)
                if not isinstance(b, int) or b >= 2:
                    sp.sem_inc(parted, 1)
                    sp.wait_ge(scored, (b - 1) * SLOTS)
                for g in range(GROUPS):
                    for part, src in enumerate((khigh, kT, khigh, kT)):
                        sp.dma_start(kstack[32 * part:32 * part + 32, j, g * SK:(g + 1) * SK].bitcast(F32),
                                     src[32 * g:32 * g + 32, :]).then_inc(stack_in, 16)

            load(0, 0)
            load_row(0)
            load(1, 1)
            for g in range(GROUPS):
                for part, n in enumerate((0, 0, 1, 1)):
                    if g == 0 and part in (0, 2):
                        sp.wait_ge(q_split, n + 1)
                    sp.dma_start(qrep[32 * part:32 * part + 32, g, :, :].rearrange("p b q -> p (b q)"),
                                 qparts[32 * g:32 * g + 32, n, :]).then_inc(rep_in, 16)
            restack(0, 0)
            load_row(1)
            load(2, 0, use(-1, "V2") + 1)
            restack(1, 1)
            load_row(2)
            load(3, 1, use(0, "V2") + 1)
            with sp.Fori(0, (B - 4) // 2) as i:
                for n in range(2):
                    b = 2 * i + 1 + n
                    restack(b + 1, n)
                    load_row(b + 2)
                    load(b + 3, n, use(b, "V2") + 1)
            restack(B - 2, 0)
            load_row(B - 1)
            restack(B - 1, 1)

        @block.tensor
        def _(pe):
            pe.wait_ge(w_in, 64)
            for g in range(TG):
                pe.matmul(score[:, g * 512:g * 512 + NTG], w[:, 0, :], k.xnT[:, g * NTG:(g + 1) * NTG],
                          start=True, stop=True).then_inc(q_full, 1)
            if normed:
                for g in range(TG):
                    pe.wait_ge(q_ready, g + 1)
                    pe.matmul(score[:, g * 512:g * 512 + NTG], k.blockavg[:, :],
                              qsq[:, g * NTG:(g + 1) * NTG], start=True, stop=True).then_inc(q_full, 1)

            def piece(b, name, j, pb, hh):
                pe.wait_ge(misc_free, use(b, name) + 1)
                n = int(name[-1]) if name != "bound" else 0
                if name[0] == "K":
                    if n == 0:
                        pe.wait_ge(ctx_in[j], 16 * hh + 16)
                    a, m = KCHUNKS[n]
                    last = pe.matmul(misc[:, 0:m], w[:, 1, :], ctxT[:, j, a:a + m], start=True, stop=True)
                elif name[0] == "N":
                    a, m = KCHUNKS[n]
                    pe.wait_ge(ksq_ready, pb * 3 + n + 1)
                    last = pe.matmul(misc[:, 0:m], k.blockavg[:, :], ksq[:, 0:m], start=True, stop=True)
                elif name[0] == "V":
                    for t in range(4 * n, 4 * n + 4):
                        last = pe.matmul(misc[0:rows(t), (t % 4) * 128:(t % 4) * 128 + D],
                                         ctxT[:, j, t * 128:t * 128 + rows(t)], w[:, 2, :], start=True, stop=True)
                else:
                    pe.wait_ge(prod_ready, pb + 1)
                    last = pe.matmul(misc[0:1, 0:H], kmax[:, j, 1:2], k.headmask[:, :], start=True, stop=True)
                last.then_inc(misc_full, 1)

            def mix(b, m, j):
                t, hf = m // 2, m % 2
                if m == 0:
                    pe.wait_ge(v_ready, 4 * b + 4)
                    pe.wait_ge(numer_free, b + 1)
                pe.wait_ge(exped, b * SLOTS + m + 1 + CR_S)
                if t == KT - 1:
                    pe.sem_inc(parted, 1)
                for gg in range(2):
                    g = 2 * hf + gg
                    last = pe.matmul(numer[32 * g:32 * g + 32, 0:GQ], v[0:rows(t), j, t, 32 * g:32 * g + 32],
                                     probs[0:rows(t), m % NP, gg * GQ:(gg + 1) * GQ],
                                     start=(t == 0), stop=(t == KT - 1))
                last.then_inc(mixed, 1)

            def maxima(b, j):
                pe.wait_ge(exped, b * SLOTS + CR_S)
                for h in range(H):
                    pe.wait_ge(max_free, b * H + h + 1)
                    for a, m in KCHUNKS:
                        at_ = (h % 2) * 1536 + a
                        g = h // GH
                        last = pe.matmul(score[0:SQ, at_:at_ + m], qstack[:, j, h, :],
                                         kstack[:, j, g * SK + a:g * SK + a + m], start=True, stop=True)
                    last.then_inc(max_full, 1)
                pe.wait_ge(max_free, b * H + H + 2)
                pe.wait_ge(misc_free, use(b, "max") + 1)
                pe.transpose(misc[0:H, 0:SQ], rowmax[:, :], k.ident[0:SQ, 0:SQ]).then_inc(misc_full, 1)
                pe.wait_ge(shift_ready, b + 1)

            def body(b, j, hh, shifted):
                if not (isinstance(b, int) and b == B):
                    if shifted:
                        maxima(b, j)
                    else:
                        pe.sem_inc(max_full, H)
                        pe.sem_inc(misc_full, 1)
                for n in range(SLOTS):
                    end = isinstance(b, int) and b == B
                    if end and n > Y:
                        break
                    if not end:
                        t, hf = n // 2, n % 2
                        pe.wait_ge(exped, b * SLOTS + n + 1)
                        for gg in range(2):
                            g = 2 * hf + gg
                            to = score[:, (n % 3) * 1024 + gg * 512:(n % 3) * 1024 + gg * 512 + GQ]
                            last = pe.matmul(to, kstack[:, j, g * SK + t * 128:g * SK + (t + 1) * 128],
                                             qstack[:, j, g * GH:(g + 1) * GH, :], start=True, stop=not shifted)
                            if shifted:
                                last = pe.matmul(to, k.ones[0:H, :], shift[:, g * GH:(g + 1) * GH, :],
                                                 start=False, stop=True)
                        last.then_inc(scored, 1)
                        for name, s in at.items():
                            if s == n and hh is not None:
                                piece(b, name, 1 - j, b + 1, hh)
                    if not (isinstance(b, int) and b == 0):
                        if n == SUMS:
                            pe.wait_ge(summed_v, b * (KT - 1) + CR_A)
                            pe.wait_ge(summed_p, b * (KT - 1) + CR_A)
                            pe.wait_ge(misc_free, use(b, "sums") + 1)
                            for g in range(GROUPS):
                                last = pe.matmul(misc[32 * g:32 * g + 32, 0:GQ], k.ones[:, 0:32],
                                                 sums[:, 1 - j, g // 2, (g % 2) * GQ:(g % 2 + 1) * GQ],
                                                 start=True, stop=True)
                            last.then_inc(misc_full, 1)
                        if n == Y:
                            pe.wait_ge(att_ready, b)
                            pe.wait_ge(misc_free, use(b, "y") + 1)
                            pe.matmul(misc[0:SQ, 0:D], att[:, 4, :], w[:, 3, :],
                                      start=True, stop=True).then_inc(misc_full, 1)
                        if n < 2:
                            mix(b - 1, SLOTS - 2 + n, 1 - j)
                    if n >= 2 and not end:
                        mix(b, n - 2, j)

            def batch(b, j, hh):
                if isinstance(b, int) and b == B:
                    body(b, j, hh, False)
                    return
                pe.wait_ge(flag_ready, b + 1)
                pe.wait_ge(stack_in, 256 * b + 256)
                pe.wait_ge(qstack_ready, b + 1)
                pe.sem_inc(parted, 1)
                flag = pe.value_load(unsafe[0:1, j:j + 1], min_val=0, max_val=1)
                with pe.If(flag):
                    body(b, j, hh, True)
                with pe.Else():
                    body(b, j, hh, False)

            for name in prep:
                piece(-1, name, 0, 0, 0)
            pe.wait_ge(tail_clear, 1)
            whole(pe, batch)

        @block.scalar
        def _(act):
            act.sem_inc(exped, CR_S)
            act.wait_ge(cols_in, COLS)
            steps = Chain(act, a_step)
            if normed:
                for g in range(TG):
                    act.wait_ge(q_full, TG + g + 1)
                    steps.done(act.activation(klog[:, 0:NTG], score[:, g * 512:g * 512 + NTG], ACT.Ln,
                                              bias=eps[:, 0:1]))
                    act.activation(qparts[:, 0, g * NTG:(g + 1) * NTG], klog[:, 0:NTG], ACT.Exp,
                                   scale=-0.5).then_inc(q_free, 1)
                    act.wait_ge(q_free, g + 1)

            def evacuate(b, name, j, pb):
                n = int(name[-1])
                a, m = KCHUNKS[n]
                if name[0] == "K" and not masked:
                    act.wait_ge(misc_full, use(b, name) + 1)
                    if not (isinstance(b, int) and b < 0) and n == 0:
                        act.wait_ge(stack_in, 256 * pb)
                    if normed:
                        act.activation(kT[:, a:a + m], misc[:, 0:m], ACT.Identity,
                                       bias=cols[:, 1:2]).then_inc(kraw_ready, 1)
                        act.activation(ksq[:, 0:m], misc[:, 0:m], ACT.Square, bias=cols[:, 1:2]).then_inc(ksq_ready, 1)
                        act.wait_ge(ksq_ready, 3 * pb + n + 1)
                        act.wait_ge(kraw_ready, 3 * pb + n + 1)
                        act.sem_inc(misc_free, 1)
                    else:
                        act.activation(kT[:, a:a + m], misc[:, 0:m], ACT.Identity,
                                       bias=cols[:, 1:2]).then_inc(k_made, 1)
                        act.wait_ge(k_made, 3 * pb + n + 1)
                        act.sem_inc(misc_free, 1)
                if name[0] == "N":
                    act.wait_ge(misc_full, use(b, name) + 1)
                    act.activation(klog[:, 0:m], misc[:, 0:m], ACT.Ln, bias=eps[:, 0:1]).then_inc(misc_free, 1)
                    act.wait_ge(misc_free, use(b, name) + 2)
                    act.wait_ge(kinv_used, 3 * pb + n + 1)
                    act.activation(kinv[:, 0:m], klog[:, 0:m], ACT.Exp, scale=-0.5).then_inc(kinv_ready, 1)

            def batch(b, j, hh):
                if isinstance(b, int) and b == B:
                    return
                for n in range(SLOTS):
                    t, hf = n // 2, n % 2
                    r = rows(t)
                    if masked and n == 0:
                        act.wait_ge(bias_ready, b + 1)
                    act.wait_ge(scored, b * SLOTS + n + 1)
                    act.wait_ge(mixed, b * SLOTS + n + 1 + (CR_M - NP))
                    tb = NP // 2
                    act.wait_ge(summed_p if hf else summed_v,
                                b * (KT - 1) + CR_A + (max(1, t - tb) if t >= tb else t + 1 - tb))
                    act.activation(probs[0:r, n % NP, :].rearrange("p (g q) -> p g q", g=2),
                                   slot_ps[0:r, n % 3, :, 0:GQ], ACT.Exp, scale=HSCALE,
                                   bias=(keybias[0:r, j, t:t + 1] if masked else 0.0)).then_inc(exped, 1)
                    for name, s in at.items():
                        if s == n and hh is not None and name != "bound":
                            evacuate(b, name, 1 - j, b + 1)

            for name in prep:
                if name != "bound":
                    evacuate(-1, name, 0, 0)
            whole(act, batch)

        @block.gpsimd
        def _(pool):
            pool.sem_inc(summed_p, CR_A)

            def block_queries(b, j):
                if not isinstance(b, int) or b >= 2:
                    pool.wait_ge(scored, (b - 1) * SLOTS)
                for g in range(GROUPS):
                    last = pool.tensor_tensor(qstack[:, j, g * GH:(g + 1) * GH, :],
                                              qrep[:, g, b, :].unsqueeze(1).to_broadcast([128, GH, SQ]),
                                              k.groupmask[:, :].unsqueeze(2).to_broadcast([128, GH, SQ]), ALU.mult)
                    last.then_inc(blocked, 1)
                pool.wait_ge(blocked, GROUPS * b + GROUPS)
                pool.sem_inc(qstack_ready, 1)

            def batch(b, j, hh):
                if isinstance(b, int) and b == B:
                    return
                for n in range(1, SLOTS, 2):
                    if n >= 3:
                        add(pool, summed_p, b, n, j, True)
                    if n == 9 and hh is not None:
                        block_queries(b + 1, 1 - j)

            pool.wait_ge(rep_in, 256)
            block_queries(0, 0)
            whole(pool, batch)

        @block.vector
        def _(dve):
            dve.sem_inc(summed_v, CR_A)
            dve.sem_inc(mixed, CR_M)
            dve.sem_inc(misc_free, 1)
            dve.sem_inc(numer_free, 1)
            dve.sem_inc(max_free, 2)
            if normed:
                dve.sem_inc(kinv_used, 1)
            steps = Chain(dve, v_step)
            if normed:
                steps.done(dve.memset(eps[:, :], 1e-6))
            dve.wait_ge(cols_in, COLS)
            if masked:
                steps.done(dve.tensor_scalar(droppedcol[:, :, :], maskcol[:, :, :], 0, NEG * HSCALE, ALU.is_equal, ALU.mult))
            for g in range(TG):
                dve.wait_ge(q_full, g + 1)
                steps.done(dve.tensor_scalar(qT[:, g * BG:(g + 1) * BG, :],
                                             score[:, g * 512:g * 512 + NTG].rearrange("p (b q) -> p b q", q=SQ),
                                             cols[:, 0:1], None, ALU.add))
                if normed:
                    dve.tensor_tensor(qsq[:, g * NTG:(g + 1) * NTG].rearrange("p (b q) -> p b q", q=SQ), qT[:, g * BG:(g + 1) * BG, :],
                                      qT[:, g * BG:(g + 1) * BG, :], ALU.mult).then_inc(q_ready, 1)
            if normed:
                for g in range(TG):
                    dve.wait_ge(q_free, g + 1)
                    steps.done(dve.scalar_tensor_tensor(
                        qT[:, g * BG:(g + 1) * BG, :], qT[:, g * BG:(g + 1) * BG, :], cols[:, 3:4],
                        qparts[:, 0, g * NTG:(g + 1) * NTG].rearrange("p (b q) -> p b q", q=SQ),
                        ALU.mult, ALU.mult))
            dve.memset(kstack[:, :, GROUPS * SK:].bitcast(F32), 0.0).then_inc(tail_clear, 1)
            steps.done(dve.tensor_reduce(qmax[:, :], qT[:, :, :], X, ALU.max, apply_absolute_value=True))
            dve.tensor_copy(qparts[:, 0, :].bitcast(F32R), early[:, 0:NT]).then_inc(q_split, 1)
            dve.wait_ge(q_split, 1)
            dve.tensor_tensor(qparts[:, 1, :].bitcast(F32R), early[:, 0:NT], qparts[:, 0, :], ALU.subtract).then_inc(q_split, 1)
            steps.done(dve.tensor_tensor(k.x[:, :, :], k.x[:, :, :], bo[:, :].unsqueeze(1).to_broadcast([SQ, B, D]), ALU.add))

            fin = Chain(dve, f_step, 10 if masked else 9)

            def piece(b, name, j, pb, hh):
                n = int(name[-1]) if name != "bound" else 0
                if name[0] == "K" and masked:
                    a, m = KCHUNKS[n]
                    if n == 0:
                        dve.wait_ge(row_in, 16 * pb + 16)
                        dve.tensor_scalar(valid[:, :], maskrow[:, :], 0, None, ALU.not_equal).then_inc(valid_ready, 1)
                        dve.wait_ge(valid_ready, pb + 1)
                        if not (isinstance(b, int) and b < 0):
                            dve.wait_ge(stack_in, 256 * pb)
                        if not (isinstance(b, int) and b <= 0):
                            dve.wait_ge(exped, b * SLOTS + CR_S)
                        step(dve.tensor_reduce(anyvalid[:, j:j + 1], valid[:, :], X, ALU.max))
                        dve.tensor_scalar(keybias[:, j, :], droppedcol[:, pb, :], anyvalid[:, j:j + 1], None,
                                          ALU.mult).then_inc(bias_ready, 1)
                    dve.wait_ge(misc_full, use(b, name) + 1)
                    dve.scalar_tensor_tensor(kT[:, a:a + m], misc[:, 0:m], cols[:, 1:2], valid[:, a:a + m],
                                             ALU.add, ALU.mult).then_inc(k_made, 1)
                    dve.wait_ge(k_made, 3 * pb + n + 1)
                    dve.sem_inc(misc_free, 1)
                if name[0] == "N":
                    a, m = KCHUNKS[n]
                    dve.wait_ge(kinv_ready, 3 * pb + n + 1)
                    dve.scalar_tensor_tensor(kT[:, a:a + m], kT[:, a:a + m], cols[:, 4:5], kinv[:, 0:m],
                                             ALU.mult, ALU.mult).then_inc(k_made, 1)
                    dve.wait_ge(k_made, 3 * pb + n + 1)
                    dve.sem_inc(kinv_used, 1)
                if name[0] == ("N" if normed else "K"):
                    a, m = KCHUNKS[n]
                    dve.wait_ge(k_made, 3 * pb + n + 1)
                    dve.tensor_copy(khigh[:, a:a + m].bitcast(F32R), kT[:, a:a + m]).then_inc(k_high, 1)
                    dve.wait_ge(k_high, 3 * pb + n + 1)
                    dve.tensor_tensor(kT[:, a:a + m].bitcast(F32R), kT[:, a:a + m], khigh[:, a:a + m],
                                      ALU.subtract).then_inc(k_split, 1)
                if name[0] == "V":
                    dve.wait_ge(misc_full, use(b, name) + 1)
                    if n == 0 and not (isinstance(b, int) and b <= 0):
                        dve.wait_ge(mixed, b * SLOTS + CR_M)
                    full = [t for t in range(4 * n, 4 * n + 4) if rows(t) == 128]
                    dve.tensor_copy(v[:, j, full[0]:full[-1] + 1, :],
                                    misc[:, 0:128 * len(full)].rearrange("p (t d) -> p t d", d=D)).then_inc(v_ready, 1)
                    if len(full) < 4:
                        dve.tensor_copy(v[0:KLAST, j, KT - 1, :], misc[0:KLAST, 384:384 + D]).then_inc(v_ready, 1)
                    dve.wait_ge(v_ready, 4 * pb + n + 1 + (len(full) < 4))
                    dve.sem_inc(misc_free, 1)
                if name == "bound":
                    dve.wait_ge(k_high, 3 * pb + 3)
                    step(dve.tensor_reduce(kmax[:, j, 0:1], khigh[:, :], X, ALU.max, apply_absolute_value=True))
                    dve.tensor_scalar(kmax[:, j, 1:2], kmax[:, j, 0:1], qmax[:, pb:pb + 1] if isinstance(pb, int)
                                      else qmax[:, bass.ds(pb, 1)], None, ALU.mult).then_inc(prod_ready, 1)
                    dve.wait_ge(misc_full, use(b, name) + 1)
                    step(dve.tensor_reduce(bound[:, j:j + 1], misc[0:1, 0:H], X, ALU.max))
                    dve.sem_inc(misc_free, 1)
                    step(dve.tensor_scalar(bound[:, j:j + 1], bound[:, j:j + 1], SAFE / HSCALE, -1.0, ALU.is_lt, ALU.mult))
                    dve.tensor_scalar(unsafe[:, j:j + 1], bound[:, j:j + 1], 1.0, None, ALU.add).then_inc(flag_ready, 1)

            prep_steps = Chain(dve, v_step)
            prep_steps.n = steps.n
            step = prep_steps.done
            for name in prep:
                piece(-1, name, 0, 0, 0)

            def finish(b, j, n):
                if n == 1:
                    dve.wait_ge(mixed, b * SLOTS + CR_M)
                    dve.tensor_tensor(own[:, :, :], numer[:, 0:GQ].rearrange("p (j q) -> p j q", j=GH),
                                      k.groupmask[:, :].unsqueeze(2).to_broadcast([128, GH, SQ]),
                                      ALU.mult).then_inc(numer_free, 1)
                    dve.wait_ge(numer_free, b + 1)
                    fin.done(dve.tensor_reduce(att[:, 0, :], own[:, :, :].rearrange("p j q -> p q j"), X, ALU.add))
                if n == SUMS:
                    dve.wait_ge(misc_full, use(b, "sums") + 1)
                    fin.done(dve.tensor_tensor(own[:, :, :], misc[:, 0:GQ].rearrange("p (j q) -> p j q", j=GH),
                                               k.groupmask[:, :].unsqueeze(2).to_broadcast([128, GH, SQ]), ALU.mult))
                    dve.sem_inc(misc_free, 1)
                    fin.done(dve.tensor_reduce(att[:, 1, :], own[:, :, :].rearrange("p j q -> p q j"), X, ALU.add))
                    fin.done(dve.reciprocal(att[:, 2, :], att[:, 1, :]))
                    fin.done(dve.tensor_tensor(att[:, 3, :], att[:, 0, :], att[:, 2, :], ALU.mult))
                    dve.tensor_scalar(att[:, 4, :], att[:, 3, :], cols[:, 2:3], None, ALU.add).then_inc(att_ready, 1)
                if n == Y:
                    dve.wait_ge(misc_full, use(b, "y") + 1)
                    fin.done(dve.tensor_tensor(k.x[:, b - 1, :], k.x[:, b - 1, :], misc[0:SQ, 0:D], ALU.add))
                    dve.sem_inc(misc_free, 1)

            def maxima(b, j):
                if not (isinstance(b, int) and b == 0):
                    dve.wait_ge(scored, b * SLOTS)
                if masked:
                    s = Chain(dve, m_step, MSTEPS)
                    s.begin(b)
                    s.done(dve.tensor_scalar(weight[:, :], anyvalid[0:SQ, j:j + 1], -NEG, None, ALU.mult))
                    s.done(dve.tensor_scalar(valid[0:SQ, :], valid[0:SQ, :], -1.0, weight[:, 0:1], ALU.add, ALU.mult))
                for h in range(H):
                    dve.wait_ge(max_full, b * H + h + 1)
                    src = score[0:SQ, (h % 2) * 1536:(h % 2) * 1536 + SK]
                    if masked:
                        s.done(dve.tensor_tensor(lifted[:, :], src, valid[0:SQ, :], ALU.add))
                        src = lifted[:, :]
                    dve.tensor_reduce(rowmax[:, h:h + 1], src, X, ALU.max).then_inc(max_free, 1)
                    if masked:
                        dve.wait_ge(max_free, b * H + h + 3)
                dve.wait_ge(misc_full, use(b, "max") + 1)
                dve.tensor_tensor(shift[:, :, :], misc[0:H, 0:SQ].unsqueeze(1).to_broadcast([H, H, SQ]),
                                  k.negident[:, :].unsqueeze(2).to_broadcast([H, H, SQ]), ALU.mult).then_inc(shift_ready, 1)
                dve.wait_ge(shift_ready, b + 1)
                dve.sem_inc(misc_free, 1)

            MSTEPS = 2 + H
            m_step = c.sem("m_step")

            def batch(b, j, hh):
                nonlocal step
                end = isinstance(b, int) and b == B
                if not end:
                    dve.wait_ge(flag_ready, b + 1)
                    dve.sem_inc(parted, 1)
                    flag = dve.value_load(unsafe[0:1, j:j + 1], min_val=0, max_val=1)
                    with dve.If(flag):
                        maxima(b, j)
                    with dve.Else():
                        if masked:
                            dve.sem_inc(m_step, MSTEPS)
                        dve.sem_inc(max_free, H)
                        dve.sem_inc(shift_ready, 1)
                        dve.sem_inc(misc_free, 1)
                fin.n = 0
                fin.base = b * fin.per
                step = fin.done
                for n in range(SLOTS):
                    if not end and n % 2 == 0 and n >= 2:
                        add(dve, summed_v, b, n, j, False)
                    if not (isinstance(b, int) and b == 0) and n in (1, SUMS, Y):
                        finish(b, j, n)
                    elif isinstance(b, int) and b == 0 and n == 1:
                        for _ in range(6):
                            dve.sem_inc(f_step, 1)
                            fin.n += 1
                    for name, s in at.items():
                        if s == n and hh is not None:
                            piece(b, name, 1 - j, b + 1, hh)
                if isinstance(b, int) and b == B - 1:
                    while fin.n < fin.per:
                        dve.sem_inc(f_step, 1)
                        fin.n += 1

            whole(dve, batch)


def softmax_rows(dve, act_done, ch, logits, top, e, total, inv, probs, exp_ready, exped, E):
    wide = lambda a: a.unsqueeze(2).to_broadcast([SQ, B, E])
    ch.done(dve.tensor_reduce(top[:, :], logits[:, :, :], X, ALU.max))
    dve.tensor_tensor(e[:, :, :], logits[:, :, :], wide(top[:, :]), ALU.subtract).then_inc(exp_ready, 1)
    dve.wait_ge(exped, act_done)
    ch.done(dve.tensor_reduce(total[:, :], e[:, :, :], X, ALU.add))
    ch.done(dve.reciprocal(inv[:, :], total[:, :]))
    ch.done(dve.tensor_tensor(probs[:, :, :], e[:, :, :], wide(inv[:, :]), ALU.mult))


def first_largest(dve, ch, k, values, top, hit, onehot, E):
    wide = lambda a: a.unsqueeze(2).to_broadcast([SQ, B, E])
    back = k.backwards[0:SQ, 0:E].unsqueeze(1).to_broadcast([SQ, B, E])
    ch.done(dve.tensor_reduce(top[:, :], values[:, :, :], X, ALU.max))
    ch.done(dve.tensor_tensor(hit[:, :, :], values[:, :, :], wide(top[:, :]), ALU.is_equal))
    ch.done(dve.tensor_tensor(hit[:, :, :], hit[:, :, :], back, ALU.mult))
    best = k.best
    ch.done(dve.tensor_reduce(best[:, :], hit[:, :, :], X, ALU.max))
    ch.done(dve.tensor_tensor(onehot[:, :, :], wide(best[:, :]), back, ALU.is_equal))


def l1_ffn(nc, k, ins):
    with Scope(nc, "f1") as c:
        w = c.sb("w", [128, 3, D])
        mu = c.sb("mu", [128, 4])
        xr = c.sb("xr", [128, B, SQ])
        xk = c.sb("xk", [128, B, SQ])
        act_k = c.sb("act_k", [128, NT])
        sq_k = c.sb("sq_k", [128, NT])
        gate = c.sb("gate", [SQ, B, D])
        part = c.sb("part", [SQ, B, D])
        ps = c.ps("ps", [128, TG, 512])
        pv = c.ps("pv", [128, TG, 512])
        w_in, k_full, relued, squared, r_full, gated, v_full, step = c.sems(
            "w_in k_full relued squared r_full gated v_full step")
        block = c.block()

        @block.sync
        def _(sp):
            for n, name in enumerate(("W_rT", "W_kT", "W_vT")):
                sp.dma_start(w[:, n, :], ins[name]).then_inc(w_in, 16)
            sp.dma_start(mu[:, 0:1], ins["mu_r"]).then_inc(w_in, 16)
            sp.dma_start(mu[:, 1:2], ins["mu_k"]).then_inc(w_in, 16)

        @block.vector
        def _(dve):
            ch = Chain(dve, step)
            xn = k.xnT[:, :].rearrange("p (b q) -> p b q", q=SQ)
            dve.wait_ge(w_in, 80)
            ch.done(dve.tensor_scalar(mu[:, 2:4], mu[:, 0:2], -1.0, 1.0, ALU.mult, ALU.add))
            for n, t in ((1, xk), (0, xr)):
                ch.done(dve.tensor_scalar(t[:, :, :], xn, mu[:, n:n + 1], None, ALU.mult))
                ch.done(dve.scalar_tensor_tensor(t[:, :, 1:SQ], xn[:, :, 0:SQ - 1], mu[:, 2 + n:3 + n],
                                                 t[:, :, 1:SQ], ALU.mult, ALU.add))
            for g in range(TG):
                dve.wait_ge(relued, g + 1)
                dve.tensor_tensor(sq_k[:, g * NTG:(g + 1) * NTG], act_k[:, g * NTG:(g + 1) * NTG],
                                  act_k[:, g * NTG:(g + 1) * NTG], ALU.mult).then_inc(squared, 1)
            for g in range(TG):
                dve.wait_ge(v_full, g + 1)
                dve.wait_ge(gated, g + 1)
                s = slice(g * BG, (g + 1) * BG)
                ch.done(dve.tensor_tensor(part[:, s, :], gate[:, s, :],
                                          pv[0:SQ, g, :].rearrange("q (b d) -> q b d", d=D), ALU.mult))
                ch.done(dve.tensor_tensor(k.x[:, s, :], k.x[:, s, :], part[:, s, :], ALU.add))

        @block.tensor
        def _(pe):
            pe.wait_ge(step, 3)
            for g in range(TG):
                pe.matmul(ps[:, g, 0:NTG], w[:, 1, :], xk[:, g * BG:(g + 1) * BG, :],
                          start=True, stop=True).then_inc(k_full, 1)
            pe.wait_ge(step, 5)
            for g in range(TG):
                pe.wait_ge(relued, g + 1)
                for j in range(BG):
                    last = pe.matmul(ps[0:SQ, g, j * D:(j + 1) * D], xr[:, g * BG + j, :], w[:, 0, :],
                                     start=True, stop=True)
                last.then_inc(r_full, 1)
            for g in range(TG):
                pe.wait_ge(squared, g + 1)
                for j in range(BG):
                    b = g * BG + j
                    last = pe.matmul(pv[0:SQ, g, j * D:(j + 1) * D], sq_k[:, b * SQ:(b + 1) * SQ], w[:, 2, :],
                                     start=True, stop=True)
                last.then_inc(v_full, 1)

        @block.scalar
        def _(act):
            for g in range(TG):
                act.wait_ge(k_full, g + 1)
                act.activation(act_k[:, g * NTG:(g + 1) * NTG], ps[:, g, 0:NTG], ACT.Relu).then_inc(relued, 1)
            for g in range(TG):
                act.wait_ge(r_full, g + 1)
                act.activation(gate[:, g * BG:(g + 1) * BG, :], ps[0:SQ, g, :].rearrange("q (b d) -> q b d", d=D),
                               ACT.Sigmoid).then_inc(gated, 1)


def l2_ffn(nc, k, ins):
    with Scope(nc, "f2") as c:
        router = c.sb("router", [128, E2])
        router_b = c.sb("router_b", [SQ, E2])
        w1 = c.sb("w1", [128, (HC2 + SC2) * 128])
        b1 = c.sb("b1", [128, HC2 + SC2])
        w2 = c.sb("w2", [128, HC2 + SC2, D])
        b2 = c.sb("b2", [E2, D])
        sb2 = c.sb("sb2", [ES, D])
        logits, e, probs, left, chosen, weights = (
            c.sb(n, [SQ, B, E2]) for n in "logits e probs left chosen weights".split())
        top, total, inv = (c.sb(n, [SQ, B]) for n in "top total inv".split())
        best8 = c.sb("best8", [SQ, B, K2])
        weightsT = c.sb("weightsT", [E2, NT])
        own = c.sb("own", [E2, 2, BG, SQ])
        NH = 4
        hidden = c.sb("hidden", [128, HC2 + SC2, NTG])
        ph = c.ps("ph", [128, 3, 512])
        pw = c.ps("pw", [128, 3, 512])
        py = c.ps("py", [128, 2, 512])
        (w_in, routed, exp_ready, exped, top_done, weighted, turned, weightsT_ready, own_ready,
         h_full, h_free, w_full, h_ready, scaled, y_full, y_added, step) = c.sems(
            "w_in routed exp_ready exped top_done weighted turned weightsT own_ready h_full h_free w_full "
            "h_ready scaled y_full y_added step")
        block = c.block()
        CH = HC2 + SC2

        @block.sync
        def _(sp):
            for t, name in ((router[:, :], "router_w"), (w1[:, 0:HC2 * 128], "w1"), (w1[:, HC2 * 128:], "sw1"),
                            (b1[:, 0:HC2], "b1"), (b1[:, HC2:], "sb1"), (w2[:, 0:HC2, :], "w2"),
                            (w2[:, HC2:, :], "sw2"), (b2[:, :], "b2"), (sb2[:, :], "sb2")):
                sp.dma_start(t, ins[name]).then_inc(w_in, 16)
            sp.dma_start(router_b[:, :], ins["router_b"].partition_broadcast(SQ)).then_inc(w_in, 16)

        @block.vector
        def _(dve):
            ch = Chain(dve, step)
            dve.wait_ge(w_in, 160)
            dve.wait_ge(routed, 1)
            ch.done(dve.tensor_tensor(logits[:, :, :], ph[0:SQ, 0:2, :].rearrange("q g (b e) -> q (g b) e", e=E2),
                                      router_b[:, :].unsqueeze(1).to_broadcast([SQ, B, E2]), ALU.add))
            softmax_rows(dve, 1, ch, logits, top, e, total, inv, probs, exp_ready, exped, E2)
            for b in range(B):
                dve.max(best8[:, b, :], probs[:, b, :]).then_inc(top_done, 1)
            for b in range(B):
                dve.wait_ge(top_done, b + 1)
                last = dve.match_replace(left[:, b, :], best8[:, b, :], probs[:, b, :], -1.0)
                last.then_inc(top_done, 1)
            dve.wait_ge(top_done, 2 * B)
            ch.done(dve.tensor_scalar(chosen[:, :, :], left[:, :, :], -1.0, None, ALU.is_equal))
            ch.done(dve.tensor_tensor(chosen[:, :, :], chosen[:, :, :], probs[:, :, :], ALU.mult))
            ch.done(dve.tensor_reduce(total[:, :], best8[:, :, :], X, ALU.add))
            ch.done(dve.reciprocal(inv[:, :], total[:, :]))
            dve.tensor_tensor(weights[:, :, :], chosen[:, :, :], inv[:, :].unsqueeze(2).to_broadcast([SQ, B, E2]),
                              ALU.mult).then_inc(weighted, 1)
            dve.wait_ge(weightsT_ready, TG)

            def group(g, first):
                if not first:
                    dve.wait_ge(y_full, g)
                dve.tensor_copy(own[:, 0, :, :], weightsT[:, :].rearrange("e (g b q) -> e g b q", g=TG, q=SQ)[:, g, :, :])\
                    .then_inc(own_ready, 1)
                for ci in range(HC2):
                    dve.wait_ge(w_full, g * HC2 + ci + 1)
                    dve.wait_ge(h_ready, g * CH + ci + 1)
                    dve.tensor_tensor(hidden[:, ci, :], hidden[:, ci, :], pw[:, ci % 3, 0:NTG], ALU.mult).then_inc(scaled, 1)
                dve.wait_ge(y_full, g + 1)
                dve.tensor_tensor(k.x[:, :, :].rearrange("q (g b) d -> q g b d", b=BG)[:, g, :, :],
                                  k.x[:, :, :].rearrange("q (g b) d -> q g b d", b=BG)[:, g, :, :],
                                  py[0:SQ, 0, :].rearrange("q (b d) -> q b d", d=D), ALU.add).then_inc(y_added, 1)

            group(0, True)
            with dve.Fori(1, TG) as g:
                group(g, False)

        @block.scalar
        def _(act):
            act.wait_ge(exp_ready, 1)
            act.activation(e[:, :, :], e[:, :, :], ACT.Exp).then_inc(exped, 1)
            for g in range(TG):
                act.wait_ge(turned, g + 1)
                act.copy(weightsT[:, g * NTG:(g + 1) * NTG], pw[0:E2, g % 2, 0:NTG]).then_inc(weightsT_ready, 1)
            act.sem_inc(h_free, 3)

            def group(g):
                for ci in range(CH):
                    act.wait_ge(h_full, g * CH + ci + 1)
                    if ci == 0:
                        act.wait_ge(y_full, g) if not isinstance(g, int) or g > 0 else None
                    act.activation(hidden[:, ci, :], ph[:, ci % 3, 0:NTG], ACT.Silu, bias=b1[:, ci:ci + 1]).then_inc(h_ready, 1)
                    act.wait_ge(h_ready, g * CH + ci + 1)
                    act.sem_inc(h_free, 1)

            group(0)
            with act.Fori(1, TG) as g:
                group(g)

        @block.tensor
        def _(pe):
            pe.wait_ge(w_in, 160)
            for b in range(B):
                last = pe.matmul(ph[0:SQ, b // 8, (b % 8) * E2:(b % 8 + 1) * E2], k.xnT[:, b * SQ:(b + 1) * SQ],
                                 router[:, :], start=True, stop=True)
            last.then_inc(routed, 1)
            pe.wait_ge(weighted, 1)
            for g in range(TG):
                if g >= 2:
                    pe.wait_ge(weightsT_ready, g - 1)
                for j in range(BG):
                    last = pe.transpose(pw[0:E2, g % 2, j * SQ:(j + 1) * SQ], weights[:, g * BG + j, :], k.ident[0:SQ, 0:SQ])
                last.then_inc(turned, 1)
            pe.wait_ge(weightsT_ready, TG)
            xg = k.xnT[:, :].rearrange("p (g t) -> p g t", g=TG)

            def group(g):
                pe.wait_ge(own_ready, g + 1)
                for ci in range(CH):
                    pe.wait_ge(h_free, g * CH + ci + 1)
                    pe.matmul(ph[:, ci % 3, 0:NTG], w1[:, ci * 128:(ci + 1) * 128], xg[:, g, :],
                              start=True, stop=True).then_inc(h_full, 1)
                    if ci < HC2:
                        if ci >= 3 or not isinstance(g, int):
                            pe.wait_ge(scaled, g * HC2 + ci - 2 if ci >= 3 else g * HC2)
                        pe.matmul(pw[:, ci % 3, 0:NTG], k.expertcols[:, ci, :], own[:, 0, :, :],
                                  start=True, stop=True).then_inc(w_full, 1)
                pe.wait_ge(scaled, g * HC2 + HC2)
                pe.wait_ge(h_ready, g * CH + CH)
                if not isinstance(g, int):
                    pe.wait_ge(y_added, g)
                for j in range(BG):
                    to = py[0:SQ, 0, j * D:(j + 1) * D]
                    for ci in range(CH):
                        pe.matmul(to, hidden[:, ci, j * SQ:(j + 1) * SQ], w2[:, ci, :], start=(ci == 0), stop=False)
                    pe.matmul(to, own[:, 0, j, :], b2[:, :], start=False, stop=False)
                    last = pe.matmul(to, k.ones[0:ES, 0:SQ], sb2[:, :], start=False, stop=True)
                last.then_inc(y_full, 1)

            group(0)
            with pe.Fori(1, TG) as g:
                group(g)


def dense_block(nc, k, ins, tag, layer, E, func, gates, acc, biased):
    with Scope(nc, tag) as c:
        w1 = c.sb("w1", [128, 2, FF])
        w2 = c.sb("w2", [128, 2, FC, D])
        b1 = c.sb("b1", [128, 2, FC])
        own = c.sb("own", [SQ, 2, B])
        hidden = c.sb("hidden", [128, 2, FC, NTG])
        ph = c.ps("ph", [128, 4, 512])
        py = c.ps("py", [128, 2, 512])
        w_in = c.sems("w_in0 w_in1")
        h_full, h_ready, y_full, y_added, own_ready, step = c.sems(
            "h_full h_ready y_full y_added own_ready step")
        block = c.block()
        HALVES = E // 2

        @block.sync
        def _(sp):
            def load(e, j, again=True):
                if again:
                    sp.wait_ge(y_full, TG * e - TG + 2)
                sp.dma_start(w1[:, j, :], ins[f"L{layer}_W1"][e]).then_inc(w_in[j], 16)
                sp.dma_start(w2[:, j, :, :], ins[f"L{layer}_W2"][e].rearrange("(c p) d -> p c d", p=128)).then_inc(w_in[j], 16)
                if biased:
                    sp.dma_start(b1[:, j, :], ins[f"L{layer}_b1"][e]).then_inc(w_in[j], 16)

            load(0, 0, False)
            load(1, 1, False)
            with sp.Fori(1, HALVES) as i:
                load(2 * i, 0)
                load(2 * i + 1, 1)

        W_IN = 48 if biased else 32

        @block.tensor
        def _(pe):
            def up(e, i, j, g):
                s = TG * e + g
                if g == 0:
                    pe.wait_ge(w_in[j], W_IN * i + W_IN)
                for ci in range(FC):
                    pe.wait_ge(h_ready, FC * s + ci + 1)
                    pe.matmul(ph[:, ci, 0:NTG], w1[:, j, ci * 128:(ci + 1) * 128], k.xnT[:, g * NTG:(g + 1) * NTG],
                              start=True, stop=True).then_inc(h_full, 1)

            def down(e, j, g, prev=0):
                s = TG * e + g - prev
                pe.wait_ge(h_ready, FC * s + 2 * FC)
                pe.wait_ge(y_added, s + 1)
                gg = (g - prev) % TG
                for jb in range(BG):
                    for ci in range(FC):
                        last = pe.matmul(py[0:SQ, gg % 2, jb * D:(jb + 1) * D], hidden[:, gg % 2, ci, jb * SQ:(jb + 1) * SQ],
                                         w2[:, j, ci, :], start=(ci == 0), stop=(ci == FC - 1))
                last.then_inc(y_full, 1)

            up(0, 0, 0, 0)
            for g in range(1, TG):
                up(0, 0, 0, g)
                down(0, 0, g, 1)
            up(1, 0, 1, 0)
            down(1, 0, 0, 1)
            for g in range(1, TG):
                up(1, 0, 1, g)
                down(1, 1, g, 1)
            with pe.Fori(1, HALVES) as i:
                for j in range(2):
                    for g in range(TG):
                        up(2 * i + j, i, j, g)
                        down(2 * i + j, j if g else 1 - j, g, 1)
            down(E, 1, 0, 1)

        @block.scalar
        def _(act):
            act.sem_inc(h_ready, FC)

            def ups(e, i, j):
                if biased:
                    act.wait_ge(w_in[j], W_IN * i + W_IN)
                for g in range(TG):
                    s = TG * e + g
                    act.wait_ge(y_full, s + 1)
                    for ci in range(FC):
                        act.wait_ge(h_full, FC * s + ci + 1)
                        act.activation(hidden[:, g % 2, ci, :], ph[:, ci, 0:NTG], func,
                                       bias=(b1[:, j, ci:ci + 1] if biased else 0.0)).then_inc(h_ready, 1)

            act.sem_inc(y_full, 2)
            with act.Fori(0, HALVES) as i:
                ups(2 * i, i, 0)
                ups(2 * i + 1, i, 1)

        @block.vector
        def _(dve):
            dve.sem_inc(y_added, 2)

            def adds(e, j):
                dve.tensor_copy(own[:, j, :], gates[:, :, e]).then_inc(own_ready, 1)
                dve.wait_ge(own_ready, e + 1)
                for g in range(TG):
                    s = TG * e + g
                    dve.wait_ge(y_full, s + 3)
                    for jb in range(BG):
                        b = g * BG + jb
                        dve.scalar_tensor_tensor(acc[:, b, :], py[0:SQ, g % 2, jb * D:(jb + 1) * D], own[:, j, b:b + 1],
                                                 acc[:, b, :], ALU.mult, ALU.add).then_inc(step, 1)
                    dve.wait_ge(step, s * BG + BG)
                    dve.sem_inc(y_added, 1)

            with dve.Fori(0, HALVES) as i:
                adds(2 * i, 0)
                adds(2 * i + 1, 1)


def l0_ffn(nc, k, ins):
    with Scope(nc, "f0") as o:
        acc = o.sb("acc", [SQ, B, D])
        gates = o.sb("gates", [SQ, B, E0])
        router = o.sb("router", [128, L0, E0])
        for layer in range(L0):
            with Scope(nc, f"f0r{layer}") as c:
                logits, e, probs, hit, onehot = (c.sb(n, [SQ, B, E0]) for n in "logits e probs hit onehot".split())
                top, total, inv = (c.sb(n, [SQ, B]) for n in "top total inv".split())
                ps = c.ps("ps", [128, 512])
                r_in, routed, exp_ready, exped, step = c.sems("r_in routed exp_ready exped step")
                block = c.block()

                @block.sync
                def _(sp):
                    if layer == 0:
                        sp.dma_start(router[:, :, :], ins["L0_routers"]).then_inc(r_in, 16)

                @block.tensor
                def _(pe):
                    if layer == 0:
                        pe.wait_ge(r_in, 16)
                    for b in range(B):
                        last = pe.matmul(ps[0:SQ, b * E0:(b + 1) * E0], k.xnT[:, b * SQ:(b + 1) * SQ],
                                         router[:, layer, :], start=True, stop=True)
                    last.then_inc(routed, 1)

                @block.scalar
                def _(act):
                    act.wait_ge(exp_ready, 1)
                    act.activation(e[:, :, :], e[:, :, :], ACT.Exp).then_inc(exped, 1)

                @block.vector
                def _(dve):
                    ch = Chain(dve, step)
                    ch.done(dve.memset(acc[:, :, :], 0.0))
                    dve.wait_ge(routed, 1)
                    ch.done(dve.tensor_copy(logits[:, :, :], ps[0:SQ, 0:B * E0].rearrange("q (b e) -> q b e", e=E0)))
                    softmax_rows(dve, 1, ch, logits, top, e, total, inv, probs, exp_ready, exped, E0)
                    first_largest(dve, ch, k, probs, top, hit, onehot, E0)
                    ch.done(dve.tensor_tensor(gates[:, :, :], onehot[:, :, :], probs[:, :, :], ALU.mult))

            dense_block(nc, k, ins, f"f0d{layer}", 0, E0, ACT.Silu, gates, acc, False)
            with Scope(nc, f"f0t{layer}") as c:
                turned_ps = c.ps("turned", [128, TG, 512])
                turned, copied, added = c.sems("turned copied added")
                block = c.block()
                if layer < L0 - 1:
                    @block.tensor
                    def _(pe):
                        for g in range(TG):
                            for j in range(BG):
                                last = pe.transpose(turned_ps[:, g, j * SQ:(j + 1) * SQ], acc[:, g * BG + j, :],
                                                    k.ident[0:SQ, 0:SQ])
                            last.then_inc(turned, 1)

                    @block.scalar
                    def _(act):
                        for g in range(TG):
                            act.wait_ge(turned, g + 1)
                            act.copy(k.xnT[:, g * NTG:(g + 1) * NTG], turned_ps[:, g, 0:NTG]).then_inc(copied, 1)
                else:
                    @block.vector
                    def _(dve):
                        dve.tensor_tensor(k.x[:, :, :], k.x[:, :, :], acc[:, :, :], ALU.add).then_inc(added, 1)


def l3_ffn(nc, k, ins):
    with Scope(nc, "f3") as o:
        gates = o.sb("gates", [SQ, B, E3])
        with Scope(nc, "f3r") as c:
            wg = c.sb("wg", [128, E3])
            b2 = c.sb("b2", [E3, D])
            logits, e, probs, hit, one1, one2, rest, pos, before, keep, left = (
                c.sb(n, [SQ, B, E3]) for n in "logits e probs hit one1 one2 rest pos before keep left".split())
            count = c.sb("count", [SQ, 2, B, E3])
            start_ = c.sb("start", [SQ, 2, B + 1, E3])
            top, total, inv, g1, g2, den = (c.sb(n, [SQ, B]) for n in "top total inv g1 g2 den".split())
            gatesT = c.sb("gatesT", [E3, NT])
            ps = c.ps("ps", [128, 512])
            pc = c.ps("pc", [128, 512])
            pt = c.ps("pt", [128, TG, 512])
            r_in, routed, exp_ready, exped, ones_ready, counted, gated, turned, turned_in, b2_full, step, s_step = c.sems(
                "r_in routed exp_ready exped ones_ready counted gated turned turned_in b2_full step s_step")
            block = c.block()

            @block.sync
            def _(sp):
                sp.dma_start(wg[:, :], ins["L3_Wg"]).then_inc(r_in, 16)
                sp.dma_start(b2[:, :], ins["L3_b2"]).then_inc(r_in, 16)

            @block.tensor
            def _(pe):
                pe.wait_ge(r_in, 32)
                for b in range(B):
                    last = pe.matmul(ps[0:SQ, b * E3:(b + 1) * E3], k.xnT[:, b * SQ:(b + 1) * SQ], wg[:, :],
                                     start=True, stop=True)
                last.then_inc(routed, 1)
                pe.wait_ge(ones_ready, 1)
                for n, one in enumerate((one1, one2)):
                    pe.matmul(pc[0:SQ, n * 256:n * 256 + B * E3], k.lower[0:SQ, 0:SQ], one[:, :, :], start=True, stop=True)
                    last = pe.matmul(pc[0:SQ, n * 256 + 128:n * 256 + 128 + B * E3], k.ones[0:SQ, 0:SQ], one[:, :, :],
                                     start=True, stop=True)
                last.then_inc(counted, 1)
                pe.wait_ge(gated, 1)
                for g in range(TG):
                    for j in range(BG):
                        last = pe.transpose(pt[0:E3, g, j * SQ:(j + 1) * SQ], gates[:, g * BG + j, :], k.ident[0:SQ, 0:SQ])
                last.then_inc(turned, 1)
                pe.wait_ge(turned_in, 1)
                for b in range(B):
                    last = pe.matmul(pt[0:SQ, b // 4, (b % 4) * D:(b % 4 + 1) * D], gatesT[:, b * SQ:(b + 1) * SQ], b2[:, :],
                                     start=True, stop=True)
                last.then_inc(b2_full, 1)

            @block.scalar
            def _(act):
                act.wait_ge(exp_ready, 1)
                act.activation(e[:, :, :], e[:, :, :], ACT.Exp).then_inc(exped, 1)
                act.wait_ge(turned, 1)
                act.copy(gatesT[:, :].rearrange("e (g t) -> e g t", g=TG), pt[0:E3, :, 0:NTG]).then_inc(turned_in, 1)

            @block.vector
            def _(dve):
                ch = Chain(dve, step)
                wide = lambda a: a.unsqueeze(2).to_broadcast([SQ, B, E3])
                dve.wait_ge(routed, 1)
                ch.done(dve.tensor_copy(logits[:, :, :], ps[0:SQ, 0:B * E3].rearrange("q (b e) -> q b e", e=E3)))
                softmax_rows(dve, 1, ch, logits, top, e, total, inv, probs, exp_ready, exped, E3)
                first_largest(dve, ch, k, probs, top, hit, one1, E3)
                ch.done(dve.tensor_scalar(hit[:, :, :], one1[:, :, :], -3.0e38, None, ALU.mult))
                ch.done(dve.tensor_scalar(left[:, :, :], one1[:, :, :], -1.0, 1.0, ALU.mult, ALU.add))
                ch.done(dve.tensor_tensor(rest[:, :, :], logits[:, :, :], left[:, :, :], ALU.mult))
                ch.done(dve.tensor_tensor(rest[:, :, :], rest[:, :, :], hit[:, :, :], ALU.add))
                first_largest(dve, ch, k, rest, top, hit, one2, E3)
                dve.sem_inc(ones_ready, 1)
                for one, g in ((one1, g1), (one2, g2)):
                    ch.done(dve.tensor_tensor(hit[:, :, :], one[:, :, :], probs[:, :, :], ALU.mult))
                    ch.done(dve.tensor_reduce(g[:, :], hit[:, :, :], X, ALU.add))
                ch.done(dve.tensor_tensor(den[:, :], g1[:, :], g2[:, :], ALU.add))
                ch.done(dve.tensor_scalar(den[:, :], den[:, :], 1e-9, None, ALU.add))
                ch.done(dve.reciprocal(inv[:, :], den[:, :]))
                for g in (g1, g2):
                    ch.done(dve.tensor_tensor(g[:, :], g[:, :], inv[:, :], ALU.mult))
                dve.wait_ge(counted, 1)
                ch.done(dve.memset(start_[:, 0, 0, :], 0.0))
                for n in range(2):
                    ch.done(dve.tensor_copy(count[:, n, :, :],
                                            pc[0:SQ, n * 256 + 128:n * 256 + 256].rearrange("q (b e) -> q b e", e=E3)))
                    if n:
                        ch.done(dve.tensor_copy(start_[:, 1, 0, :], start_[:, 0, B, :]))
                    for b in range(B):
                        ch.done(dve.tensor_tensor(start_[:, n, b + 1, :], start_[:, n, b, :], count[:, n, b, :], ALU.add))
                for n, (one, g) in enumerate(((one1, g1), (one2, g2))):
                    ch.done(dve.tensor_tensor(pos[:, :, :], pc[0:SQ, n * 256:n * 256 + 128].rearrange("q (b e) -> q b e", e=E3),
                                              start_[:, n, 0:B, :], ALU.add))
                    ch.done(dve.tensor_scalar(keep[:, :, :], pos[:, :, :], float(CAP), None, ALU.is_lt))
                    ch.done(dve.tensor_tensor(keep[:, :, :], keep[:, :, :], one[:, :, :], ALU.mult))
                    t = (before, left)[n]
                    ch.done(dve.tensor_tensor(t[:, :, :], keep[:, :, :], wide(g[:, :]), ALU.mult))
                dve.tensor_tensor(gates[:, :, :], before[:, :, :], left[:, :, :], ALU.add).then_inc(gated, 1)
                dve.wait_ge(b2_full, 1)
                ch.done(dve.tensor_tensor(k.x[:, :, :].rearrange("q (g b) d -> q g b d", b=BG),
                                          k.x[:, :, :].rearrange("q (g b) d -> q g b d", b=BG),
                                          pt[0:SQ, :, :].rearrange("q g (b d) -> q g b d", d=D), ALU.add))

        dense_block(nc, k, ins, "f3d", 3, E3, ACT.Gelu, gates, k.x, True)


def store(nc, k, out):
    with Scope(nc, "store") as c:
        (stored,) = c.sems("stored")
        block = c.block()

        @block.sync
        def _(sp):
            sp.dma_start(out.rearrange("b q d -> q b d"), k.x[:, :, :]).then_inc(stored, 16)
            sp.wait_ge(stored, 16)


class Shared:
    pass


def program(nc, ins, out, stages=8):
    k = Shared()
    with Scope(nc, "k") as c:
        k.x = c.sb("x", [SQ, B, D])
        k.xnT = c.sb("xnT", [128, NT])
        k.ident = c.sb("ident", [128, 128])
        k.negident = c.sb("negident", [H, H])
        k.headmask = c.sb("headmask", [128, H])
        k.groupmask = c.sb("groupmask", [128, GH])
        k.blockavg = c.sb("blockavg", [128, 128])
        k.expertcols = c.sb("expertcols", [E2, HC2, 128])
        k.lower = c.sb("lower", [128, 128])
        k.ones = c.sb("ones", [128, 128])
        k.backwards = c.sb("backwards", [128, E2])
        k.best = c.sb("best", [SQ, B])
        setup(nc, k, ins)
        steps = [
            lambda: l0_attention(nc, k, ins),
            lambda: l0_ffn(nc, k, ins),
            lambda: heads_attention(nc, k, ins, 1),
            lambda: l1_ffn(nc, k, ins),
            lambda: heads_attention(nc, k, ins, 2),
            lambda: l2_ffn(nc, k, ins),
            lambda: heads_attention(nc, k, ins, 3),
            lambda: l3_ffn(nc, k, ins),
        ]
        for n in STAGES:
            layernorm(nc, k, f"ln{n}")
            steps[n]()
        store(nc, k, out)


STAGES = range(8)


def _layouts(a):
    import numpy as np

    col = lambda v: v.reshape(-1, 1)
    t = {
        "x": a["x"], "ctx_1024": a["ctx_1024"], "ctxT": a["ctx_1024"].transpose(0, 2, 1),
        "mask_BxSxS2_ik0": a["mask_BxSxS2_ik0"],
        "keymask": a["mask_Bx1x1xS2_ik0"].reshape(B, 1, SK),
        "L0_xattn_W": a["L0_xattn_W"].T, "L0_xattn_b": col(a["L0_xattn_b"]),
        "L0_routers": a["L0_ffn_routers"].transpose(1, 0, 2),
        "L0_W1": a["L0_ffn_W1"], "L0_W2": a["L0_ffn_W2"],
        "L3_Wg": a["L3_ffn_Wg"], "L3_W1": a["L3_ffn_W1"], "L3_W2": a["L3_ffn_W2"],
        "L3_b1": a["L3_ffn_b1"].reshape(E3, FC, 128).transpose(0, 2, 1), "L3_b2": a["L3_ffn_b2"],
        "mu_r": col(a["L1_ffn_mu_r"]), "mu_k": col(a["L1_ffn_mu_k"]),
        "W_rT": a["L1_ffn_W_r"].T, "W_kT": a["L1_ffn_W_k"].T, "W_vT": a["L1_ffn_W_v"].T,
        "router_w": a["L2_ffn_router_w"], "router_b": a["L2_ffn_router_b"].reshape(1, E2),
        "w1": a["L2_ffn_w1"].transpose(1, 0, 2).reshape(D, E2 * H2),
        "b1": a["L2_ffn_b1"].reshape(HC2, 128).T,
        "w2": a["L2_ffn_w2"].reshape(HC2, 128, D).transpose(1, 0, 2), "b2": a["L2_ffn_b2"],
        "sw1": a["L2_ffn_sw1"].transpose(1, 0, 2).reshape(D, ES * HS2),
        "sb1": a["L2_ffn_sb1"].reshape(SC2, 128).T,
        "sw2": a["L2_ffn_sw2"].reshape(SC2, 128, D).transpose(1, 0, 2), "sb2": a["L2_ffn_sb2"],
    }
    pad = np.zeros((B, 128 * KT), a["mask_Bx1x1xS2_ik0"].dtype)
    pad[:, 0:SK] = a["mask_Bx1x1xS2_ik0"].reshape(B, SK)
    t["keymask_cols"] = pad.reshape(B, KT, 128).transpose(2, 0, 1)
    for n, (q, kk, v, o, turn) in {
        1: ("L1_xattn_wq", "L1_xattn_wk", "L1_xattn_wv", "L1_xattn_wo", False),
        2: ("L2_xattn_wq", "L2_xattn_wk", "L2_xattn_wv", "L2_xattn_wo", True),
    }.items():
        for name, w in zip(("wq", "wk", "wv", "wo"), (q, kk, v, o)):
            t[f"{name}{n}"] = a[w].T if turn else a[w]
        for name in ("bq", "bk", "bv"):
            t[f"{name}{n}"] = col(a[f"L{n}_xattn_{name}"])
        t[f"bo{n}"] = a[f"L{n}_xattn_bo"].reshape(1, D)
    t["wq3"], t["wo3"] = a["L3_xattn_Wq"], a["L3_xattn_Wproj"]
    t["wk3"], t["wv3"] = a["L3_xattn_Wkv"][:, 0:D], a["L3_xattn_Wkv"][:, D:]
    t["bq3"] = col(a["L3_xattn_bq"])
    t["bk3"], t["bv3"] = col(a["L3_xattn_bkv"][0:D]), col(a["L3_xattn_bkv"][D:])
    t["bo3"] = a["L3_xattn_bproj"].reshape(1, D)
    t["gq3"], t["gk3"] = col(np.tile(a["L3_xattn_gq"], H)), col(np.tile(a["L3_xattn_gk"], H))
    return {n: np.ascontiguousarray(v) for n, v in t.items()}


def kernel(**inputs):
    import numpy as np
    import concourse.bacc as bacc
    from concourse.bass_utils import run_bass_kernel_spmd as run

    nc = bacc.Bacc("TRN2", target_bir_lowering=False, num_devices=1)
    arrays = _layouts({n: np.asarray(v) for n, v in inputs.items()})
    ins = {n: nc.dram_tensor(f"in_{n}", a.shape, mybir.dt.from_np(a.dtype), kind="ExternalInput").ap()
           for n, a in arrays.items()}
    out = nc.dram_tensor("out_x", (B, SQ, D), F32, kind="ExternalOutput").ap()
    program(nc, ins, out)
    r = run(nc, [{f"in_{n}": a for n, a in arrays.items()}], core_ids=[0])
    return r.results[0]["out_x"]
```

```python
from contextlib import ExitStack

import concourse.bass as bass
from concourse import mybir

F32 = mybir.dt.float32
F32R = mybir.dt.float32r
I32 = mybir.dt.int32
U32 = mybir.dt.uint32
ALU = mybir.AluOpType
ACT = mybir.ActivationFunctionType
X = mybir.AxisListType.X

B, SQ, D = 16, 100, 128
SK = 1444
NT = B * SQ
KT = (SK + 127) // 128
KLAST = SK - 128 * (KT - 1)
H, HD = 16, 8
GH = 4
GROUPS = H // GH
GQ = GH * SQ
HALF = 2 * GQ
SLOTS = 2 * KT
TG = 4
BG = B // TG
NTG = NT // TG
E0, FF, L0 = 16, 512, 4
FC = FF // 128
MOST = (NT + 127) // 128
GB = 4
BLOCKS = -(-(NT // 128 + E0) // GB) * GB
E2, H2, K2 = 64, 32, 8
HC2 = E2 * H2 // 128
ES, HS2 = 2, 256
SC2 = ES * HS2 // 128
E3, K3 = 8, 2
CAP = 2 * K3 * NT // E3
NEG = -1.0e9
HSCALE = float(HD) ** -0.5
KCHUNKS = [(0, 512), (512, 512), (1024, SK - 1024)]
SAFE = 60.0


def rows(t):
    return 128 if t < KT - 1 else KLAST


class Chain:

    def __init__(self, eng, sem, per=0):
        self.eng, self.sem, self.per, self.base, self.n = eng, sem, per, 0, 0

    def begin(self, b):
        assert self.n in (0, self.per), (self.n, self.per)
        self.base, self.n = b * self.per, 0

    def done(self, ins):
        ins.then_inc(self.sem, 1)
        self.n += 1
        self.eng.wait_ge(self.sem, self.base + self.n)


class Scope:

    def __init__(self, nc, tag):
        self.nc, self.tag, self.stack, self.taken = nc, tag, ExitStack(), []

    def __enter__(self):
        self.stack.__enter__()
        return self

    def __exit__(self, *a):
        said = self.stack.__exit__(*a)
        if self.taken:
            self.nc.clear_and_free_semaphores(self.taken)
            self.nc.all_engine_barrier()
        return said

    def sb(self, name, shape, dtype=F32):
        return self.stack.enter_context(self.nc.sbuf_tensor(f"{self.tag}_{name}", shape, dtype))

    def ps(self, name, shape):
        return self.stack.enter_context(self.nc.psum_tensor(f"{self.tag}_{name}", shape, F32))

    def sem(self, name):
        self.taken.append(self.nc.alloc_semaphore(f"{self.tag}_{name}"))
        return self.taken[-1]

    def sems(self, names):
        return [self.sem(n) for n in names.split()]

    def block(self):
        return self.stack.enter_context(self.nc.Block())


def setup(nc, k, ins):
    with Scope(nc, "setup") as c:
        x_in, filled, cut, made = c.sems("x_in filled cut made")
        block = c.block()

        @block.sync
        def _(sp):
            sp.dma_start(k.x[:, :, :], ins["x"].rearrange("b q d -> q b d")).then_inc(x_in, 16)
            sp.wait_ge(x_in, 16)

        @block.gpsimd
        def _(pool):
            pool.memset(k.ident[:, :], 0.0).then_inc(filled, 1)
            pool.memset(k.headmask[:, :], 1.0).then_inc(filled, 1)
            pool.memset(k.blockavg[:, :], 1.0 / HD).then_inc(filled, 1)
            pool.memset(k.lower[:, :], 1.0).then_inc(filled, 1)
            pool.memset(k.ones[:, :], 1.0).then_inc(filled, 1)
            pool.wait_ge(filled, 5)

            def select(t, pattern, base, mult, op, fill=0.0):
                pool.affine_select(out=t, in_=t, pattern=pattern, base=base, channel_multiplier=mult,
                                   compare_op=op, fill=fill).then_inc(cut, 1)

            select(k.headmask[:, :], [[-HD, H]], 0, 1, ALU.is_ge)
            select(k.blockavg[:, :].rearrange("p (h d) -> p h d", d=HD), [[-HD, H], [0, HD]], 0, 1, ALU.is_ge)
            pool.wait_ge(cut, 2)
            select(k.headmask[:, :], [[HD, H]], HD - 1, -1, ALU.is_ge)
            select(k.blockavg[:, :].rearrange("p (h d) -> p h d", d=HD), [[HD, H], [0, HD]], HD - 1, -1, ALU.is_ge)
            select(k.ident[:, :], [[-1, 128]], 0, 1, ALU.not_equal, 1.0)
            select(k.lower[:, :], [[1, 128]], 0, -1, ALU.is_gt)
            pool.iota(k.backwards[:, :], [[-1, E2]], base=E2, channel_multiplier=0,
                      allow_small_or_imprecise_dtypes=True).then_inc(cut, 1)
            pool.wait_ge(cut, 7)
            pool.sem_inc(made, 1)

        @block.vector
        def _(dve):
            dve.wait_ge(made, 1)
            ch = Chain(dve, made)
            ch.n = 1
            ch.done(dve.tensor_reduce(k.groupmask[:, :], k.headmask[:, :].rearrange("p (g j) -> p j g", j=GH), X, ALU.add))
            ch.done(dve.tensor_scalar(k.negident[:, :], k.ident[0:H, 0:H], -1.0, None, ALU.mult))


def layernorm(nc, k, tag, rows_to=None, loads=None):
    with Scope(nc, tag) as c:
        centred = c.sb("centred", [SQ, B, D])
        square = c.sb("square", [SQ, B, D]) if rows_to is None else rows_to
        total, mean, spread, var, std, inv = (c.sb(n, [SQ, B]) for n in "total mean spread var std inv".split())
        turned = c.ps("turned", [128, TG, 512])
        step, centred_ready, squared, var_ready, std_ready, xn_ready, turned_ready, copied = c.sems(
            "step centred squared var std xn turned copied")
        halves = [slice(h * B // 2, (h + 1) * B // 2) for h in range(2)]
        block = c.block()

        if loads is not None:
            @block.sync
            def _(sp):
                loads(sp)

        @block.vector
        def _(dve):
            ch = Chain(dve, step)
            for h, s in enumerate(halves):
                ch.done(dve.tensor_reduce(total[:, s], k.x[:, s, :], X, ALU.add))
                ch.done(dve.tensor_scalar(mean[:, s], total[:, s], 1.0 / D, None, ALU.mult))
                dve.tensor_tensor(centred[:, s, :], k.x[:, s, :],
                                  mean[:, s].unsqueeze(2).to_broadcast([SQ, B // 2, D]), ALU.subtract).then_inc(centred_ready, 1)
            for h, s in enumerate(halves):
                dve.wait_ge(squared, h + 1)
                ch.done(dve.tensor_reduce(spread[:, s], square[:, s, :], X, ALU.add))
                dve.tensor_scalar(var[:, s], spread[:, s], 1.0 / D, 1e-5, ALU.mult, ALU.add).then_inc(var_ready, 1)
            for h, s in enumerate(halves):
                dve.wait_ge(std_ready, h + 1)
                ch.done(dve.reciprocal(inv[:, s], std[:, s]))
                for g in range(h * TG // 2, (h + 1) * TG // 2):
                    s = slice(g * BG, (g + 1) * BG)
                    dve.tensor_tensor(square[:, s, :], centred[:, s, :],
                                      inv[:, s].unsqueeze(2).to_broadcast([SQ, BG, D]), ALU.mult).then_inc(xn_ready, 1)

        @block.tensor
        def _(pe):
            for g in range(TG):
                pe.wait_ge(xn_ready, g + 1)
                for j in range(BG):
                    last = pe.transpose(turned[:, g, j * SQ:(j + 1) * SQ], square[:, g * BG + j, :], k.ident[0:SQ, 0:SQ])
                last.then_inc(turned_ready, 1)

        @block.scalar
        def _(act):
            act.preload_act_table(ACT.Sqrt)
            for h, s in enumerate(halves):
                act.wait_ge(centred_ready, h + 1)
                act.activation(square[:, s, :], centred[:, s, :], ACT.Square).then_inc(squared, 1)
            for h, s in enumerate(halves):
                act.wait_ge(var_ready, h + 1)
                act.activation(std[:, s], var[:, s], ACT.Sqrt).then_inc(std_ready, 1)
            for g in range(TG):
                act.wait_ge(turned_ready, g + 1)
                act.copy(k.xnT[:, g * NTG:(g + 1) * NTG], turned[:, g, 0:NTG]).then_inc(copied, 1)


def l0_attention(nc, k, m, ins):
    with Scope(nc, "l0a") as c:
        w = c.sb("w", [128, D])
        bias = c.sb("b", [128, 1])
        (w_in,) = c.sems("w_in")

        def loads(sp):
            sp.dma_start(w[:, :], ins["L0_xattn_W"]).then_inc(w_in, 16)
            sp.dma_start(bias[:, :], ins["L0_xattn_b"]).then_inc(w_in, 16)

        layernorm(nc, k, "ln0", loads=loads)
        qT = c.sb("qT", [128, B, SQ])
        q1 = c.sb("q1", [128, 2, SQ])
        ctxT = c.sb("ctxT", [128, 2, SK])
        ctxN = c.sb("ctx", [128, 2, KT, D])
        mask = c.sb("mask", [SQ, 2, SK], I32)
        dropped = c.sb("dropped", [SQ, 2, SK])
        logits = c.sb("logits", [SQ, 2, SK])
        probs = c.sb("probs", [SQ, 2, SK])
        probsT = c.sb("probsT", [128, 2, KT, SQ])
        negmax = c.sb("negmax", [SQ, 2])
        total = c.sb("total", [SQ, 2])
        inv = c.sb("inv", [SQ, 2])
        ps = c.ps("ps", [128, 2, 3 * 512])
        py = c.ps("py", [128, 2, 512])
        q_made, q_kept = c.sems("q_made q_kept")
        ctxT_in = c.sems("ctxT_in0 ctxT_in1")
        ctx_in = c.sems("ctx_in0 ctx_in1")
        mask_in = c.sems("mask_in0 mask_in1")
        m_made, pooled = c.sems("m_made pooled")
        q1_ready, scored, masked, maxed, exped, turned, kept, outed, added, step = c.sems(
            "q1_ready scored masked maxed exped turned kept outed added step")
        block = c.block()

        @block.sync
        def _(sp):
            def load(b, j, again):
                if again:
                    sp.wait_ge(scored, b - 1)
                sp.dma_start(ctxT[:, j, :], ins["ctxT"][b]).then_inc(ctxT_in[j], 16)
                if again:
                    sp.wait_ge(masked, b - 1)
                sp.dma_start(mask[:, j, :], ins["mask_BxSxS2_ik0"][b]).then_inc(mask_in[j], 16)
                if again:
                    sp.wait_ge(outed, b + 1)
                n = 128 * (KT - 1)
                sp.dma_start(ctxN[:, j, 0:KT - 1, :],
                             ins["ctx_1024"][b][0:n, :].rearrange("(t p) d -> p t d", p=128)).then_inc(ctx_in[j], 16)
                sp.dma_start(ctxN[0:KLAST, j, KT - 1, :], ins["ctx_1024"][b][n:SK, :]).then_inc(ctx_in[j], 16)

            load(0, 0, False)
            load(1, 1, False)
            with sp.Fori(0, (B - 2) // 2) as i:
                load(2 * i + 2, 0, True)
                load(2 * i + 3, 1, True)

        @block.gpsimd
        def _(pool):
            pool.memset(m.rows[:, :, :], 0.0).then_inc(m_made, 1)
            pool.iota(m.multiples[:, :], [[128, MOST]], base=0, channel_multiplier=0,
                      allow_small_or_imprecise_dtypes=True).then_inc(m_made, 1)
            pool.iota(m.block_number[:, :], [[1, BLOCKS]], base=0, channel_multiplier=0,
                      allow_small_or_imprecise_dtypes=True).then_inc(m_made, 1)
            pool.memset(m.is_before[:, :, :], 1.0).then_inc(m_made, 1)
            pool.wait_ge(m_made, 4)
            pool.affine_select(out=m.is_before[:, :, :], in_=m.is_before[:, :, :], pattern=[[1, E0], [-1, E0]], base=0,
                               channel_multiplier=0, compare_op=ALU.is_gt, fill=0.0).then_inc(m_made, 1)
            pool.wait_ge(m_made, 5)
            pool.dma_start(m.router[:, :, :], ins["L0_routers"]).then_inc(m.router_in, 16)
            for at in range(0, BLOCKS * 128, SQ * B):
                n = min(SQ * B, BLOCKS * 128 - at) // B * B
                pool.dma_start(m.sorted[at:at + n, :].rearrange("(q b) d -> q b d", b=B),
                               m.rows[0:n // B, :, :]).then_inc(m.cleared, 16)
            with pool.Fori(0, E0) as e:
                pool.wait_ge(scored, e + 1)
                pool.sem_inc(pooled, 1)
                pool.dma_start(m.w1[:, bass.ds(e, 1), :].rearrange("p e f -> p (e f)"), ins["L0_W1"][e]).then_inc(m.weights_in, 16)
                pool.dma_start(m.w2[:, bass.ds(e, 1), :, :].rearrange("p e c d -> p (e c) d"),
                               ins["L0_W2"][e].rearrange("(c p) d -> p c d", p=128)).then_inc(m.weights_in, 16)

        @block.tensor
        def _(pe):
            pe.wait_ge(w_in, 32)
            for g in range(TG):
                if g >= 2:
                    pe.wait_ge(q_kept, g - 1)
                pe.matmul(py[:, g % 2, 0:NTG], w[:, :], k.xnT[:, g * NTG:(g + 1) * NTG],
                          start=True, stop=True).then_inc(q_made, 1)

            def scores(b, h, j):
                pe.wait_ge(ctxT_in[j], 16 * h + 16)
                pe.wait_ge(q1_ready, b + 1)
                pe.wait_ge(kept, b + 1)
                for at, n in KCHUNKS:
                    last = pe.matmul(ps[0:SQ, j, at:at + n], q1[:, j, :], ctxT[:, j, at:at + n],
                                     start=True, stop=True)
                last.then_inc(scored, 1)

            def outputs(b, h, j):
                pe.wait_ge(exped, b + 1)
                for t in range(KT):
                    last = pe.transpose(ps[0:rows(t), j, t * 128:t * 128 + SQ],
                                        probs[:, j, t * 128:t * 128 + rows(t)], k.ident[0:SQ, 0:SQ])
                last.then_inc(turned, 1)
                pe.wait_ge(kept, b + 3)
                pe.wait_ge(ctx_in[j], 32 * h + 32)
                pe.wait_ge(added, b + 1)
                for t in range(KT):
                    last = pe.matmul(py[0:SQ, j, 0:D], probsT[0:rows(t), j, t, :], ctxN[0:rows(t), j, t, :],
                                     start=(t == 0), stop=(t == KT - 1))
                last.then_inc(outed, 1)

            scores(0, 0, 0)
            with pe.Fori(0, (B - 2) // 2) as i:
                scores(2 * i + 1, i, 1)
                outputs(2 * i, i, 0)
                scores(2 * i + 2, i + 1, 0)
                outputs(2 * i + 1, i, 1)
            scores(B - 1, B // 2 - 1, 1)
            outputs(B - 2, B // 2 - 1, 0)
            outputs(B - 1, B // 2 - 1, 1)

        @block.scalar
        def _(act):
            act.sem_inc(kept, 2)

            def exps(b, j):
                act.wait_ge(maxed, b + 1)
                act.wait_ge(turned, b + 1)
                act.wait_ge(added, b + 1)
                act.activation(probs[:, j, :], logits[:, j, :], ACT.Exp, bias=negmax[:, j:j + 1],
                               accum_out=total[:, j:j + 1]).then_inc(exped, 1)

            def turns(b, j):
                act.wait_ge(turned, b + 3)
                act.wait_ge(outed, b + 1)
                act.copy(probsT[:, j, 0:KT - 1, :],
                         ps[:, j, 0:128 * (KT - 1)].rearrange("p (t q) -> p t q", q=128)[:, :, 0:SQ]).then_inc(step, 1)
                act.copy(probsT[0:KLAST, j, KT - 1, :],
                         ps[0:KLAST, j, 128 * (KT - 1):128 * (KT - 1) + SQ]).then_inc(step, 1)
                act.wait_ge(step, 2 * b + 2)
                act.sem_inc(kept, 1)

            act.sem_inc(turned, 2)
            act.sem_inc(outed, 2)
            exps(0, 0)
            with act.Fori(0, (B - 2) // 2) as i:
                turns(2 * i, 0)
                exps(2 * i + 1, 1)
                turns(2 * i + 1, 1)
                exps(2 * i + 2, 0)
            turns(B - 2, 0)
            exps(B - 1, 1)
            turns(B - 1, 1)

        @block.vector
        def _(dve):
            dve.sem_inc(added, 2)
            for g in range(TG):
                dve.wait_ge(q_made, g + 1)
                dve.tensor_scalar(qT[:, g * BG:(g + 1) * BG, :], py[:, g % 2, 0:NTG].rearrange("p (b q) -> p b q", q=SQ), bias[:, 0:1],
                                  None, ALU.add).then_inc(q_kept, 1)
            dve.wait_ge(q_kept, TG)
            PER = 4
            base = c.sem("dve_step")

            def maxes(b, h, j):
                dve.tensor_copy(q1[:, j, :], qT[:, b, :]).then_inc(q1_ready, 1)
                dve.wait_ge(mask_in[j], 16 * h + 16)
                dve.tensor_scalar(dropped[:, j, :], mask[:, j, :], -1.0, 1.0, ALU.mult, ALU.add).then_inc(masked, 1)
                dve.wait_ge(masked, b + 1)
                dve.wait_ge(scored, b + 1)
                dve.scalar_tensor_tensor(logits[:, j, :], dropped[:, j, :], NEG, ps[0:SQ, j, 0:SK],
                                         ALU.mult, ALU.add).then_inc(base, 1)
                dve.wait_ge(base, b + 1)
                dve.tensor_reduce(negmax[:, j:j + 1], logits[:, j, :], X, ALU.max, negate=True).then_inc(maxed, 1)

            def adds(b, j):
                dve.wait_ge(exped, b + 1)
                dve.reciprocal(inv[:, j:j + 1], total[:, j:j + 1]).then_inc(inv_ready, 1)
                dve.wait_ge(outed, b + 3)
                dve.wait_ge(inv_ready, b + 1)
                dve.scalar_tensor_tensor(k.x[:, b, :], py[0:SQ, j, 0:D], inv[:, j:j + 1], k.x[:, b, :],
                                         ALU.mult, ALU.add).then_inc(added, 1)

            inv_ready = c.sem("inv_ready")
            maxes(0, 0, 0)
            with dve.Fori(0, (B - 2) // 2) as i:
                maxes(2 * i + 1, i, 1)
                adds(2 * i, 0)
                maxes(2 * i + 2, i + 1, 0)
                adds(2 * i + 1, 1)
            maxes(B - 1, B // 2 - 1, 1)
            adds(B - 2, 0)
            adds(B - 1, 1)


def heads_attention(nc, k, ins, layer):
    masked, normed = layer == 2, layer == 3
    with Scope(nc, f"a{layer}") as c:
        w = c.sb("w", [128, 4, D])
        cols = c.sb("cols", [128, 8])
        bo = c.sb("bo", [SQ, D])
        ctxT = c.sb("ctxT", [128, 2, SK])
        maskcol = c.sb("maskcol", [128, B, KT], I32) if masked else None
        w_in, cols_in, ctx_in = c.sem("w_in"), c.sem("cols_in"), c.sems("ctx_in0 ctx_in1")

        def loads(sp):
            for n, name in enumerate(("wq", "wk", "wv", "wo")):
                sp.dma_start(w[:, n, :], ins[f"{name}{layer}"]).then_inc(w_in, 16)
            names = ["bq", "bk", "bv"] + (["gq", "gk"] if normed else [])
            for n, name in enumerate(names):
                sp.dma_start(cols[:, n:n + 1], ins[f"{name}{layer}"]).then_inc(cols_in, 16)
            sp.dma_start(bo[:, :], ins[f"bo{layer}"].partition_broadcast(SQ)).then_inc(cols_in, 16)
            if masked:
                sp.dma_start(maskcol[:, :, :], ins["keymask_cols"]).then_inc(cols_in, 16)
            for b in range(2):
                sp.dma_start(ctxT[:, b, :], ins["ctxT"][b]).then_inc(ctx_in[b], 16)

        layernorm(nc, k, f"ln{layer}", loads=loads)
        qrep = c.sb("qrep", [128, GROUPS, B, SQ])
        qmax = c.sb("qmax", [128, B])
        kT = c.sb("kT", [128, SK])
        khigh = c.sb("khigh", [128, SK])
        kstack = c.sb("kstack", [128, 2, GROUPS * SK + 128 - KLAST], F32R)
        v = c.sb("v", [128, 2, KT, D])
        qstack = c.sb("qstack", [128, 2, H, SQ], F32R)
        NP = 6
        probs = c.sb("probs", [128, NP, HALF])
        sums = c.sb("sums", [128, 2, 2, HALF])
        own = c.sb("own", [128, GH, SQ])
        att = c.sb("att", [128, 5, SQ])
        kmax = c.sb("kmax", [128, 2, 2])
        bound = c.sb("bound", [1, 2])
        unsafe = c.sb("unsafe", [1, 2], I32)
        rowmax = c.sb("rowmax", [SQ, H])
        shift = k.xnT[0:H, :].rearrange("h (a q) -> h a q", q=SQ)
        early = probs[:, :, :].rearrange("p n c -> p (n c)")
        qT = early[:, 0:NT].rearrange("p (b q) -> p b q", q=SQ)
        qsq = early[:, NT:2 * NT]
        qparts = sums[:, :, :, :].rearrange("p n h c -> p n (h c)")
        if masked:
            maskrow = c.sb("maskrow", [128, SK], I32)
            valid = c.sb("valid", [128, SK])
            anyvalid = c.sb("anyvalid", [128, 2])
            droppedcol = c.sb("droppedcol", [128, B, KT])
            keybias = c.sb("keybias", [128, 2, KT])
            lifted = kT[0:SQ, :]
            weight = c.sb("weight", [SQ, 1])
        if normed:
            eps = c.sb("eps", [128, 1])
            ksq = c.sb("ksq", [128, 512])
            klog = c.sb("klog", [128, 512])
            kinv = c.sb("kinv", [128, 512])
        score = c.ps("score", [128, 6 * 512])
        numer = c.ps("numer", [128, 512])
        misc = c.ps("misc", [128, 512])
        slot_ps = score[:, :].rearrange("p (s g c) -> p s g c", s=3, g=2)

        q_full, q_free, q_ready, row_in = c.sems("q_full q_free q_ready row_in")
        scored, exped, mixed, summed_v, summed_p = c.sems("scored exped mixed summed_v summed_p")
        misc_full, misc_free = c.sems("misc_full misc_free")
        k_made, k_high, k_split, stack_in, q_split, v_ready, qstack_ready, numer_free, att_ready = c.sems(
            "k_made k_high k_split stack_in q_split v_ready qstack_ready numer_free att_ready")
        rep_in = c.sems("rep_in0 rep_in1")
        prod_ready, flag_ready, tail_clear = c.sems("prod_ready flag_ready tail_clear")
        max_full, max_free, shift_ready = c.sems("max_full max_free shift_ready")
        valid_ready, bias_ready, ksq_ready, kraw_ready, kinv_ready, kinv_used = c.sems(
            "valid_ready bias_ready ksq_ready kraw_ready kinv_ready kinv_used")
        v_step, f_step, a_step, parted, blocked = c.sems("v_step f_step a_step parted blocked")
        block = c.block()

        if normed:
            uses = dict(K0=1, N0=2, K1=3, N1=4, K2=6, sums=7, N2=9, V0=11, y=13, V1=16, V2=17, bound=20)
        elif masked:
            uses = dict(K0=1, K1=3, sums=6, K2=8, y=10, V0=13, V1=15, V2=17, bound=20)
        else:
            uses = dict(K0=2, sums=4, K1=6, K2=9, y=12, V0=14, V1=16, V2=18, bound=20)
        SUMS, Y = uses["sums"], uses["y"]
        prep = [n for n in uses if n not in ("sums", "y")]
        at = {n: uses[n] for n in prep}
        AHEAD = dict(K=1 if masked else 0, N=0, V=2 if masked else 1, b=2, s=0 if normed else 1, y=0 if normed else 2)
        dve_at = {n: uses[n] - AHEAD[n[0]] for n in uses}
        dve_at["peak"] = dve_at[prep[-5]] + 1
        QUERIES_AT = 9
        order = ["max"] + list(uses)
        PRE, USES = len(prep), len(order)

        def use(b, name):
            if isinstance(b, int):
                if b < 0:
                    return prep.index(name)
                if b == 0:
                    return PRE + (["max"] + prep).index(name)
                if b == B - 1:
                    return PRE + b * USES - 2 + ["max", "sums", "y"].index(name)
                if b == B:
                    return use(B - 1, "y") + ["max", "sums", "y"].index(name)
            return PRE + b * USES - 2 + order.index(name)

        COLS = 16 * (4 + (2 if normed else 0) + (1 if masked else 0))
        CR_S, CR_M, CR_A = 3, NP // 2, NP // 2

        def whole(eng, batch):
            batch(0, 0, 0)
            with eng.Fori(0, (B - 2) // 2) as i:
                batch(2 * i + 1, 1, i + 1)
                batch(2 * i + 2, 0, i + 1)
            batch(B - 1, 1, None)
            batch(B, 0, None)

        def add(eng, done, b, n, j, pooled):
            t, hf = n // 2, n % 2
            r = rows(t)
            if t == 1 and pooled and not (isinstance(b, int) and b < 1):
                eng.wait_ge(misc_full, use(b - 1, "sums") + 1 if not isinstance(b, int) or b > 1 else PRE)
            eng.wait_ge(exped, b * SLOTS + n + 1 + CR_S)
            if t > 1:
                eng.wait_ge(done, b * (KT - 1) + CR_A + t - 1)
            old = probs[0:r, (n - 2) % NP, :] if t == 1 else sums[0:r, j, hf, :]
            eng.tensor_tensor(sums[0:r, j, hf, :], old, probs[0:r, n % NP, :], ALU.add).then_inc(done, 1)

        def replicate(eng, groups, done):
            for part, n in enumerate((0, 0, 1, 1)):
                if part in (0, 2):
                    eng.wait_ge(q_split, n + 1)
                for g in groups:
                    eng.dma_start(qrep[32 * part:32 * part + 32, g, :, :].rearrange("p b q -> p (b q)"),
                                  qparts[32 * g:32 * g + 32, n, :]).then_inc(done, 16)

        @block.sync
        def _(sp):
            def load(b, j, free_at):
                sp.wait_ge(misc_full, free_at)
                sp.dma_start(ctxT[:, j, :], ins["ctxT"][b]).then_inc(ctx_in[j], 16)

            def load_row(b):
                if masked:
                    if not isinstance(b, int) or b > 0:
                        sp.wait_ge(valid_ready, b)
                    sp.dma_start(maskrow[:, :], ins["keymask"][b].partition_broadcast(128)).then_inc(row_in, 16)

            def restack(b, j):
                sp.wait_ge(k_split, 3 * b + 3)
                if not isinstance(b, int) or b >= 2:
                    sp.sem_inc(parted, 1)
                    sp.wait_ge(scored, (b - 1) * SLOTS)
                for g in range(GROUPS):
                    for part, src in enumerate((khigh, kT, khigh, kT)):
                        sp.dma_start(kstack[32 * part:32 * part + 32, j, g * SK:(g + 1) * SK].bitcast(F32),
                                     src[32 * g:32 * g + 32, :]).then_inc(stack_in, 16)

            replicate(sp, range(2, GROUPS), rep_in[1])
            load_row(0)
            restack(0, 0)
            load_row(1)
            load(2, 0, use(-1, "V2") + 1)
            restack(1, 1)
            load_row(2)
            load(3, 1, use(0, "V2") + 1)
            with sp.Fori(0, (B - 4) // 2) as i:
                for n in range(2):
                    b = 2 * i + 1 + n
                    restack(b + 1, n)
                    load_row(b + 2)
                    load(b + 3, n, use(b, "V2") + 1)
            restack(B - 2, 0)
            load_row(B - 1)
            restack(B - 1, 1)

        @block.tensor
        def _(pe):
            pe.wait_ge(w_in, 64)
            for g in range(TG):
                pe.matmul(score[:, g * 512:g * 512 + NTG], w[:, 0, :], k.xnT[:, g * NTG:(g + 1) * NTG],
                          start=True, stop=True).then_inc(q_full, 1)
            if normed:
                for g in range(TG):
                    pe.wait_ge(q_ready, g + 1)
                    pe.matmul(score[:, g * 512:g * 512 + NTG], k.blockavg[:, :],
                              qsq[:, g * NTG:(g + 1) * NTG], start=True, stop=True).then_inc(q_full, 1)

            def piece(b, name, j, pb, hh):
                pe.wait_ge(misc_free, use(b, name) + 1)
                n = int(name[-1]) if name != "bound" else 0
                if name[0] == "K":
                    if n == 0:
                        pe.wait_ge(ctx_in[j], 16 * hh + 16)
                    a, m = KCHUNKS[n]
                    last = pe.matmul(misc[:, 0:m], w[:, 1, :], ctxT[:, j, a:a + m], start=True, stop=True)
                elif name[0] == "N":
                    a, m = KCHUNKS[n]
                    pe.wait_ge(ksq_ready, pb * 3 + n + 1)
                    last = pe.matmul(misc[:, 0:m], k.blockavg[:, :], ksq[:, 0:m], start=True, stop=True)
                elif name[0] == "V":
                    for t in range(4 * n, 4 * n + 4):
                        last = pe.matmul(misc[0:rows(t), (t % 4) * 128:(t % 4) * 128 + D],
                                         ctxT[:, j, t * 128:t * 128 + rows(t)], w[:, 2, :], start=True, stop=True)
                else:
                    pe.wait_ge(prod_ready, pb + 1)
                    last = pe.matmul(misc[0:1, 0:H], kmax[:, j, 1:2], k.headmask[:, :], start=True, stop=True)
                last.then_inc(misc_full, 1)

            def mix(b, t, j):
                if t == 0:
                    pe.wait_ge(v_ready, 4 * b + 4)
                    pe.wait_ge(numer_free, b + 1)
                pe.wait_ge(exped, b * SLOTS + 2 * t + 2 + CR_S)
                if t == KT - 1:
                    pe.sem_inc(parted, 1)
                for g in range(GROUPS):
                    last = pe.matmul(numer[32 * g:32 * g + 32, 0:GQ], v[0:rows(t), j, t, 32 * g:32 * g + 32],
                                     probs[0:rows(t), (2 * t + g // 2) % NP, (g % 2) * GQ:(g % 2 + 1) * GQ],
                                     start=(t == 0), stop=(t == KT - 1))
                last.then_inc(mixed, 1)

            def maxima(b, j):
                pe.wait_ge(exped, b * SLOTS + CR_S)
                for h in range(H):
                    pe.wait_ge(max_free, b * H + h + 1)
                    for a, m in KCHUNKS:
                        at_ = (h % 2) * 1536 + a
                        g = h // GH
                        last = pe.matmul(score[0:SQ, at_:at_ + m], qstack[:, j, h, :],
                                         kstack[:, j, g * SK + a:g * SK + a + m], start=True, stop=True)
                    last.then_inc(max_full, 1)
                pe.wait_ge(max_free, b * H + H + 2)
                pe.wait_ge(misc_free, use(b, "max") + 1)
                pe.transpose(misc[0:H, 0:SQ], rowmax[:, :], k.ident[0:SQ, 0:SQ]).then_inc(misc_full, 1)
                pe.wait_ge(shift_ready, b + 1)

            def body(b, j, hh, shifted):
                if not (isinstance(b, int) and b == B):
                    if shifted:
                        maxima(b, j)
                    else:
                        pe.sem_inc(max_full, H)
                        pe.sem_inc(misc_full, 1)
                for n in range(SLOTS):
                    end = isinstance(b, int) and b == B
                    if end and n > Y:
                        break
                    if not end:
                        t, hf = n // 2, n % 2
                        pe.wait_ge(exped, b * SLOTS + n + 1)
                        for gg in range(2):
                            g = 2 * hf + gg
                            to = score[:, (n % 3) * 1024 + gg * 512:(n % 3) * 1024 + gg * 512 + GQ]
                            last = pe.matmul(to, kstack[:, j, g * SK + t * 128:g * SK + (t + 1) * 128],
                                             qstack[:, j, g * GH:(g + 1) * GH, :], start=True, stop=not shifted)
                            if shifted:
                                last = pe.matmul(to, k.ones[0:H, :], shift[:, g * GH:(g + 1) * GH, :],
                                                 start=False, stop=True)
                        last.then_inc(scored, 1)
                        for name, s in at.items():
                            if s == n and hh is not None:
                                piece(b, name, 1 - j, b + 1, hh)
                    if not (isinstance(b, int) and b == 0):
                        if n == SUMS:
                            pe.wait_ge(summed_v, b * (KT - 1) + CR_A)
                            pe.wait_ge(summed_p, b * (KT - 1) + CR_A)
                            pe.wait_ge(misc_free, use(b, "sums") + 1)
                            for g in range(GROUPS):
                                last = pe.matmul(misc[32 * g:32 * g + 32, 0:GQ], k.ones[:, 0:32],
                                                 sums[:, 1 - j, g // 2, (g % 2) * GQ:(g % 2 + 1) * GQ],
                                                 start=True, stop=True)
                            last.then_inc(misc_full, 1)
                        if n == Y:
                            pe.wait_ge(att_ready, b)
                            pe.wait_ge(misc_free, use(b, "y") + 1)
                            pe.matmul(misc[0:SQ, 0:D], att[:, 4, :], w[:, 3, :],
                                      start=True, stop=True).then_inc(misc_full, 1)
                        if n == 1:
                            mix(b - 1, KT - 1, 1 - j)
                    if n >= 3 and n % 2 and not end:
                        mix(b, (n - 3) // 2, j)

            def batch(b, j, hh):
                if isinstance(b, int) and b == B:
                    body(b, j, hh, False)
                    return
                pe.wait_ge(flag_ready, b + 1)
                pe.wait_ge(stack_in, 256 * b + 256)
                pe.wait_ge(qstack_ready, b + 1)
                pe.sem_inc(parted, 1)
                flag = pe.value_load(unsafe[0:1, j:j + 1], min_val=0, max_val=1)
                with pe.If(flag):
                    body(b, j, hh, True)
                with pe.Else():
                    body(b, j, hh, False)

            for name in prep:
                piece(-1, name, 0, 0, 0)
            pe.wait_ge(tail_clear, 1)
            whole(pe, batch)

        @block.scalar
        def _(act):
            act.sem_inc(exped, CR_S)
            if not normed:
                act.preload_act_table(ACT.Exp)
            act.wait_ge(cols_in, COLS)
            steps = Chain(act, a_step)
            if normed:
                act.preload_act_table_set("natural_log_exp_and_others")
                for g in range(TG):
                    act.wait_ge(q_full, TG + g + 1)
                    steps.done(act.activation(klog[:, 0:NTG], score[:, g * 512:g * 512 + NTG], ACT.Ln,
                                              bias=eps[:, 0:1]))
                    act.activation(qparts[:, 0, g * NTG:(g + 1) * NTG], klog[:, 0:NTG], ACT.Exp,
                                   scale=-0.5).then_inc(q_free, 1)
                    act.wait_ge(q_free, g + 1)

            def evacuate(b, name, j, pb):
                n = int(name[-1])
                a, m = KCHUNKS[n] if name[0] != "V" else (0, 0)
                if name[0] == "K" and not masked:
                    act.wait_ge(misc_full, use(b, name) + 1)
                    if not (isinstance(b, int) and b < 0) and n == 0:
                        act.wait_ge(stack_in, 256 * pb)
                    if normed:
                        act.activation(kT[:, a:a + m], misc[:, 0:m], ACT.Identity,
                                       bias=cols[:, 1:2]).then_inc(kraw_ready, 1)
                        act.activation(ksq[:, 0:m], misc[:, 0:m], ACT.Square, bias=cols[:, 1:2]).then_inc(ksq_ready, 1)
                        act.wait_ge(ksq_ready, 3 * pb + n + 1)
                        act.wait_ge(kraw_ready, 3 * pb + n + 1)
                        act.sem_inc(misc_free, 1)
                    else:
                        act.activation(kT[:, a:a + m], misc[:, 0:m], ACT.Identity,
                                       bias=cols[:, 1:2]).then_inc(k_made, 1)
                        act.wait_ge(k_made, 3 * pb + n + 1)
                        act.sem_inc(misc_free, 1)
                if name[0] == "N":
                    act.wait_ge(misc_full, use(b, name) + 1)
                    act.activation(klog[:, 0:m], misc[:, 0:m], ACT.Ln, bias=eps[:, 0:1]).then_inc(misc_free, 1)
                    act.wait_ge(misc_free, use(b, name) + 2)
                    act.wait_ge(kinv_used, 3 * pb + n + 1)
                    act.activation(kinv[:, 0:m], klog[:, 0:m], ACT.Exp, scale=-0.5).then_inc(kinv_ready, 1)
                if name[0] == "V" and masked:
                    act.wait_ge(misc_full, use(b, name) + 1)
                    if n == 0 and not (isinstance(b, int) and b <= 0):
                        act.wait_ge(mixed, b * KT + CR_M)
                    full = [t for t in range(4 * n, 4 * n + 4) if rows(t) == 128]
                    act.copy(v[:, j, full[0]:full[-1] + 1, :],
                                    misc[:, 0:128 * len(full)].rearrange("p (t d) -> p t d", d=D)).then_inc(v_ready, 1)
                    if len(full) < 4:
                        act.copy(v[0:KLAST, j, KT - 1, :], misc[0:KLAST, 384:384 + D]).then_inc(v_ready, 1)
                    act.wait_ge(v_ready, 4 * pb + n + 1 + (len(full) < 4))
                    act.sem_inc(misc_free, 1)

            def batch(b, j, hh):
                if isinstance(b, int) and b == B:
                    return
                for n in range(SLOTS):
                    t, hf = n // 2, n % 2
                    r = rows(t)
                    if masked and n == 0:
                        act.wait_ge(bias_ready, b + 1)
                    act.wait_ge(scored, b * SLOTS + n + 1)
                    if hf == 0:
                        act.wait_ge(mixed, b * KT + t + 1)
                    tb = NP // 2
                    act.wait_ge(summed_p if hf else summed_v,
                                b * (KT - 1) + CR_A + (max(1, t - tb) if t >= tb else t + 1 - tb))
                    act.activation(probs[0:r, n % NP, :].rearrange("p (g q) -> p g q", g=2),
                                   slot_ps[0:r, n % 3, :, 0:GQ], ACT.Exp, scale=HSCALE,
                                   bias=(keybias[0:r, j, t:t + 1] if masked else 0.0)).then_inc(exped, 1)
                    for name, s in at.items():
                        if s == n and hh is not None and name != "bound":
                            evacuate(b, name, 1 - j, b + 1)

            for name in prep:
                if name != "bound":
                    evacuate(-1, name, 0, 0)
            whole(act, batch)

        @block.gpsimd
        def _(pool):
            pool.sem_inc(summed_p, CR_A)

            def block_queries(b, j):
                if not isinstance(b, int) or b >= 2:
                    pool.wait_ge(scored, (b - 1) * SLOTS)
                for g in range(GROUPS):
                    last = pool.tensor_tensor(qstack[:, j, g * GH:(g + 1) * GH, :],
                                              qrep[:, g, b, :].unsqueeze(1).to_broadcast([128, GH, SQ]),
                                              k.groupmask[:, :].unsqueeze(2).to_broadcast([128, GH, SQ]), ALU.mult)
                    last.then_inc(blocked, 1)
                pool.wait_ge(blocked, GROUPS * b + GROUPS)
                pool.sem_inc(qstack_ready, 1)

            def batch(b, j, hh):
                if isinstance(b, int) and b == B:
                    return
                for n in range(1, SLOTS, 2):
                    if n >= 3:
                        add(pool, summed_p, b, n, j, True)
                    if n == QUERIES_AT and hh is not None:
                        block_queries(b + 1, 1 - j)

            replicate(pool, range(0, 2), rep_in[0])
            for n in range(2):
                pool.wait_ge(rep_in[n], 128)
            block_queries(0, 0)
            whole(pool, batch)

        @block.vector
        def _(dve):
            dve.sem_inc(summed_v, CR_A)
            dve.sem_inc(mixed, CR_M)
            dve.sem_inc(misc_free, 1)
            dve.sem_inc(numer_free, 1)
            dve.sem_inc(max_free, 2)
            if normed:
                dve.sem_inc(kinv_used, 1)
            steps = Chain(dve, v_step)
            if normed:
                steps.done(dve.memset(eps[:, :], 1e-6))
            dve.wait_ge(cols_in, COLS)
            if masked:
                steps.done(dve.tensor_scalar(droppedcol[:, :, :], maskcol[:, :, :], 0, NEG * HSCALE, ALU.is_equal, ALU.mult))
            for g in range(TG):
                dve.wait_ge(q_full, g + 1)
                steps.done(dve.tensor_scalar(qT[:, g * BG:(g + 1) * BG, :],
                                             score[:, g * 512:g * 512 + NTG].rearrange("p (b q) -> p b q", q=SQ),
                                             cols[:, 0:1], None, ALU.add))
                if normed:
                    dve.tensor_tensor(qsq[:, g * NTG:(g + 1) * NTG].rearrange("p (b q) -> p b q", q=SQ), qT[:, g * BG:(g + 1) * BG, :],
                                      qT[:, g * BG:(g + 1) * BG, :], ALU.mult).then_inc(q_ready, 1)
            if normed:
                for g in range(TG):
                    dve.wait_ge(q_free, g + 1)
                    steps.done(dve.scalar_tensor_tensor(
                        qT[:, g * BG:(g + 1) * BG, :], qT[:, g * BG:(g + 1) * BG, :], cols[:, 3:4],
                        qparts[:, 0, g * NTG:(g + 1) * NTG].rearrange("p (b q) -> p b q", q=SQ),
                        ALU.mult, ALU.mult))
            dve.memset(kstack[:, :, GROUPS * SK:].bitcast(F32), 0.0).then_inc(tail_clear, 1)
            steps.done(dve.tensor_reduce(qmax[:, :], qT[:, :, :], X, ALU.max, apply_absolute_value=True))
            dve.tensor_copy(qparts[:, 0, :].bitcast(F32R), early[:, 0:NT]).then_inc(q_split, 1)
            dve.wait_ge(q_split, 1)
            dve.tensor_tensor(qparts[:, 1, :].bitcast(F32R), early[:, 0:NT], qparts[:, 0, :], ALU.subtract).then_inc(q_split, 1)

            fin = Chain(dve, f_step, 10 if masked else 9)

            def piece(b, name, j, pb, hh):
                n = int(name[-1]) if name[-1].isdigit() else 0
                if name[0] == "K" and masked:
                    a, m = KCHUNKS[n]
                    if n == 0:
                        dve.wait_ge(row_in, 16 * pb + 16)
                        dve.tensor_scalar(valid[:, :], maskrow[:, :], 0, None, ALU.not_equal).then_inc(valid_ready, 1)
                        dve.wait_ge(valid_ready, pb + 1)
                        if not (isinstance(b, int) and b < 0):
                            dve.wait_ge(stack_in, 256 * pb)
                        if not (isinstance(b, int) and b <= 0):
                            dve.wait_ge(exped, b * SLOTS + CR_S)
                        step(dve.tensor_reduce(anyvalid[:, j:j + 1], valid[:, :], X, ALU.max))
                        dve.tensor_scalar(keybias[:, j, :], droppedcol[:, pb, :], anyvalid[:, j:j + 1], None,
                                          ALU.mult).then_inc(bias_ready, 1)
                    dve.wait_ge(misc_full, use(b, name) + 1)
                    dve.scalar_tensor_tensor(kT[:, a:a + m], misc[:, 0:m], cols[:, 1:2], valid[:, a:a + m],
                                             ALU.add, ALU.mult).then_inc(k_made, 1)
                    dve.wait_ge(k_made, 3 * pb + n + 1)
                    dve.sem_inc(misc_free, 1)
                if name[0] == "N":
                    a, m = KCHUNKS[n]
                    dve.wait_ge(kinv_ready, 3 * pb + n + 1)
                    dve.scalar_tensor_tensor(kT[:, a:a + m], kT[:, a:a + m], cols[:, 4:5], kinv[:, 0:m],
                                             ALU.mult, ALU.mult).then_inc(k_made, 1)
                    dve.wait_ge(k_made, 3 * pb + n + 1)
                    dve.sem_inc(kinv_used, 1)
                if name[0] == ("N" if normed else "K"):
                    a, m = KCHUNKS[n]
                    dve.wait_ge(k_made, 3 * pb + n + 1)
                    dve.tensor_copy(khigh[:, a:a + m].bitcast(F32R), kT[:, a:a + m]).then_inc(k_high, 1)
                    dve.wait_ge(k_high, 3 * pb + n + 1)
                    dve.tensor_tensor(kT[:, a:a + m].bitcast(F32R), kT[:, a:a + m], khigh[:, a:a + m],
                                      ALU.subtract).then_inc(k_split, 1)
                if name[0] == "V" and not masked:
                    dve.wait_ge(misc_full, use(b, name) + 1)
                    if n == 0 and not (isinstance(b, int) and b <= 0):
                        dve.wait_ge(mixed, b * KT + CR_M)
                    full = [t for t in range(4 * n, 4 * n + 4) if rows(t) == 128]
                    dve.tensor_copy(v[:, j, full[0]:full[-1] + 1, :],
                                    misc[:, 0:128 * len(full)].rearrange("p (t d) -> p t d", d=D)).then_inc(v_ready, 1)
                    if len(full) < 4:
                        dve.tensor_copy(v[0:KLAST, j, KT - 1, :], misc[0:KLAST, 384:384 + D]).then_inc(v_ready, 1)
                    dve.wait_ge(v_ready, 4 * pb + n + 1 + (len(full) < 4))
                    dve.sem_inc(misc_free, 1)
                if name == "peak":
                    dve.wait_ge(k_high, 3 * pb + 3)
                    step(dve.tensor_reduce(kmax[:, j, 0:1], khigh[:, :], X, ALU.max, apply_absolute_value=True))
                    dve.tensor_scalar(kmax[:, j, 1:2], kmax[:, j, 0:1], qmax[:, pb:pb + 1] if isinstance(pb, int)
                                      else qmax[:, bass.ds(pb, 1)], None, ALU.mult).then_inc(prod_ready, 1)
                if name == "bound":
                    dve.wait_ge(misc_full, use(b, name) + 1)
                    step(dve.tensor_reduce(bound[:, j:j + 1], misc[0:1, 0:H], X, ALU.max))
                    dve.sem_inc(misc_free, 1)
                    step(dve.tensor_scalar(bound[:, j:j + 1], bound[:, j:j + 1], SAFE / HSCALE, -1.0, ALU.is_lt, ALU.mult))
                    dve.tensor_scalar(unsafe[:, j:j + 1], bound[:, j:j + 1], 1.0, None, ALU.add).then_inc(flag_ready, 1)

            prep_steps = Chain(dve, v_step)
            prep_steps.n = steps.n
            step = prep_steps.done
            for name in prep:
                if name == "bound":
                    piece(-1, "peak", 0, 0, 0)
                piece(-1, name, 0, 0, 0)
            prep_steps.done(dve.tensor_tensor(k.x[:, :, :], k.x[:, :, :], bo[:, :].unsqueeze(1).to_broadcast([SQ, B, D]),
                                              ALU.add))

            def finish(b, j, n):
                if n == 1:
                    dve.wait_ge(mixed, b * KT + CR_M)
                    dve.tensor_tensor(own[:, :, :], numer[:, 0:GQ].rearrange("p (j q) -> p j q", j=GH),
                                      k.groupmask[:, :].unsqueeze(2).to_broadcast([128, GH, SQ]),
                                      ALU.mult).then_inc(numer_free, 1)
                    dve.wait_ge(numer_free, b + 1)
                    fin.done(dve.tensor_reduce(att[:, 0, :], own[:, :, :].rearrange("p j q -> p q j"), X, ALU.add))
                if n == dve_at["sums"]:
                    dve.wait_ge(misc_full, use(b, "sums") + 1)
                    fin.done(dve.tensor_tensor(own[:, :, :], misc[:, 0:GQ].rearrange("p (j q) -> p j q", j=GH),
                                               k.groupmask[:, :].unsqueeze(2).to_broadcast([128, GH, SQ]), ALU.mult))
                    dve.sem_inc(misc_free, 1)
                    fin.done(dve.tensor_reduce(att[:, 1, :], own[:, :, :].rearrange("p j q -> p q j"), X, ALU.add))
                    fin.done(dve.reciprocal(att[:, 2, :], att[:, 1, :]))
                    fin.done(dve.tensor_tensor(att[:, 3, :], att[:, 0, :], att[:, 2, :], ALU.mult))
                    dve.tensor_scalar(att[:, 4, :], att[:, 3, :], cols[:, 2:3], None, ALU.add).then_inc(att_ready, 1)
                if n == dve_at["y"]:
                    dve.wait_ge(misc_full, use(b, "y") + 1)
                    fin.done(dve.tensor_tensor(k.x[:, b - 1, :], k.x[:, b - 1, :], misc[0:SQ, 0:D], ALU.add))
                    dve.sem_inc(misc_free, 1)

            def maxima(b, j):
                if not (isinstance(b, int) and b == 0):
                    dve.wait_ge(scored, b * SLOTS)
                if masked:
                    s = Chain(dve, m_step, MSTEPS)
                    s.begin(b)
                    s.done(dve.tensor_scalar(weight[:, :], anyvalid[0:SQ, j:j + 1], -NEG, None, ALU.mult))
                    s.done(dve.tensor_scalar(valid[0:SQ, :], valid[0:SQ, :], -1.0, weight[:, 0:1], ALU.add, ALU.mult))
                for h in range(H):
                    dve.wait_ge(max_full, b * H + h + 1)
                    src = score[0:SQ, (h % 2) * 1536:(h % 2) * 1536 + SK]
                    if masked:
                        s.done(dve.tensor_tensor(lifted[:, :], src, valid[0:SQ, :], ALU.add))
                        src = lifted[:, :]
                    dve.tensor_reduce(rowmax[:, h:h + 1], src, X, ALU.max).then_inc(max_free, 1)
                    if masked:
                        dve.wait_ge(max_free, b * H + h + 3)
                dve.wait_ge(misc_full, use(b, "max") + 1)
                dve.tensor_tensor(shift[:, :, :], misc[0:H, 0:SQ].unsqueeze(1).to_broadcast([H, H, SQ]),
                                  k.negident[:, :].unsqueeze(2).to_broadcast([H, H, SQ]), ALU.mult).then_inc(shift_ready, 1)
                dve.wait_ge(shift_ready, b + 1)
                dve.sem_inc(misc_free, 1)

            MSTEPS = 2 + H
            m_step = c.sem("m_step")

            def batch(b, j, hh):
                nonlocal step
                end = isinstance(b, int) and b == B
                if not end:
                    dve.wait_ge(flag_ready, b + 1)
                    dve.sem_inc(parted, 1)
                    flag = dve.value_load(unsafe[0:1, j:j + 1], min_val=0, max_val=1)
                    with dve.If(flag):
                        maxima(b, j)
                    with dve.Else():
                        if masked:
                            dve.sem_inc(m_step, MSTEPS)
                        dve.sem_inc(max_free, H)
                        dve.sem_inc(shift_ready, 1)
                        dve.sem_inc(misc_free, 1)
                fin.n = 0
                fin.base = b * fin.per
                step = fin.done
                for n in range(SLOTS):
                    if not end and n % 2 == 0 and n >= 2:
                        add(dve, summed_v, b, n, j, False)
                    if not (isinstance(b, int) and b == 0) and n in (1, dve_at["sums"], dve_at["y"]):
                        finish(b, j, n)
                    elif isinstance(b, int) and b == 0 and n == 1:
                        for _ in range(6):
                            dve.sem_inc(f_step, 1)
                            fin.n += 1
                    for name in prep + ["peak"]:
                        if dve_at[name] == n and hh is not None:
                            piece(b, name, 1 - j, b + 1, hh)
                if isinstance(b, int) and b == B - 1:
                    while fin.n < fin.per:
                        dve.sem_inc(f_step, 1)
                        fin.n += 1

            whole(dve, batch)


def softmax_rows(dve, act_done, ch, logits, top, e, total, inv, probs, exp_ready, exped, E):
    wide = lambda a: a.unsqueeze(2).to_broadcast([SQ, B, E])
    ch.done(dve.tensor_reduce(top[:, :], logits[:, :, :], X, ALU.max))
    dve.tensor_tensor(e[:, :, :], logits[:, :, :], wide(top[:, :]), ALU.subtract).then_inc(exp_ready, 1)
    dve.wait_ge(exped, act_done)
    ch.done(dve.tensor_reduce(total[:, :], e[:, :, :], X, ALU.add))
    ch.done(dve.reciprocal(inv[:, :], total[:, :]))
    ch.done(dve.tensor_tensor(probs[:, :, :], e[:, :, :], wide(inv[:, :]), ALU.mult))


def first_largest(dve, ch, k, values, top, hit, onehot, E):
    wide = lambda a: a.unsqueeze(2).to_broadcast([SQ, B, E])
    back = k.backwards[0:SQ, 0:E].unsqueeze(1).to_broadcast([SQ, B, E])
    ch.done(dve.tensor_reduce(top[:, :], values[:, :, :], X, ALU.max))
    ch.done(dve.tensor_tensor(hit[:, :, :], values[:, :, :], wide(top[:, :]), ALU.is_equal))
    ch.done(dve.tensor_tensor(hit[:, :, :], hit[:, :, :], back, ALU.mult))
    best = k.best
    ch.done(dve.tensor_reduce(best[:, :], hit[:, :, :], X, ALU.max))
    ch.done(dve.tensor_tensor(onehot[:, :, :], wide(best[:, :]), back, ALU.is_equal))


def l1_ffn(nc, k, ins):
    with Scope(nc, "f1") as c:
        w = c.sb("w", [128, 3, D])
        mu = c.sb("mu", [128, 4])
        (w_in,) = c.sems("w_in")

        def loads(sp):
            for n, name in enumerate(("W_rT", "W_kT", "W_vT")):
                sp.dma_start(w[:, n, :], ins[name]).then_inc(w_in, 16)
            sp.dma_start(mu[:, 0:1], ins["mu_r"]).then_inc(w_in, 16)
            sp.dma_start(mu[:, 1:2], ins["mu_k"]).then_inc(w_in, 16)

        layernorm(nc, k, "ln1f", loads=loads)
        xr = c.sb("xr", [128, B, SQ])
        xk = c.sb("xk", [128, B, SQ])
        act_k = c.sb("act_k", [128, NT])
        sq_k = c.sb("sq_k", [128, NT])
        gate = c.sb("gate", [SQ, B, D])
        part = c.sb("part", [SQ, B, D])
        ps = c.ps("ps", [128, TG, 512])
        pv = c.ps("pv", [128, TG, 512])
        k_full, relued, squared, r_full, gated, v_full, step = c.sems(
            "k_full relued squared r_full gated v_full step")
        block = c.block()

        @block.vector
        def _(dve):
            ch = Chain(dve, step)
            xn = k.xnT[:, :].rearrange("p (b q) -> p b q", q=SQ)
            dve.wait_ge(w_in, 80)
            ch.done(dve.tensor_scalar(mu[:, 2:4], mu[:, 0:2], -1.0, 1.0, ALU.mult, ALU.add))
            for n, t in ((1, xk), (0, xr)):
                ch.done(dve.tensor_scalar(t[:, :, :], xn, mu[:, n:n + 1], None, ALU.mult))
                ch.done(dve.scalar_tensor_tensor(t[:, :, 1:SQ], xn[:, :, 0:SQ - 1], mu[:, 2 + n:3 + n],
                                                 t[:, :, 1:SQ], ALU.mult, ALU.add))
            for g in range(TG):
                dve.wait_ge(relued, g + 1)
                dve.tensor_tensor(sq_k[:, g * NTG:(g + 1) * NTG], act_k[:, g * NTG:(g + 1) * NTG],
                                  act_k[:, g * NTG:(g + 1) * NTG], ALU.mult).then_inc(squared, 1)
            for g in range(TG):
                dve.wait_ge(v_full, g + 1)
                dve.wait_ge(gated, g + 1)
                s = slice(g * BG, (g + 1) * BG)
                ch.done(dve.tensor_tensor(part[:, s, :], gate[:, s, :],
                                          pv[0:SQ, g, :].rearrange("q (b d) -> q b d", d=D), ALU.mult))
                ch.done(dve.tensor_tensor(k.x[:, s, :], k.x[:, s, :], part[:, s, :], ALU.add))

        @block.tensor
        def _(pe):
            pe.wait_ge(step, 3)
            for g in range(TG):
                pe.matmul(ps[:, g, 0:NTG], w[:, 1, :], xk[:, g * BG:(g + 1) * BG, :],
                          start=True, stop=True).then_inc(k_full, 1)
            pe.wait_ge(step, 5)
            for g in range(TG):
                pe.wait_ge(relued, g + 1)
                for j in range(BG):
                    last = pe.matmul(ps[0:SQ, g, j * D:(j + 1) * D], xr[:, g * BG + j, :], w[:, 0, :],
                                     start=True, stop=True)
                last.then_inc(r_full, 1)
            for g in range(TG):
                pe.wait_ge(squared, g + 1)
                for j in range(BG):
                    b = g * BG + j
                    last = pe.matmul(pv[0:SQ, g, j * D:(j + 1) * D], sq_k[:, b * SQ:(b + 1) * SQ], w[:, 2, :],
                                     start=True, stop=True)
                last.then_inc(v_full, 1)

        @block.scalar
        def _(act):
            for g in range(TG):
                act.wait_ge(k_full, g + 1)
                act.activation(act_k[:, g * NTG:(g + 1) * NTG], ps[:, g, 0:NTG], ACT.Relu).then_inc(relued, 1)
            for g in range(TG):
                act.wait_ge(r_full, g + 1)
                act.activation(gate[:, g * BG:(g + 1) * BG, :], ps[0:SQ, g, :].rearrange("q (b d) -> q b d", d=D),
                               ACT.Sigmoid).then_inc(gated, 1)


def l2_ffn(nc, k, ins):
    with Scope(nc, "f2") as c:
        router = c.sb("router", [128, E2])
        router_b = c.sb("router_b", [SQ, E2])
        w1 = c.sb("w1", [128, (HC2 + SC2) * 128])
        b1 = c.sb("b1", [128, HC2 + SC2])
        w2 = c.sb("w2", [128, HC2 + SC2, D])
        b2 = c.sb("b2", [2 * E2, D])
        picked = c.sb("picked", [E2, HC2, 128])
        picker = c.sb("picker", [2 * E2, HC2, 128], F32R)
        sb2 = c.sb("sb2", [ES, D])
        (w_in,) = c.sems("w_in")

        def loads(sp):
            for t, name in ((router[:, :], "router_w"), (w1[:, 0:HC2 * 128], "w1"), (w1[:, HC2 * 128:], "sw1"),
                            (b1[:, 0:HC2], "b1"), (b1[:, HC2:], "sb1"), (w2[:, 0:HC2, :], "w2"),
                            (w2[:, HC2:, :], "sw2"), (b2[:, :], "b2"), (sb2[:, :], "sb2")):
                sp.dma_start(t, ins[name]).then_inc(w_in, 16)
            sp.dma_start(router_b[:, :], ins["router_b"].partition_broadcast(SQ)).then_inc(w_in, 16)

        layernorm(nc, k, "ln2f", loads=loads)
        logits, e, probs, left, chosen = (c.sb(n, [SQ, B, E2]) for n in "logits e probs left chosen".split())
        weights = c.sb("weights", [SQ, B, 2, E2])
        top, total, inv = (c.sb(n, [SQ, B]) for n in "top total inv".split())
        best8 = c.sb("best8", [SQ, B, K2])
        weightsT = c.sb("weightsT", [2 * E2, NT])
        own = c.sb("own", [2 * E2, BG, SQ], F32R)
        hidden = c.sb("hidden", [128, HC2 + SC2, NTG])
        ph = c.ps("ph", [128, 3, 512])
        pw = c.ps("pw", [128, 3, 512])
        py = c.ps("py", [128, 2, 512])
        (routed, exp_ready, exped, top_done, weighted, turned, weightsT_ready, own_ready,
         h_full, h_free, w_full, h_ready, scaled, y_full, y_added, step, cut, picker_in) = c.sems(
            "routed exp_ready exped top_done weighted turned weightsT own_ready h_full h_free w_full "
            "h_ready scaled y_full y_added step cut picker_in")
        block = c.block()
        CH = HC2 + SC2

        @block.sync
        def _(sp):
            sp.wait_ge(cut, 3)
            for part in range(2):
                sp.dma_start(picker[part * E2:(part + 1) * E2, :, :].bitcast(F32), picked[:, :, :]).then_inc(picker_in, 16)

        @block.gpsimd
        def _(pool):
            band = picked[:, :, :].rearrange("e c (j f) -> e (c j) f", f=H2)
            pool.memset(picked[:, :, :], 1.0).then_inc(cut, 1)
            for n, sign in enumerate((-1, 1)):
                pool.wait_ge(cut, n + 1)
                pool.affine_select(out=band, in_=band, pattern=[[sign, E2], [0, H2]], base=0, channel_multiplier=-sign,
                                   compare_op=ALU.is_ge, fill=0.0).then_inc(cut, 1)

        @block.vector
        def _(dve):
            ch = Chain(dve, step)
            dve.wait_ge(w_in, 160)
            dve.wait_ge(routed, 1)
            ch.done(dve.tensor_tensor(logits[:, :, :], py[0:SQ, 0:2, :].rearrange("q g (b e) -> q (g b) e", e=E2),
                                      router_b[:, :].unsqueeze(1).to_broadcast([SQ, B, E2]), ALU.add))
            softmax_rows(dve, 1, ch, logits, top, e, total, inv, probs, exp_ready, exped, E2)
            for b in range(B):
                dve.max(best8[:, b, :], probs[:, b, :]).then_inc(top_done, 1)
            for b in range(B):
                dve.wait_ge(top_done, b + 1)
                last = dve.match_replace(left[:, b, :], best8[:, b, :], probs[:, b, :], -1.0)
                last.then_inc(top_done, 1)
            dve.wait_ge(top_done, 2 * B)
            ch.done(dve.tensor_scalar(chosen[:, :, :], left[:, :, :], -1.0, None, ALU.is_equal))
            ch.done(dve.tensor_tensor(chosen[:, :, :], chosen[:, :, :], probs[:, :, :], ALU.mult))
            ch.done(dve.tensor_reduce(total[:, :], best8[:, :, :], X, ALU.add))
            ch.done(dve.reciprocal(inv[:, :], total[:, :]))
            ch.done(dve.tensor_tensor(left[:, :, :], chosen[:, :, :], inv[:, :].unsqueeze(2).to_broadcast([SQ, B, E2]),
                                      ALU.mult))
            ch.done(dve.tensor_copy(weights[:, :, 0, :].bitcast(F32R), left[:, :, :]))
            dve.tensor_tensor(weights[:, :, 1, :].bitcast(F32R), left[:, :, :], weights[:, :, 0, :],
                              ALU.subtract).then_inc(weighted, 1)
            dve.wait_ge(weightsT_ready, TG)

            def group(g, first):
                if not first:
                    dve.wait_ge(y_full, g)
                dve.tensor_copy(own[:, :, :], weightsT[:, :].rearrange("e (g b q) -> e g b q", g=TG, q=SQ)[:, g, :, :])\
                    .then_inc(own_ready, 1)
                for ci in range(HC2):
                    dve.wait_ge(w_full, g * HC2 + ci + 1)
                    dve.wait_ge(h_ready, g * CH + ci + 1)
                    dve.tensor_tensor(hidden[:, ci, :], hidden[:, ci, :], pw[:, ci % 3, 0:NTG], ALU.mult).then_inc(scaled, 1)
                dve.wait_ge(y_full, g + 1)
                dve.tensor_tensor(k.x[:, :, :].rearrange("q (g b) d -> q g b d", b=BG)[:, g, :, :],
                                  k.x[:, :, :].rearrange("q (g b) d -> q g b d", b=BG)[:, g, :, :],
                                  py[0:SQ, 0, :].rearrange("q (b d) -> q b d", d=D), ALU.add).then_inc(y_added, 1)

            group(0, True)
            with dve.Fori(1, TG) as g:
                group(g, False)

        @block.scalar
        def _(act):
            act.preload_act_table(ACT.Exp)
            act.wait_ge(exp_ready, 1)
            act.activation(e[:, :, :], e[:, :, :], ACT.Exp).then_inc(exped, 1)
            act.sem_inc(h_free, 3)

            def group(g):
                for ci in range(CH):
                    act.wait_ge(h_full, g * CH + ci + 1)
                    if ci == 0:
                        act.wait_ge(y_full, g) if not isinstance(g, int) or g > 0 else None
                    act.activation(hidden[:, ci, :], ph[:, ci % 3, 0:NTG], ACT.Silu, bias=b1[:, ci:ci + 1]).then_inc(h_ready, 1)
                    act.wait_ge(h_ready, g * CH + ci + 1)
                    act.sem_inc(h_free, 1)

            group(0)
            for g in range(TG):
                act.wait_ge(turned, g + 1)
                act.copy(weightsT[:, g * NTG:(g + 1) * NTG], pw[:, g % 2, 0:NTG]).then_inc(weightsT_ready, 1)
            with act.Fori(1, TG) as g:
                group(g)

        @block.tensor
        def _(pe):
            pe.wait_ge(w_in, 160)
            for b in range(B):
                last = pe.matmul(py[0:SQ, b // 8, (b % 8) * E2:(b % 8 + 1) * E2], k.xnT[:, b * SQ:(b + 1) * SQ],
                                 router[:, :], start=True, stop=True)
            last.then_inc(routed, 1)
            xg = k.xnT[:, :].rearrange("p (g t) -> p g t", g=TG)

            def up(g, ci):
                pe.wait_ge(h_free, g * CH + ci + 1)
                pe.matmul(ph[:, ci % 3, 0:NTG], w1[:, ci * 128:(ci + 1) * 128], xg[:, g, :],
                          start=True, stop=True).then_inc(h_full, 1)

            for ci in range(CH):
                up(0, ci)
            pe.wait_ge(weighted, 1)
            for g in range(TG):
                if g >= 2:
                    pe.wait_ge(weightsT_ready, g - 1)
                for j in range(BG):
                    last = pe.transpose(pw[:, g % 2, j * SQ:(j + 1) * SQ],
                                        weights[:, g * BG + j, :, :].rearrange("q n e -> q (n e)"), k.ident[0:SQ, 0:SQ])
                last.then_inc(turned, 1)
            pe.wait_ge(weightsT_ready, TG)
            pe.wait_ge(picker_in, 32)

            def group(g):
                pe.wait_ge(own_ready, g + 1)
                for ci in range(CH):
                    if not isinstance(g, int):
                        up(g, ci)
                    if ci < HC2:
                        if ci >= 3 or not isinstance(g, int):
                            pe.wait_ge(scaled, g * HC2 + ci - 2 if ci >= 3 else g * HC2)
                        pe.matmul(pw[:, ci % 3, 0:NTG], picker[:, ci, :], own[:, :, :],
                                  start=True, stop=True).then_inc(w_full, 1)
                pe.wait_ge(scaled, g * HC2 + HC2)
                pe.wait_ge(h_ready, g * CH + CH)
                if not isinstance(g, int):
                    pe.wait_ge(y_added, g)
                for j in range(BG):
                    to = py[0:SQ, 0, j * D:(j + 1) * D]
                    for ci in range(CH):
                        pe.matmul(to, hidden[:, ci, j * SQ:(j + 1) * SQ], w2[:, ci, :], start=(ci == 0), stop=False)
                    pe.matmul(to, own[:, j, :].bitcast(F32), b2[:, :], start=False, stop=False)
                    last = pe.matmul(to, k.ones[0:ES, 0:SQ], sb2[:, :], start=False, stop=True)
                last.then_inc(y_full, 1)

            group(0)
            with pe.Fori(1, TG) as g:
                group(g)


class Experts:

    def __init__(self, o, ins):
        self.w1 = o.sb("w1", [128, 2, FF])
        self.w2 = o.sb("w2", [128, 2, FC, D])
        self.b1 = o.sb("b1", [128, 2, FC])
        self.loaded = o.sems("w_in0 w_in1")
        self.ins = ins

    def load(self, sp, e, j):
        ins = self.ins
        sp.dma_start(self.w1[:, j, :], ins["L3_W1"][e]).then_inc(self.loaded[j], 16)
        sp.dma_start(self.w2[:, j, :, :], ins["L3_W2"][e].rearrange("(c p) d -> p c d", p=128)).then_inc(self.loaded[j], 16)
        sp.dma_start(self.b1[:, j, :], ins["L3_b1"][e]).then_inc(self.loaded[j], 16)


def all_experts(nc, k, experts, E, func, gates, acc):
    with Scope(nc, "f3d") as c:
        w1, w2, b1, w_in = experts.w1, experts.w2, experts.b1, experts.loaded
        own = c.sb("own", [SQ, 2, B])
        hidden = c.sb("hidden", [128, 2, FC, NTG])
        ph = c.ps("ph", [128, 4, 512])
        py = c.ps("py", [128, 2, 512])
        h_full, h_ready, y_full, y_added, own_ready, step = c.sems(
            "h_full h_ready y_full y_added own_ready step")
        block = c.block()
        HALVES = E // 2

        @block.sync
        def _(sp):
            with sp.Fori(1, HALVES) as i:
                for j in range(2):
                    sp.wait_ge(y_full, TG * (2 * i + j) - TG + 2)
                    experts.load(sp, 2 * i + j, j)

        W_IN = 48

        @block.tensor
        def _(pe):
            def up(e, i, j, g):
                s = TG * e + g
                if g == 0:
                    pe.wait_ge(w_in[j], W_IN * i + W_IN)
                for ci in range(FC):
                    pe.wait_ge(h_ready, FC * s + ci + 1)
                    pe.matmul(ph[:, ci, 0:NTG], w1[:, j, ci * 128:(ci + 1) * 128], k.xnT[:, g * NTG:(g + 1) * NTG],
                              start=True, stop=True).then_inc(h_full, 1)

            def down(e, j, g, prev=0):
                s = TG * e + g - prev
                pe.wait_ge(h_ready, FC * s + 2 * FC)
                pe.wait_ge(y_added, s + 1)
                gg = (g - prev) % TG
                for jb in range(BG):
                    for ci in range(FC):
                        last = pe.matmul(py[0:SQ, gg % 2, jb * D:(jb + 1) * D], hidden[:, gg % 2, ci, jb * SQ:(jb + 1) * SQ],
                                         w2[:, j, ci, :], start=(ci == 0), stop=(ci == FC - 1))
                last.then_inc(y_full, 1)

            up(0, 0, 0, 0)
            for g in range(1, TG):
                up(0, 0, 0, g)
                down(0, 0, g, 1)
            up(1, 0, 1, 0)
            down(1, 0, 0, 1)
            for g in range(1, TG):
                up(1, 0, 1, g)
                down(1, 1, g, 1)
            with pe.Fori(1, HALVES) as i:
                for j in range(2):
                    for g in range(TG):
                        up(2 * i + j, i, j, g)
                        down(2 * i + j, j if g else 1 - j, g, 1)
            down(E, 1, 0, 1)

        @block.scalar
        def _(act):
            act.sem_inc(h_ready, FC)
            act.preload_act_table(func)

            def ups(e, i, j):
                act.wait_ge(w_in[j], W_IN * i + W_IN)
                for g in range(TG):
                    s = TG * e + g
                    act.wait_ge(y_full, s + 1)
                    for ci in range(FC):
                        act.wait_ge(h_full, FC * s + ci + 1)
                        act.activation(hidden[:, g % 2, ci, :], ph[:, ci, 0:NTG], func,
                                       bias=b1[:, j, ci:ci + 1]).then_inc(h_ready, 1)

            act.sem_inc(y_full, 2)
            with act.Fori(0, HALVES) as i:
                ups(2 * i, i, 0)
                ups(2 * i + 1, i, 1)

        @block.vector
        def _(dve):
            dve.sem_inc(y_added, 2)

            def adds(e, j):
                dve.tensor_copy(own[:, j, :], gates[:, :, e]).then_inc(own_ready, 1)
                dve.wait_ge(own_ready, e + 1)
                for g in range(TG):
                    s = TG * e + g
                    dve.wait_ge(y_full, s + 3)
                    for jb in range(BG):
                        b = g * BG + jb
                        dve.scalar_tensor_tensor(acc[:, b, :], py[0:SQ, g % 2, jb * D:(jb + 1) * D], own[:, j, b:b + 1],
                                                 acc[:, b, :], ALU.mult, ALU.add).then_inc(step, 1)
                    dve.wait_ge(step, s * BG + BG)
                    dve.sem_inc(y_added, 1)

            with dve.Fori(0, HALVES) as i:
                adds(2 * i, 0)
                adds(2 * i + 1, 1)


def l0_round(nc, k, m, ins, layer):
    rows_, router = m.rows, m.router
    with Scope(nc, f"f0r{layer}") as c:
        logits, e, probs, hit, onehot, pos = (c.sb(n, [SQ, B, E0]) for n in "logits e probs hit onehot pos".split())
        before = c.sb("before", [SQ, B + 1, E0])
        full = c.sb("full", [SQ, E0, MOST])
        blocks_ = c.sb("blocks", [SQ, E0])
        earlier = c.sb("earlier", [SQ, E0, E0])
        first, end = c.sb("first", [SQ, E0]), c.sb("end", [SQ, E0])
        passed = c.sb("passed", [1, BLOCKS, E0])
        owner = c.sb("owner", [1, BLOCKS])
        expert = c.sb("expert", [1, BLOCKS], I32)
        place = c.sb("place", [SQ, B])
        slot = c.sb("slot", [SQ, B], U32)
        top, total, inv = (c.sb(n, [SQ, B]) for n in "top total inv".split())
        xs = c.sb("xs", [128, BLOCKS, D])
        xsT = c.sb("xsT", [128, BLOCKS, 128])
        ys = c.sb("ys", [128, BLOCKS, D])
        w1 = c.sb("w1", [128, 2, FF])
        hidden = c.sb("hidden", [128, 2, FC, 128])
        ph = c.ps("ph", [128, 2, 512])
        py = c.ps("py", [128, 2, 512])
        pt = c.ps("pt", [128, 2, 512])
        pr = c.ps("pr", [128, 2, 512])
        (routed, exp_ready, exped, ones_ready, counted, slot_ready, expert_ready, sorted_, turned, xsT_ready,
         w1_ready, up_full, silued, down_full, ys_ready, ys_out, scaled, rows_turned, copied, step,
         parted) = c.sems(
            "routed exp_ready exped ones_ready counted slot_ready expert_ready sorted turned xsT_ready "
            "w1_ready up_full silued down_full ys_ready ys_out scaled rows_turned copied step parted")
        block = c.block()
        xs_in = c.sems(" ".join(f"xs_in{i}" for i in range(BLOCKS // GB)))
        fetched = c.sems(" ".join(f"fetched{g}" for g in range(TG)))
        more = layer < L0 - 1
        C = 2

        def groups(eng, group):
            group(0, True, False)
            with eng.Fori(1, BLOCKS // GB - 1) as i:
                group(i, False, False)
            group(BLOCKS // GB - 1, False, True)

        @block.sync
        def _(sp):
            sp.wait_ge(sorted_, 16 * B)
            for i in range(BLOCKS // GB):
                sp.dma_start(xs[:, i * GB:(i + 1) * GB, :],
                             m.sorted[i * GB * 128:(i + 1) * GB * 128, :].rearrange("(s p) d -> p s d", p=128))\
                    .then_inc(xs_in[i], 16)
            for i in range(BLOCKS // GB):
                sp.wait_ge(ys_ready, C + (i + 1) * GB)
                sp.dma_start(m.outputs[i * GB * 128:(i + 1) * GB * 128, :].rearrange("(s p) d -> p s d", p=128),
                             ys[:, i * GB:(i + 1) * GB, :]).then_inc(ys_out, 16)

        @block.gpsimd
        def _(pool):
            pool.wait_ge(slot_ready, 1)
            if layer == 0:
                pool.wait_ge(m.cleared, 16 * -(-BLOCKS * 128 // NT))
            for b in range(B):
                pool.indirect_dma_start(m.sorted, bass.IndirectOffsetOnAxis(slot[:, b:b + 1], 0),
                                        rows_[:, b, :], None).then_inc(sorted_, 16)
            pool.wait_ge(sorted_, 16 * B)
            pool.wait_ge(ys_out, 16 * (BLOCKS // GB))
            for b in range(B):
                pool.indirect_dma_start(rows_[:, b, :], None, m.outputs,
                                        bass.IndirectOffsetOnAxis(slot[:, b:b + 1], 0)).then_inc(fetched[b // BG], 16)

        @block.tensor
        def _(pe):
            if layer == 0:
                pe.wait_ge(m.router_in, 16)
            for b in range(B):
                last = pe.matmul(pr[0:SQ, 0, b * E0:(b + 1) * E0], k.xnT[:, b * SQ:(b + 1) * SQ],
                                 router[:, layer, :], start=True, stop=True)
            last.then_inc(routed, 1)
            pe.wait_ge(ones_ready, 1)
            pe.matmul(pr[0:SQ, 0, 0:B * E0], k.lower[0:SQ, 0:SQ], onehot[:, :, :], start=True, stop=True).then_inc(counted, 1)
            pe.matmul(pr[0:SQ, 1, 0:B * E0], k.ones[0:SQ, 0:SQ], onehot[:, :, :], start=True, stop=True).then_inc(counted, 1)
            if layer == 0:
                pe.wait_ge(m.weights_in, 32 * E0)

            def up(s, j):
                pe.wait_ge(w1_ready, s + 1)
                pe.wait_ge(silued, s + 1)
                for ci in range(FC):
                    last = pe.matmul(ph[:, j, ci * 128:(ci + 1) * 128], w1[:, j, ci * 128:(ci + 1) * 128],
                                     xsT[:, s, :] if isinstance(s, int) else xsT[:, bass.ds(s, 1), :],
                                     start=True, stop=True)
                last.then_inc(up_full, 1)

            def down(s, j):
                pe.wait_ge(silued, s + 1 + C)
                pe.wait_ge(ys_ready, s + 1)
                pe.sem_inc(parted, 1)
                ex = pe.value_load(expert[0:1, s:s + 1] if isinstance(s, int) else expert[0:1, bass.ds(s, 1)],
                                   min_val=0, max_val=E0 - 1)
                for ci in range(FC):
                    last = pe.matmul(py[:, j, 0:D], hidden[:, j, ci, :], m.w2[:, bass.ds(ex, 1), ci, :],
                                     start=(ci == 0), stop=(ci == FC - 1))
                last.then_inc(down_full, 1)

            def group(i, head, tail):
                for n in range(GB):
                    s = i * GB + n
                    up(s, n % 2)
                    if not (head and n == 0):
                        down(s - 1, (n - 1) % 2)
                if tail:
                    down(BLOCKS - 1, (BLOCKS - 1) % 2)

            for i in range(BLOCKS // GB):
                pe.wait_ge(xs_in[i], 16)
                if i >= 2:
                    pe.wait_ge(xsT_ready, i - 1)
                for n in range(GB):
                    last = pe.transpose(pt[:, i % 2, n * 128:(n + 1) * 128], xs[:, i * GB + n, :], k.ident[:, :])
                last.then_inc(turned, 1)
            pe.wait_ge(xsT_ready, BLOCKS // GB)
            pe.wait_ge(expert_ready, 1)
            groups(pe, group)
            for g in range(TG if more else 0):
                pe.wait_ge(scaled, g + 1)
                if g >= 2:
                    pe.wait_ge(copied, g - 1)
                for j in range(BG):
                    last = pe.transpose(ph[:, g % 2, j * SQ:(j + 1) * SQ], rows_[:, g * BG + j, :], k.ident[0:SQ, 0:SQ])
                last.then_inc(rows_turned, 1)

        @block.scalar
        def _(act):
            act.preload_act_table(ACT.Exp)
            act.wait_ge(exp_ready, 1)
            act.activation(e[:, :, :], e[:, :, :], ACT.Exp).then_inc(exped, 1)
            act.preload_act_table(ACT.Silu)
            act.sem_inc(silued, C)

            def group(i, head, tail):
                for n in range(GB):
                    s = i * GB + n
                    act.wait_ge(up_full, s + 2)
                    act.wait_ge(down_full, s + 1)
                    act.activation(hidden[:, n % 2, :, :], ph[:, n % 2, :].rearrange("p (c q) -> p c q", q=128),
                                   ACT.Silu).then_inc(silued, 1)

            groups(act, group)
            for g in range(TG if more else 0):
                act.wait_ge(rows_turned, g + 1)
                act.copy(k.xnT[:, g * NTG:(g + 1) * NTG], ph[:, g % 2, 0:NTG]).then_inc(copied, 1)

        @block.vector
        def _(dve):
            dve.sem_inc(up_full, 1)
            dve.sem_inc(down_full, C)
            dve.sem_inc(ys_ready, C)
            ch = Chain(dve, step)
            dve.wait_ge(routed, 1)
            ch.done(dve.tensor_copy(logits[:, :, :], pr[0:SQ, 0, 0:B * E0].rearrange("q (b e) -> q b e", e=E0)))
            softmax_rows(dve, 1, ch, logits, top, e, total, inv, probs, exp_ready, exped, E0)
            first_largest(dve, ch, k, probs, top, hit, onehot, E0)
            dve.sem_inc(ones_ready, 1)
            ch.done(dve.memset(before[:, 0, :], 0.0))
            dve.wait_ge(counted, 2)
            for b in range(B):
                ch.done(dve.tensor_tensor(before[:, b + 1, :], before[:, b, :], pr[0:SQ, 1, b * E0:(b + 1) * E0], ALU.add))
            ch.done(dve.tensor_tensor(full[:, :, :], before[:, B, :].unsqueeze(2).to_broadcast([SQ, E0, MOST]),
                                      m.multiples[:, :].unsqueeze(1).to_broadcast([SQ, E0, MOST]), ALU.is_gt))
            ch.done(dve.tensor_reduce(blocks_[:, :], full[:, :, :], X, ALU.add))
            ch.done(dve.tensor_tensor(earlier[:, :, :], blocks_[:, :].unsqueeze(1).to_broadcast([SQ, E0, E0]),
                                      m.is_before[:, :, :], ALU.mult))
            ch.done(dve.tensor_reduce(first[:, :], earlier[:, :, :], X, ALU.add))
            ch.done(dve.tensor_tensor(end[:, :], first[:, :], blocks_[:, :], ALU.add))
            ch.done(dve.tensor_scalar(first[:, :], first[:, :], 128.0, None, ALU.mult))
            ch.done(dve.tensor_tensor(pos[:, :, :], pr[0:SQ, 0, 0:B * E0].rearrange("q (b e) -> q b e", e=E0),
                                      before[:, 0:B, :], ALU.add))
            ch.done(dve.tensor_tensor(pos[:, :, :], pos[:, :, :], first[:, :].unsqueeze(1).to_broadcast([SQ, B, E0]), ALU.add))
            ch.done(dve.tensor_tensor(pos[:, :, :], pos[:, :, :], onehot[:, :, :], ALU.mult))
            ch.done(dve.tensor_reduce(place[:, :], pos[:, :, :], X, ALU.add))
            dve.tensor_copy(slot[:, :], place[:, :]).then_inc(slot_ready, 1)
            ch.done(dve.tensor_tensor(passed[:, :, :], m.block_number[:, :].unsqueeze(2).to_broadcast([1, BLOCKS, E0]),
                                      end[0:1, :].unsqueeze(1).to_broadcast([1, BLOCKS, E0]), ALU.is_ge))
            ch.done(dve.tensor_reduce(owner[:, :], passed[:, :, :], X, ALU.add))
            ch.done(dve.tensor_scalar(expert[:, :], owner[:, :], float(E0 - 1), None, ALU.min))
            dve.sem_inc(expert_ready, 1)
            if layer == 0:
                dve.wait_ge(m.weights_in, 32 * E0)

            def weigh(s, j):
                ex = dve.value_load(expert[0:1, s:s + 1] if isinstance(s, int) else expert[0:1, bass.ds(s, 1)],
                                    min_val=0, max_val=E0 - 1)
                dve.tensor_copy(w1[:, j, :], m.w1[:, bass.ds(ex, 1), :]).then_inc(w1_ready, 1)

            def keep(s, j):
                dve.wait_ge(down_full, s + 1 + C)
                dve.sem_inc(parted, 1)
                dve.tensor_copy(ys[:, s, :] if isinstance(s, int) else ys[:, bass.ds(s, 1), :],
                                py[:, j, 0:D]).then_inc(ys_ready, 1)

            def group(i, head, tail):
                for n in range(GB):
                    s = i * GB + n
                    if not (tail and n == GB - 1):
                        dve.wait_ge(up_full, s + 1)
                        dve.sem_inc(parted, 1)
                        weigh(s + 1, (n + 1) % 2)
                    if not (head and n == 0):
                        keep(s - 1, (n - 1) % 2)
                if tail:
                    keep(BLOCKS - 1, (BLOCKS - 1) % 2)

            weigh(0, 0)
            for i in range(BLOCKS // GB):
                dve.wait_ge(turned, i + 1)
                dve.tensor_copy(xsT[:, i * GB:(i + 1) * GB, :],
                                pt[:, i % 2, :].rearrange("p (s q) -> p s q", q=128)).then_inc(xsT_ready, 1)
            groups(dve, group)
            for g in range(TG):
                s = slice(g * BG, (g + 1) * BG)
                dve.wait_ge(fetched[g], 16 * BG)
                by = top[:, s].unsqueeze(2).to_broadcast([SQ, BG, D])
                dve.tensor_tensor(rows_[:, s, :], rows_[:, s, :], by, ALU.mult).then_inc(scaled, 1)
                if not more:
                    dve.wait_ge(scaled, g + 1)
                    ch.done(dve.tensor_tensor(k.x[:, s, :], k.x[:, s, :], rows_[:, s, :], ALU.add))


def l0_ffn(nc, k, m, ins):
    layernorm(nc, k, "ln0f", m.rows)
    for layer in range(L0):
        l0_round(nc, k, m, ins, layer)


class FirstMixture:

    def __init__(self, nc, o, ins):
        self.w1 = o.sb("w1", [128, E0, FF])
        self.w2 = o.sb("w2", [128, E0, FC, D])
        self.rows = o.sb("rows", [SQ, B, D])
        self.router = o.sb("router", [128, L0, E0])
        self.multiples = o.sb("multiples", [SQ, MOST])
        self.is_before = o.sb("is_before", [SQ, E0, E0])
        self.block_number = o.sb("block_number", [1, BLOCKS])
        self.sorted = nc.dram_tensor("sorted", (BLOCKS * 128, D), F32, kind="Internal").ap()
        self.outputs = nc.dram_tensor("outputs", (BLOCKS * 128, D), F32, kind="Internal").ap()
        self.weights_in, self.router_in, self.cleared = o.sems("weights_in router_in cleared")


def l3_ffn(nc, k, ins):
    with Scope(nc, "f3") as o:
        gates = o.sb("gates", [SQ, B, E3])
        experts = Experts(o, ins)
        with Scope(nc, "f3r") as c:
            wg = c.sb("wg", [128, E3])
            b2 = c.sb("b2", [E3, D])
            (r_in,) = c.sems("r_in")

            def loads(sp):
                sp.dma_start(wg[:, :], ins["L3_Wg"]).then_inc(r_in, 16)
                sp.dma_start(b2[:, :], ins["L3_b2"]).then_inc(r_in, 16)
                experts.load(sp, 0, 0)
                experts.load(sp, 1, 1)

            layernorm(nc, k, "ln3f", loads=loads)
            logits, e, probs, hit, one1, one2, rest, pos, before, keep, left = (
                c.sb(n, [SQ, B, E3]) for n in "logits e probs hit one1 one2 rest pos before keep left".split())
            count = c.sb("count", [SQ, 2, B, E3])
            start_ = c.sb("start", [SQ, 2, B + 1, E3])
            top, total, inv, g1, g2, den = (c.sb(n, [SQ, B]) for n in "top total inv g1 g2 den".split())
            gatesT = c.sb("gatesT", [E3, NT])
            ps = c.ps("ps", [128, 512])
            pc = c.ps("pc", [128, 512])
            pt = c.ps("pt", [128, TG, 512])
            routed, exp_ready, exped, ones_ready, counted, gated, turned, turned_in, b2_full, step = c.sems(
                "routed exp_ready exped ones_ready counted gated turned turned_in b2_full step")
            block = c.block()

            @block.tensor
            def _(pe):
                pe.wait_ge(r_in, 32)
                for b in range(B):
                    last = pe.matmul(ps[0:SQ, b * E3:(b + 1) * E3], k.xnT[:, b * SQ:(b + 1) * SQ], wg[:, :],
                                     start=True, stop=True)
                last.then_inc(routed, 1)
                pe.wait_ge(ones_ready, 1)
                for n, one in enumerate((one1, one2)):
                    pe.matmul(pc[0:SQ, n * 256:n * 256 + B * E3], k.lower[0:SQ, 0:SQ], one[:, :, :], start=True, stop=True)
                    last = pe.matmul(pc[0:SQ, n * 256 + 128:n * 256 + 128 + B * E3], k.ones[0:SQ, 0:SQ], one[:, :, :],
                                     start=True, stop=True)
                last.then_inc(counted, 1)
                pe.wait_ge(gated, 1)
                for g in range(TG):
                    for j in range(BG):
                        last = pe.transpose(pt[0:E3, g, j * SQ:(j + 1) * SQ], gates[:, g * BG + j, :], k.ident[0:SQ, 0:SQ])
                last.then_inc(turned, 1)
                pe.wait_ge(turned_in, 1)
                for b in range(B):
                    last = pe.matmul(pt[0:SQ, b // 4, (b % 4) * D:(b % 4 + 1) * D], gatesT[:, b * SQ:(b + 1) * SQ], b2[:, :],
                                     start=True, stop=True)
                last.then_inc(b2_full, 1)

            @block.scalar
            def _(act):
                act.preload_act_table(ACT.Exp)
                act.wait_ge(exp_ready, 1)
                act.activation(e[:, :, :], e[:, :, :], ACT.Exp).then_inc(exped, 1)
                act.wait_ge(turned, 1)
                act.copy(gatesT[:, :].rearrange("e (g t) -> e g t", g=TG), pt[0:E3, :, 0:NTG]).then_inc(turned_in, 1)

            @block.vector
            def _(dve):
                ch = Chain(dve, step)
                wide = lambda a: a.unsqueeze(2).to_broadcast([SQ, B, E3])
                dve.wait_ge(routed, 1)
                ch.done(dve.tensor_copy(logits[:, :, :], ps[0:SQ, 0:B * E3].rearrange("q (b e) -> q b e", e=E3)))
                softmax_rows(dve, 1, ch, logits, top, e, total, inv, probs, exp_ready, exped, E3)
                first_largest(dve, ch, k, probs, top, hit, one1, E3)
                ch.done(dve.tensor_scalar(hit[:, :, :], one1[:, :, :], -3.0e38, None, ALU.mult))
                ch.done(dve.tensor_scalar(left[:, :, :], one1[:, :, :], -1.0, 1.0, ALU.mult, ALU.add))
                ch.done(dve.tensor_tensor(rest[:, :, :], logits[:, :, :], left[:, :, :], ALU.mult))
                ch.done(dve.tensor_tensor(rest[:, :, :], rest[:, :, :], hit[:, :, :], ALU.add))
                first_largest(dve, ch, k, rest, top, hit, one2, E3)
                dve.sem_inc(ones_ready, 1)
                for one, g in ((one1, g1), (one2, g2)):
                    ch.done(dve.tensor_tensor(hit[:, :, :], one[:, :, :], probs[:, :, :], ALU.mult))
                    ch.done(dve.tensor_reduce(g[:, :], hit[:, :, :], X, ALU.add))
                ch.done(dve.tensor_tensor(den[:, :], g1[:, :], g2[:, :], ALU.add))
                ch.done(dve.tensor_scalar(den[:, :], den[:, :], 1e-9, None, ALU.add))
                ch.done(dve.reciprocal(inv[:, :], den[:, :]))
                for g in (g1, g2):
                    ch.done(dve.tensor_tensor(g[:, :], g[:, :], inv[:, :], ALU.mult))
                dve.wait_ge(counted, 1)
                ch.done(dve.memset(start_[:, 0, 0, :], 0.0))
                for n in range(2):
                    ch.done(dve.tensor_copy(count[:, n, :, :],
                                            pc[0:SQ, n * 256 + 128:n * 256 + 256].rearrange("q (b e) -> q b e", e=E3)))
                    if n:
                        ch.done(dve.tensor_copy(start_[:, 1, 0, :], start_[:, 0, B, :]))
                    for b in range(B):
                        ch.done(dve.tensor_tensor(start_[:, n, b + 1, :], start_[:, n, b, :], count[:, n, b, :], ALU.add))
                for n, (one, g) in enumerate(((one1, g1), (one2, g2))):
                    ch.done(dve.tensor_tensor(pos[:, :, :], pc[0:SQ, n * 256:n * 256 + 128].rearrange("q (b e) -> q b e", e=E3),
                                              start_[:, n, 0:B, :], ALU.add))
                    ch.done(dve.tensor_scalar(keep[:, :, :], pos[:, :, :], float(CAP), None, ALU.is_lt))
                    ch.done(dve.tensor_tensor(keep[:, :, :], keep[:, :, :], one[:, :, :], ALU.mult))
                    t = (before, left)[n]
                    ch.done(dve.tensor_tensor(t[:, :, :], keep[:, :, :], wide(g[:, :]), ALU.mult))
                dve.tensor_tensor(gates[:, :, :], before[:, :, :], left[:, :, :], ALU.add).then_inc(gated, 1)
                dve.wait_ge(b2_full, 1)
                ch.done(dve.tensor_tensor(k.x[:, :, :].rearrange("q (g b) d -> q g b d", b=BG),
                                          k.x[:, :, :].rearrange("q (g b) d -> q g b d", b=BG),
                                          pt[0:SQ, :, :].rearrange("q g (b d) -> q g b d", d=D), ALU.add))

        all_experts(nc, k, experts, E3, ACT.Gelu, gates, k.x)


def store(nc, k, out):
    with Scope(nc, "store") as c:
        (stored,) = c.sems("stored")
        block = c.block()

        @block.sync
        def _(sp):
            sp.dma_start(out.rearrange("b q d -> q b d"), k.x[:, :, :]).then_inc(stored, 16)
            sp.wait_ge(stored, 16)


class Shared:
    pass


def program(nc, ins, out):
    k = Shared()
    with Scope(nc, "k") as c:
        k.x = c.sb("x", [SQ, B, D])
        k.xnT = c.sb("xnT", [128, NT])
        k.ident = c.sb("ident", [128, 128])
        k.negident = c.sb("negident", [H, H])
        k.headmask = c.sb("headmask", [128, H])
        k.groupmask = c.sb("groupmask", [128, GH])
        k.blockavg = c.sb("blockavg", [128, 128])
        k.lower = c.sb("lower", [128, 128])
        k.ones = c.sb("ones", [128, 128])
        k.backwards = c.sb("backwards", [128, E2])
        k.best = c.sb("best", [SQ, B])
        setup(nc, k, ins)
        with Scope(nc, "f0") as o:
            mixture = FirstMixture(nc, o, ins)
            l0_attention(nc, k, mixture, ins)
            l0_ffn(nc, k, mixture, ins)
        heads_attention(nc, k, ins, 1)
        l1_ffn(nc, k, ins)
        heads_attention(nc, k, ins, 2)
        l2_ffn(nc, k, ins)
        heads_attention(nc, k, ins, 3)
        l3_ffn(nc, k, ins)
        store(nc, k, out)


def _layouts(a):
    import numpy as np

    col = lambda v: v.reshape(-1, 1)
    t = {
        "x": a["x"], "ctx_1024": a["ctx_1024"], "ctxT": a["ctx_1024"].transpose(0, 2, 1),
        "mask_BxSxS2_ik0": a["mask_BxSxS2_ik0"],
        "keymask": a["mask_Bx1x1xS2_ik0"].reshape(B, 1, SK),
        "L0_xattn_W": a["L0_xattn_W"].T, "L0_xattn_b": col(a["L0_xattn_b"]),
        "L0_routers": a["L0_ffn_routers"].transpose(1, 0, 2),
        "L0_W1": a["L0_ffn_W1"], "L0_W2": a["L0_ffn_W2"],
        "L3_Wg": a["L3_ffn_Wg"], "L3_W1": a["L3_ffn_W1"], "L3_W2": a["L3_ffn_W2"],
        "L3_b1": a["L3_ffn_b1"].reshape(E3, FC, 128).transpose(0, 2, 1), "L3_b2": a["L3_ffn_b2"],
        "mu_r": col(a["L1_ffn_mu_r"]), "mu_k": col(a["L1_ffn_mu_k"]),
        "W_rT": a["L1_ffn_W_r"].T, "W_kT": a["L1_ffn_W_k"].T, "W_vT": a["L1_ffn_W_v"].T,
        "router_w": a["L2_ffn_router_w"], "router_b": a["L2_ffn_router_b"].reshape(1, E2),
        "w1": a["L2_ffn_w1"].transpose(1, 0, 2).reshape(D, E2 * H2),
        "b1": a["L2_ffn_b1"].reshape(HC2, 128).T,
        "w2": a["L2_ffn_w2"].reshape(HC2, 128, D).transpose(1, 0, 2), "b2": np.concatenate([a["L2_ffn_b2"], a["L2_ffn_b2"]]),
        "sw1": a["L2_ffn_sw1"].transpose(1, 0, 2).reshape(D, ES * HS2),
        "sb1": a["L2_ffn_sb1"].reshape(SC2, 128).T,
        "sw2": a["L2_ffn_sw2"].reshape(SC2, 128, D).transpose(1, 0, 2), "sb2": a["L2_ffn_sb2"],
    }
    pad = np.zeros((B, 128 * KT), a["mask_Bx1x1xS2_ik0"].dtype)
    pad[:, 0:SK] = a["mask_Bx1x1xS2_ik0"].reshape(B, SK)
    t["keymask_cols"] = pad.reshape(B, KT, 128).transpose(2, 0, 1)
    for n, (q, kk, v, o, turn) in {
        1: ("L1_xattn_wq", "L1_xattn_wk", "L1_xattn_wv", "L1_xattn_wo", False),
        2: ("L2_xattn_wq", "L2_xattn_wk", "L2_xattn_wv", "L2_xattn_wo", True),
    }.items():
        for name, w in zip(("wq", "wk", "wv", "wo"), (q, kk, v, o)):
            t[f"{name}{n}"] = a[w].T if turn else a[w]
        for name in ("bq", "bk", "bv"):
            t[f"{name}{n}"] = col(a[f"L{n}_xattn_{name}"])
        t[f"bo{n}"] = a[f"L{n}_xattn_bo"].reshape(1, D)
    t["wq3"], t["wo3"] = a["L3_xattn_Wq"], a["L3_xattn_Wproj"]
    t["wk3"], t["wv3"] = a["L3_xattn_Wkv"][:, 0:D], a["L3_xattn_Wkv"][:, D:]
    t["bq3"] = col(a["L3_xattn_bq"])
    t["bk3"], t["bv3"] = col(a["L3_xattn_bkv"][0:D]), col(a["L3_xattn_bkv"][D:])
    t["bo3"] = a["L3_xattn_bproj"].reshape(1, D)
    t["gq3"], t["gk3"] = col(np.tile(a["L3_xattn_gq"], H)), col(np.tile(a["L3_xattn_gk"], H))
    return {n: np.ascontiguousarray(v) for n, v in t.items()}


def kernel(**inputs):
    import numpy as np
    import concourse.bacc as bacc
    from concourse.bass_utils import run_bass_kernel_spmd as run

    nc = bacc.Bacc("TRN2", target_bir_lowering=False, num_devices=1)
    arrays = _layouts({n: np.asarray(v) for n, v in inputs.items()})
    ins = {n: nc.dram_tensor(f"in_{n}", a.shape, mybir.dt.from_np(a.dtype), kind="ExternalInput").ap()
           for n, a in arrays.items()}
    out = nc.dram_tensor("out_x", (B, SQ, D), F32, kind="ExternalOutput").ap()
    program(nc, ins, out)
    r = run(nc, [{f"in_{n}": a for n, a in arrays.items()}], core_ids=[0])
    return r.results[0]["out_x"]
```
